# Optimizing a Trainium2 kernel written in Bass

```python
import numpy as np
import jax
import jax.numpy as jnp

def _softmax(x, axis=-1):
    return jax.nn.softmax(x, axis=axis)

def _gelu(x):
    return jax.nn.gelu(x, approximate=True)

def _silu(x):
    return jax.nn.silu(x)

def _sigmoid(x):
    return jax.nn.sigmoid(x)

def _layernorm(x, axis=-1, eps=1e-05):
    m = jnp.mean(x, axis=axis, keepdims=True)
    v = jnp.var(x, axis=axis, keepdims=True)
    return (x - m) / jnp.sqrt(v + eps)

def _scatter_add(tgt, idx, src, axis=0):
    return tgt.at[idx].add(src)

def _segment_sum(src, seg, n):
    return jax.ops.segment_sum(src, seg, n)
kernel_name = 'mk_seq_preln_d1_jaxref_r8_9f2f88'

def setup_inputs(seed: int=0):
    np.random.seed(seed)
    _w = jnp.asarray

    def _L0_attn_setup():
        import jax, jax.numpy as jnp
        import numpy as np
        import math
        B, S, D, H, R, DFF = (4, 128, 128, 16, 64, 512)

        def _layernorm(x, g, b, eps=1e-05):
            m = jnp.mean(x, axis=-1, keepdims=True)
            v = jnp.var(x, axis=-1, keepdims=True)
            return (x - m) / jnp.sqrt(v + eps) * g + b
        key = jax.random.key(seed)
        ks = jax.random.split(key, 12)
        sc = 0.02
        return {'src': jax.random.normal(ks[0], (B, S, D), jnp.float32), 'in_proj_w': jax.random.normal(ks[1], (3 * D, D), jnp.float32) * sc, 'in_proj_b': jnp.zeros((3 * D,), jnp.float32), 'out_proj_w': jax.random.normal(ks[2], (D, D), jnp.float32) * sc, 'out_proj_b': jnp.zeros((D,), jnp.float32), 'Qp_w': jax.random.normal(ks[3], (R, D), jnp.float32) * sc, 'Qp_b': jnp.zeros((R,), jnp.float32), 'Kp_w': jax.random.normal(ks[4], (R, D), jnp.float32) * sc, 'Kp_b': jnp.zeros((R,), jnp.float32), 'Vp_w': jax.random.normal(ks[5], (D, D), jnp.float32) * sc, 'Vp_b': jnp.zeros((D,), jnp.float32), 'lam': jnp.float32(0.5), 'ff1_w': jax.random.normal(ks[6], (DFF, D), jnp.float32) * sc, 'ff1_b': jnp.zeros((DFF,), jnp.float32), 'ff2_w': jax.random.normal(ks[7], (D, DFF), jnp.float32) * sc, 'ff2_b': jnp.zeros((D,), jnp.float32), 'ln1_g': jnp.ones((D,), jnp.float32), 'ln1_b': jnp.zeros((D,), jnp.float32), 'ln2_g': jnp.ones((D,), jnp.float32), 'ln2_b': jnp.zeros((D,), jnp.float32)}
    _L0_attn_in = _L0_attn_setup()

    def _L0_ffn_setup():
        import jax, jax.numpy as jnp
        import numpy as np
        DIM = 128
        DEPTH = 6
        HEADS = 16
        DIM_HEAD = 64
        WINDOW = 32
        INNER = HEADS * DIM_HEAD
        DIM_INNER = int(DIM * 4 * 2 / 3)
        QK_SCALE = 8.0

        def shift_tokens(t):
            a, s = jnp.split(t, 2, -1)
            s = jnp.pad(s, ((0, 0), (1, 0), (0, 0)))[:, :-1]
            return jnp.concatenate([a, s], -1)

        def l2norm(t):
            return t / jnp.maximum(jnp.linalg.norm(t, axis=-1, keepdims=True), 1e-12)

        def rotate_half(x):
            x1, x2 = jnp.split(x, 2, -1)
            return jnp.concatenate([-x2, x1], -1)

        def rotary_tables(n):
            half = jnp.arange(0, DIM_HEAD, 2, dtype=jnp.float32)
            inv_freq = 1.0 / 10000.0 ** (half / DIM_HEAD)
            t = jnp.arange(n, dtype=jnp.float32)
            freqs = t[:, None] * inv_freq[None, :]
            freqs = jnp.concatenate([freqs, freqs], -1)
            base_scale = (half + 0.4 * DIM_HEAD) / (1.4 * DIM_HEAD)
            power = (t - n // 2) / (WINDOW // 2)
            scale = base_scale[None, :] ** power[:, None]
            scale = jnp.concatenate([scale, scale], -1)
            return (freqs, scale)

        def local_attention(q, k, v):
            b, h, n, d = q.shape
            w = WINDOW
            nw = n // w
            bq = q.reshape(b, h, nw, w, d)
            bk = k.reshape(b, h, nw, w, d)
            bv = v.reshape(b, h, nw, w, d)

            def look(t):
                p = jnp.pad(t, ((0, 0), (0, 0), (1, 0), (0, 0), (0, 0)))
                return jnp.concatenate([p[:, :, :nw], p[:, :, 1:]], axis=3)
            bk2, bv2 = (look(bk), look(bv))
            seq = jnp.arange(n).reshape(nw, w)
            seq_p = jnp.pad(seq, ((1, 0), (0, 0)), constant_values=-1)
            jt = jnp.concatenate([seq_p[:nw], seq_p[1:]], axis=1)
            it = seq[:, :, None]
            jb = jt[:, None, :]
            mask = (it < jb) | (it > jb + w) | (jb == -1)
            sim = jnp.einsum('bhwie,bhwje->bhwij', bq, bk2) * QK_SCALE
            sim = jnp.where(mask, -jnp.finfo(sim.dtype).max, sim)
            attn = jax.nn.softmax(sim, -1)
            out = jnp.einsum('bhwij,bhwje->bhwie', attn, bv2)
            return out.reshape(b, h, n, d)

        def attn_layer(x, Wqkv, qs, ksc, Wo):
            b, n, _ = x.shape
            qkv = x @ Wqkv
            q, k, v = jnp.split(qkv, 3, -1)
            sh = lambda t: t.reshape(b, n, HEADS, DIM_HEAD).transpose(0, 2, 1, 3)
            q, k, v = (sh(q), sh(k), sh(v))
            q = l2norm(q) * qs
            k = l2norm(k) * ksc
            freqs, scale = rotary_tables(n)
            cos, sin = (jnp.cos(freqs), jnp.sin(freqs))
            q = q * cos * scale + rotate_half(q) * sin * scale
            inv = 1.0 / scale
            k = k * cos * inv + rotate_half(k) * sin * inv
            out = local_attention(q, k, v)
            out = out.transpose(0, 2, 1, 3).reshape(b, n, INNER)
            return out @ Wo

        def ffn_layer(x, g, bln, W1, b1, W2, b2):
            mu = x.mean(-1, keepdims=True)
            var = ((x - mu) ** 2).mean(-1, keepdims=True)
            xn = (x - mu) / jnp.sqrt(var + 1e-05) * g + bln
            hg = xn @ W1 + b1
            a, gate = jnp.split(hg, 2, -1)
            return a * jax.nn.gelu(gate, approximate=False) @ W2 + b2
        key = jax.random.key(seed)
        ks = jax.random.split(key, 8)
        B, N = (2, 256)
        init = lambda k, shape: jax.random.normal(k, shape, jnp.float32) * 0.02
        return {'x': jax.random.normal(ks[0], (B, N, DIM), jnp.float32), 'Wqkv': init(ks[1], (DEPTH, DIM, 3 * INNER)), 'q_scale': jnp.ones((DEPTH, DIM_HEAD), jnp.float32), 'k_scale': jnp.ones((DEPTH, DIM_HEAD), jnp.float32), 'Wo': init(ks[2], (DEPTH, INNER, DIM)), 'ln_g': jnp.ones((DEPTH, DIM), jnp.float32), 'ln_b': jnp.zeros((DEPTH, DIM), jnp.float32), 'W1': init(ks[3], (DEPTH, DIM, 2 * DIM_INNER)), 'b1': jnp.zeros((DEPTH, 2 * DIM_INNER), jnp.float32), 'W2': init(ks[4], (DEPTH, DIM_INNER, DIM)), 'b2': jnp.zeros((DEPTH, DIM), jnp.float32)}
    _L0_ffn_in = _L0_ffn_setup()
    _d = {'L0_attn_src': _L0_attn_in['src'], 'L0_attn_in_proj_w': _L0_attn_in['in_proj_w'], 'L0_attn_in_proj_b': _L0_attn_in['in_proj_b'], 'L0_attn_out_proj_w': _L0_attn_in['out_proj_w'], 'L0_attn_out_proj_b': _L0_attn_in['out_proj_b'], 'L0_attn_Qp_w': _L0_attn_in['Qp_w'], 'L0_attn_Qp_b': _L0_attn_in['Qp_b'], 'L0_attn_Kp_w': _L0_attn_in['Kp_w'], 'L0_attn_Kp_b': _L0_attn_in['Kp_b'], 'L0_attn_Vp_w': _L0_attn_in['Vp_w'], 'L0_attn_Vp_b': _L0_attn_in['Vp_b'], 'L0_attn_lam': _L0_attn_in['lam'], 'L0_attn_ff1_w': _L0_attn_in['ff1_w'], 'L0_attn_ff1_b': _L0_attn_in['ff1_b'], 'L0_attn_ff2_w': _L0_attn_in['ff2_w'], 'L0_attn_ff2_b': _L0_attn_in['ff2_b'], 'L0_attn_ln1_g': _L0_attn_in['ln1_g'], 'L0_attn_ln1_b': _L0_attn_in['ln1_b'], 'L0_attn_ln2_g': _L0_attn_in['ln2_g'], 'L0_attn_ln2_b': _L0_attn_in['ln2_b'], 'L0_ffn_Wqkv': _L0_ffn_in['Wqkv'], 'L0_ffn_q_scale': _L0_ffn_in['q_scale'], 'L0_ffn_k_scale': _L0_ffn_in['k_scale'], 'L0_ffn_Wo': _L0_ffn_in['Wo'], 'L0_ffn_ln_g': _L0_ffn_in['ln_g'], 'L0_ffn_ln_b': _L0_ffn_in['ln_b'], 'L0_ffn_W1': _L0_ffn_in['W1'], 'L0_ffn_b1': _L0_ffn_in['b1'], 'L0_ffn_W2': _L0_ffn_in['W2'], 'L0_ffn_b2': _L0_ffn_in['b2']}
    _x0 = _d['L0_attn_src']
    _d['L0_attn_src'] = jax.random.normal(jax.random.fold_in(jax.random.key(seed), 1), (4, 1024, 128), dtype=_x0.dtype)
    del _x0
    return _d

def reference(L0_attn_src, L0_attn_in_proj_w, L0_attn_in_proj_b, L0_attn_out_proj_w, L0_attn_out_proj_b, L0_attn_Qp_w, L0_attn_Qp_b, L0_attn_Kp_w, L0_attn_Kp_b, L0_attn_Vp_w, L0_attn_Vp_b, L0_attn_lam, L0_attn_ff1_w, L0_attn_ff1_b, L0_attn_ff2_w, L0_attn_ff2_b, L0_attn_ln1_g, L0_attn_ln1_b, L0_attn_ln2_g, L0_attn_ln2_b, L0_ffn_Wqkv, L0_ffn_q_scale, L0_ffn_k_scale, L0_ffn_Wo, L0_ffn_ln_g, L0_ffn_ln_b, L0_ffn_W1, L0_ffn_b1, L0_ffn_W2, L0_ffn_b2):

    def _L0_attn_ref(src, in_proj_w, in_proj_b, out_proj_w, out_proj_b, Qp_w, Qp_b, Kp_w, Kp_b, Vp_w, Vp_b, lam, ff1_w, ff1_b, ff2_w, ff2_b, ln1_g, ln1_b, ln2_g, ln2_b):
        import jax, jax.numpy as jnp
        import numpy as np
        import math
        B, S, D, H, R, DFF = (4, 128, 128, 16, 64, 512)

        def _layernorm(x, g, b, eps=1e-05):
            m = jnp.mean(x, axis=-1, keepdims=True)
            v = jnp.var(x, axis=-1, keepdims=True)
            return (x - m) / jnp.sqrt(v + eps) * g + b
        b, s, d = src.shape
        dh = d // H
        qkv = src @ in_proj_w.T + in_proj_b
        q, k, v = jnp.split(qkv, 3, axis=-1)
        q = q.reshape(b, s, H, dh).transpose(0, 2, 1, 3)
        k = k.reshape(b, s, H, dh).transpose(0, 2, 1, 3)
        v = v.reshape(b, s, H, dh).transpose(0, 2, 1, 3)
        scores = jnp.einsum('bhqd,bhkd->bhqk', q, k) / math.sqrt(dh)
        attn = jax.nn.softmax(scores, axis=-1)
        ctx = jnp.einsum('bhqk,bhkd->bhqd', attn, v)
        ctx = ctx.transpose(0, 2, 1, 3).reshape(b, s, d)
        dense_output = ctx @ out_proj_w.T + out_proj_b
        Q = src @ Qp_w.T + Qp_b
        K = src @ Kp_w.T + Kp_b
        V = src @ Vp_w.T + Vp_b
        QK = jnp.einsum('bqr,bkr->bqk', Q, K) / math.sqrt(R)
        aw = jax.nn.softmax(QK, axis=-1)
        kk = max(1, int(s * 0.2))
        topv, topi = jax.lax.top_k(aw, kk)
        bi = jnp.arange(b)[:, None, None]
        si = jnp.arange(s)[None, :, None]
        sparse_attn = jnp.zeros_like(aw).at[bi, si, topi].set(topv)
        sparse_attn = sparse_attn / (jnp.sum(sparse_attn, axis=-1, keepdims=True) + 1e-09)
        sparse_output = jnp.einsum('bqk,bkd->bqd', sparse_attn, V)
        sig = jax.nn.sigmoid(lam)
        fused = sig * dense_output + (1.0 - sig) * sparse_output
        x = _layernorm(src + fused, ln1_g, ln1_b)
        ff = jax.nn.relu(x @ ff1_w.T + ff1_b) @ ff2_w.T + ff2_b
        return _layernorm(x + ff, ln2_g, ln2_b)

    def _L0_ffn_ref(x, Wqkv, q_scale, k_scale, Wo, ln_g, ln_b, W1, b1, W2, b2):
        import jax, jax.numpy as jnp
        import numpy as np
        DIM = 128
        DEPTH = 6
        HEADS = 16
        DIM_HEAD = 64
        WINDOW = 32
        INNER = HEADS * DIM_HEAD
        DIM_INNER = int(DIM * 4 * 2 / 3)
        QK_SCALE = 8.0

        def shift_tokens(t):
            a, s = jnp.split(t, 2, -1)
            s = jnp.pad(s, ((0, 0), (1, 0), (0, 0)))[:, :-1]
            return jnp.concatenate([a, s], -1)

        def l2norm(t):
            return t / jnp.maximum(jnp.linalg.norm(t, axis=-1, keepdims=True), 1e-12)

        def rotate_half(x):
            x1, x2 = jnp.split(x, 2, -1)
            return jnp.concatenate([-x2, x1], -1)

        def rotary_tables(n):
            half = jnp.arange(0, DIM_HEAD, 2, dtype=jnp.float32)
            inv_freq = 1.0 / 10000.0 ** (half / DIM_HEAD)
            t = jnp.arange(n, dtype=jnp.float32)
            freqs = t[:, None] * inv_freq[None, :]
            freqs = jnp.concatenate([freqs, freqs], -1)
            base_scale = (half + 0.4 * DIM_HEAD) / (1.4 * DIM_HEAD)
            power = (t - n // 2) / (WINDOW // 2)
            scale = base_scale[None, :] ** power[:, None]
            scale = jnp.concatenate([scale, scale], -1)
            return (freqs, scale)

        def local_attention(q, k, v):
            b, h, n, d = q.shape
            w = WINDOW
            nw = n // w
            bq = q.reshape(b, h, nw, w, d)
            bk = k.reshape(b, h, nw, w, d)
            bv = v.reshape(b, h, nw, w, d)

            def look(t):
                p = jnp.pad(t, ((0, 0), (0, 0), (1, 0), (0, 0), (0, 0)))
                return jnp.concatenate([p[:, :, :nw], p[:, :, 1:]], axis=3)
            bk2, bv2 = (look(bk), look(bv))
            seq = jnp.arange(n).reshape(nw, w)
            seq_p = jnp.pad(seq, ((1, 0), (0, 0)), constant_values=-1)
            jt = jnp.concatenate([seq_p[:nw], seq_p[1:]], axis=1)
            it = seq[:, :, None]
            jb = jt[:, None, :]
            mask = (it < jb) | (it > jb + w) | (jb == -1)
            sim = jnp.einsum('bhwie,bhwje->bhwij', bq, bk2) * QK_SCALE
            sim = jnp.where(mask, -jnp.finfo(sim.dtype).max, sim)
            attn = jax.nn.softmax(sim, -1)
            out = jnp.einsum('bhwij,bhwje->bhwie', attn, bv2)
            return out.reshape(b, h, n, d)

        def attn_layer(x, Wqkv, qs, ksc, Wo):
            b, n, _ = x.shape
            qkv = x @ Wqkv
            q, k, v = jnp.split(qkv, 3, -1)
            sh = lambda t: t.reshape(b, n, HEADS, DIM_HEAD).transpose(0, 2, 1, 3)
            q, k, v = (sh(q), sh(k), sh(v))
            q = l2norm(q) * qs
            k = l2norm(k) * ksc
            freqs, scale = rotary_tables(n)
            cos, sin = (jnp.cos(freqs), jnp.sin(freqs))
            q = q * cos * scale + rotate_half(q) * sin * scale
            inv = 1.0 / scale
            k = k * cos * inv + rotate_half(k) * sin * inv
            out = local_attention(q, k, v)
            out = out.transpose(0, 2, 1, 3).reshape(b, n, INNER)
            return out @ Wo

        def ffn_layer(x, g, bln, W1, b1, W2, b2):
            mu = x.mean(-1, keepdims=True)
            var = ((x - mu) ** 2).mean(-1, keepdims=True)
            xn = (x - mu) / jnp.sqrt(var + 1e-05) * g + bln
            hg = xn @ W1 + b1
            a, gate = jnp.split(hg, 2, -1)
            return a * jax.nn.gelu(gate, approximate=False) @ W2 + b2
        for i in range(DEPTH):
            x = attn_layer(shift_tokens(x), Wqkv[i], q_scale[i], k_scale[i], Wo[i]) + x
            x = ffn_layer(shift_tokens(x), ln_g[i], ln_b[i], W1[i], b1[i], W2[i], b2[i]) + x
        return x
    x = L0_attn_src
    x = x + _L0_attn_ref(_layernorm(x, axis=-1), L0_attn_in_proj_w, L0_attn_in_proj_b, L0_attn_out_proj_w, L0_attn_out_proj_b, L0_attn_Qp_w, L0_attn_Qp_b, L0_attn_Kp_w, L0_attn_Kp_b, L0_attn_Vp_w, L0_attn_Vp_b, L0_attn_lam, L0_attn_ff1_w, L0_attn_ff1_b, L0_attn_ff2_w, L0_attn_ff2_b, L0_attn_ln1_g, L0_attn_ln1_b, L0_attn_ln2_g, L0_attn_ln2_b)
    x = x + _L0_ffn_ref(_layernorm(x, axis=-1), L0_ffn_Wqkv, L0_ffn_q_scale, L0_ffn_k_scale, L0_ffn_Wo, L0_ffn_ln_g, L0_ffn_ln_b, L0_ffn_W1, L0_ffn_b1, L0_ffn_W2, L0_ffn_b2)
    return x

_drawn_inputs = setup_inputs


def setup_inputs(seed=0):
    import zlib

    import numpy as np

    out = dict(_drawn_inputs(seed))
    spreads = {'L0_attn_in_proj_b': (0.0, 0.8),
     'L0_attn_out_proj_b': (0.0, 0.28),
     'L0_attn_Qp_b': (0.0, 0.8),
     'L0_attn_Kp_b': (0.0, 2.0),
     'L0_attn_Vp_b': (0.0, 0.408),
     'L0_attn_ff1_b': (0.0, 0.51),
     'L0_attn_ff2_b': (0.0, 0.1),
     'L0_attn_ln1_g': (1.0, 0.2),
     'L0_attn_ln1_b': (0.0, 0.1),
     'L0_attn_ln2_g': (1.0, 0.2),
     'L0_attn_ln2_b': (0.0, 0.1),
     'L0_ffn_q_scale': (1.0, 0.6),
     'L0_ffn_k_scale': (1.0, 0.6),
     'L0_ffn_ln_g': (1.0, 0.6),
     'L0_ffn_ln_b': (0.0, 0.8),
     'L0_ffn_b1': (0.0, 0.8),
     'L0_ffn_b2': (0.0, 0.289)}
    factors = {'L0_attn_in_proj_w': 8.0,
     'L0_attn_out_proj_w': 8.0,
     'L0_attn_Qp_w': 8.0,
     'L0_attn_Kp_w': 8.0,
     'L0_attn_Vp_w': 8.0,
     'L0_ffn_W1': 5.449,
     'L0_ffn_W2': 5.354}
    for name, (base, spread) in spreads.items():
        noise = np.random.default_rng([zlib.crc32(name.encode()), seed]).standard_normal(out[name].shape)
        drawn = base * np.exp(spread * noise) if base else spread * noise
        out[name] = jnp.asarray(drawn.astype(out[name].dtype))
    for name, factor in factors.items():
        out[name] = (out[name] * factor).astype(out[name].dtype)
    return out
```

```python
import concourse.bass as bass
from concourse import mybir
from contextlib import ExitStack
import numpy as np

F32 = mybir.dt.float32
BF16 = mybir.dt.bfloat16
I32 = mybir.dt.int32
ACT = mybir.ActivationFunctionType
ALU = mybir.AluOpType
AX = mybir.AxisListType

P = 128
BATCH, SEQ = 4, 1024
TPB = SEQ // P
TILES = BATCH * TPB
EPS = 1e-5
AH, AD = 16, 8
AP_ = AH // 2
RANK = 64
KEEP = int(SEQ * 0.2)
AFF = 512
PARTS_Q = (0, 0, 1, 0, 2, 1)
PARTS_K = (0, 1, 0, 2, 0, 1)
MROW = 48


DEPTH, HEADS, DH = 6, 16, 64
PAIRS = HEADS // 2
INNER = HEADS * DH
WIN = 32
NWIN = P // WIN
SPAN = 2 * WIN
FF = 341
FFC = [(0, 128), (128, 128), (256, FF - 256)]
QK_SCALE = 8.0


def stage_a(nc, X, src, scratch, wqk, wqs, wks, wv2, wout, wf1, wf2, rows, cols, ident, onesrow, lam):
    ctx = ExitStack()
    with ctx:
        def sb(name, shape, dt=F32):
            return ctx.enter_context(nc.sbuf_tensor("a_" + name, shape, dt))

        def pb(name, shape, dt=F32):
            return ctx.enter_context(nc.psum_tensor("a_" + name, shape, dt))

        def sem(name):
            return ctx.enter_context(nc.semaphore("a_" + name))

        IDN = sb("IDN", [P, P])
        IDB = sb("IDB", [P, P], BF16)
        ONR = sb("ONR", [P, P])
        WQK = sb("WQK", [P, 2, P])
        WQS = sb("WQS", [P, RANK])
        WKS = sb("WKS", [P, RANK])
        WV2 = sb("WV2", [P, 2 * P])
        WOUT = sb("WOUT", [P, P])
        WF1 = sb("WF1", [P, AFF])
        WF2 = sb("WF2", [P, 4, P])
        ROWS = sb("ROWS", [P, 4 * P])
        GB = sb("GB", [P, 4, P])
        COLS = sb("COLS", [P, 9])
        LAM = sb("LAM", [P, 1])
        SG = sb("SG", [P, 4])
        ST = sb("ST", [P, TPB, 6])
        MV = sb("MV", [P, TPB, 2])
        VE = sb("VE", [P, TPB])
        RS = sb("RS", [P, TPB])
        NHf = sb("NHf", [P, TPB])
        XNa = sb("XNa", [P, TPB, P])
        XT = sb("XT", [P, SEQ])
        Q32 = sb("Q32", [P, SEQ])
        QR = sb("QR", [P, SEQ])
        QP3 = sb("QP3", [P, 2, 3, SEQ], BF16)
        QPK = [sb(f"QPK{i}", [P, SEQ], BF16) for i in range(2)]
        KPK = [sb(f"KPK{i}", [P, SEQ], BF16) for i in range(2)]
        QM = [sb(f"QM{i}", [P, SEQ], BF16) for i in range(2)]
        V8 = sb("V8", [P, TPB, AH, AD])
        V9 = [sb(f"V9{i}", [P, TPB, 2, 32]) for i in range(2)]
        SQ = sb("SQ", [RANK, SEQ])
        SK = sb("SK", [RANK, SEQ])
        SV = sb("SV", [P, TPB, P])
        E = sb("E", [P, TPB, SEQ])
        Z = sb("Z", [P, TPB])
        SM = sb("SM", [P, TPB])
        SMS = sb("SMS", [P, TPB])
        J = sb("J", [P, TPB, SEQ], BF16)
        THR = sb("THR", [P, TPB], I32)
        CND = sb("CND", [P, TPB], I32)
        BIT = sb("BIT", [P, TPB], I32)
        CNT = sb("CNT", [P, TPB])
        MSK = sb("MSK", [P, TPB], I32)
        REM = sb("REM", [P, TPB])
        TOP = sb("TOP", [P, TPB])
        DEN = sb("DEN", [P, TPB])
        RDN = sb("RDN", [P, TPB])
        EQ = sb("EQ", [P, SEQ])
        RK = sb("RK", [P, SEQ])
        GT = sb("GT", [P, SEQ])
        W = sb("W", [P, SEQ])
        WT = sb("WT", [P, TPB, P])
        MX = sb("MX", [P, 2, TPB, 2])
        NM = sb("NM", [P, 2, TPB])
        NR = sb("NR", [P, 2, TPB])
        MT = sb("MT", [P, TPB, P], BF16)
        PX = [sb(f"PX{i}", [P, SEQ]) for i in range(2)]
        OE = sb("OE", [P, 512])
        RC = sb("RC", [P, 2, 2, 4])
        CX = sb("CX", [P, TPB, P])
        CT = sb("CT", [P, TPB, P])
        SP_ = sb("SP", [P, TPB, P])
        R1 = sb("R1", [P, TPB, P])
        X1T = sb("X1T", [P, SEQ])
        HT = sb("HT", [P, 4, SEQ])

        MXP = [pb(f"MXP{i}", [P, 512]) for i in range(2)]
        EXP = [pb(f"EXP{i}", [P, 1024]) for i in range(2)]
        OP = pb("OP", [P, 512])
        MI = pb("MI", [P, 512])
        MIB = MI[:, :].bitcast(BF16)

        names = """loaded zeroed var rstd xn xT_ps xT_ready q_ps split parts_stored pack0 pack1 s_ps s_ready v_ps v_ready
            ss_ps ssm_ready e_ready v9 mx_ps mx_red nm mt_ps qm st_ps exp pv_ps oe ot_ps ctx cT_ps cT_ready
            dense_ps w_ready wT_ps wT_ready sp_ps r1 x1 x1T_ps x1T_ready h_ps h_ready ff_ps ff_ready r2 xo lam_e
            sig pe_step sp_step thr xout""".split()
        S = {n: sem(n) for n in names}
        NL = 14

        def at(N, n, k):
            return N * n + k

        block = ctx.enter_context(nc.Block())

        @block.sync
        def _(e):
            e.dma_start(X[:, :, :], src.rearrange("b (t p) d -> p (b t) d", p=P)).then_inc(S["loaded"], 16)
            e.wait_ge(S["zeroed"], 1)
            for dst, s_ in ((IDN[:, :], ident), (ONR[:, :], onesrow), (WQK[:, :, :], wqk), (WQS[:, :], wqs),
                            (WKS[:, :], wks), (WV2[:, :], wv2), (WOUT[:, :], wout), (WF1[:, :], wf1),
                            (WF2[:, :, :], wf2), (ROWS[0:1, :], rows[0:1, 0:4 * P]),
                            (GB[:, :, :].rearrange("p a d -> p (a d)"), rows[0:1, 4 * P:8 * P].to_broadcast([P, 4 * P])),
                            (COLS[:, :], cols), (LAM[:, :], lam.to_broadcast([P, 1]))):
                e.dma_start(dst, s_).then_inc(S["loaded"], 16)
            e.wait_ge(S["sig"], 1)
            e.sem_inc(S["sp_step"], 1)
            with e.Fori(0, BATCH) as b:
                for i in range(2):
                    e.wait_ge(S["split"], b * 2 + i + 1)
                    for k in range(3):
                        e.dma_start(scratch[i, k], QP3[:, i, k, :]).then_inc(S["parts_stored"], 16)
                e.wait_ge(S["parts_stored"], (b + 1) * (16 * 6))
                e.sem_inc(S["sp_step"], 1)
                with e.Fori(0, AP_ // 2) as gp:
                    for s in range(2):
                        e.wait_ge(S["ctx"], b * AP_ + gp * 2 + s + 1)
                        p = gp * 2 + s
                        for i, (dst, parts) in enumerate(((QPK[s], PARTS_Q), (KPK[s], PARTS_K))):
                            for a in range(2):
                                for g, k in enumerate(parts):
                                    e.dma_start(dst[64 * a + 8 * g:64 * a + 8 * g + 8, :],
                                                scratch[i, k, bass.ds(p * 16 + 8 * a, 8), :]).then_inc(S["pack%d" % s], 16)
            e.wait_ge(S["xout"], 1)

        NPACK = 16 * 24

        @block.gpsimd
        def _(e):
            e.memset(NHf[:, :], -0.5)
            e.memset(ROWS[:, :], 0.0)
            e.memset(MT[:, :, :], 0.0)
            for s in range(2):
                e.memset(QPK[s][:, :], 0.0)
                e.memset(KPK[s][:, :], 0.0)
                e.memset(V9[s][:, :, :, :], 0.0)
            e.drain()
            for s in range(2):
                e.memset(V9[s][:, :, :, AD:AD + 1], 1.0)
            e.drain().then_inc(S["zeroed"], 1)
            with e.Fori(0, BATCH) as b:
                for k in range(3):
                    e.wait_ge(S["var"], b * 3 + k + 1)
                    e.tensor_tensor(RS[:, :], VE[:, :], NHf[:, :], ALU.pow).then_inc(S["rstd"], 1)

        @block.tensor
        def _(e):
            LD = NL * 16

            def max_unit(N, s, u):
                qt, a = u // 2, u % 2
                for h in range(2):
                    if u >= 1:
                        e.wait_ge(S["mx_red"], N * 32 + (2 * u + h - 1))
                        e.sem_inc(S["pe_step"], 1)
                    e.matmul(MXP[h][:, :], QPK[s][64 * a:64 * a + 64, P * qt:P * qt + P],
                             KPK[s][64 * a:64 * a + 64, 512 * h:512 * h + 512], start=True, stop=True)\
                        .then_inc(S["mx_ps"], 1)

            def m_transposes(N, s):
                e.wait_ge(S["nm"], N + 1)
                e.wait_ge(S["ctx"], N + 1)
                for t in range(TPB):
                    x = e.transpose(MIB[:, P * t:P * t + P], MT[:, t, :], IDB[:, :])
                x.then_inc(S["mt_ps"], 1)

            def pv(N, s, u):
                c, kp, a = u // 8, (u // 2) % 4, u % 2
                q = 2 * a + c
                e.wait_ge(S["exp"], N * 16 + (u + 1))
                for j in range(2):
                    x = e.matmul(OP[32 * q:32 * q + 32, :], V9[s][:, 2 * kp + j, a, :],
                                 PX[a][:, 512 * j:512 * j + 512], start=(kp == 0 and j == 0),
                                 stop=(kp == 3 and j == 1))
                x.then_inc(S["pv_ps"], 1)

            def pair(N, h, s, nxt):
                e.wait_ge(S["qm"], N + 2)
                e.sem_inc(S["pe_step"], 1)
                if nxt:
                    e.wait_ge(S["pack%d" % (1 - s)], (h + 1 + s) * NPACK)
                    e.sem_inc(S["pe_step"], 1)
                e.wait_ge(S["v9"], N + 1)
                e.sem_inc(S["pe_step"], 1)
                for u in range(17):
                    if u < 16:
                        c, kp, a = u // 8, (u // 2) % 4, u % 2
                        if u >= 2:
                            e.wait_ge(S["exp"], N * 16 + (u - 1))
                            e.sem_inc(S["pe_step"], 1)
                        for j in range(2):
                            x = e.matmul(EXP[a][:, 512 * j:512 * j + 512],
                                         KPK[s][64 * a:64 * a + 64, P * (2 * kp + j):P * (2 * kp + j) + P],
                                         QM[s][64 * a:64 * a + 64, 512 * c:512 * c + 512], start=True, stop=True)
                        x.then_inc(S["st_ps"], 1)
                        if nxt:
                            max_unit(N + 1, 1 - s, u)
                    if u >= 1:
                        pv(N, s, u - 1)
                if nxt:
                    m_transposes(N + 1, 1 - s)
                    e.wait_ge(S["qm"], N + 3)
                else:
                    e.wait_ge(S["ctx"], N + 2)
                e.wait_ge(S["oe"], N + 1)
                for t in range(4):
                    x = e.transpose(MI[:, P * t:P * t + P], OE[:, P * t:P * t + P], IDN[:, :])
                x.then_inc(S["ot_ps"], 1)

            e.wait_ge(S["loaded"], LD)
            e.wait_ge(S["sig"], 1)
            with e.Fori(0, BATCH) as b:
                e.wait_ge(S["xn"], b + 1)
                for t in range(TPB):
                    x = e.transpose(EXP[0][:, P * t:P * t + P], XNa[:, t, :], IDN[:, :])
                x.then_inc(S["xT_ps"], 1)
                e.wait_ge(S["xT_ready"], b + 1)
                for i in range(2):
                    for c in range(2):
                        x = e.matmul(EXP[i][:, 512 * c:512 * c + 512], WQK[:, i, :], XT[:, 512 * c:512 * c + 512],
                                     start=True, stop=True)
                    x.then_inc(S["q_ps"], 1)
                for i, w in enumerate((WQS, WKS)):
                    for c in range(2):
                        if i == 1:
                            e.wait_ge(S["s_ready"], b * 4 + c + 1)
                        e.matmul(MXP[c][0:RANK, :], w[:, :], XT[:, 512 * c:512 * c + 512],
                                 start=True, stop=True).then_inc(S["s_ps"], 1)
                for t in range(TPB):
                    if t % 4 == 0:
                        e.wait_ge(S["split"], b * 2 + t // 4 + 1)
                    o = EXP[t // 4][:, 256 * (t % 4):256 * (t % 4) + 256]
                    e.matmul(o, XT[:, P * t:P * t + P], WV2[:, :], start=True, stop=False)
                    x = e.matmul(o, ONR[:, :], ROWS[:, 0:256], start=False, stop=True)
                    if t % 4 == 3:
                        x.then_inc(S["v_ps"], 1)
                e.wait_ge(S["s_ready"], b * 4 + 4)
                for t in range(TPB):
                    if t < 2:
                        e.wait_ge(S["v_ready"], b * 2 + t + 1)
                    else:
                        e.wait_ge(S["e_ready"], b * TPB + t - 1)
                    e.sem_inc(S["pe_step"], 1)
                    for c in range(2):
                        x = e.matmul(EXP[t % 2][:, 512 * c:512 * c + 512], SQ[:, P * t:P * t + P],
                                     SK[:, 512 * c:512 * c + 512], start=True, stop=True)
                    x.then_inc(S["ss_ps"], 1)
                e.wait_ge(S["pack0"], b * (AP_ // 2 * NPACK) + NPACK)
                e.sem_inc(S["pe_step"], 1)
                e.wait_ge(S["e_ready"], b * TPB + TPB)
                e.sem_inc(S["pe_step"], 1)
                for u in range(16):
                    max_unit(b * AP_, 0, u)
                m_transposes(b * AP_, 0)
                with e.Fori(0, AP_ // 2 - 1) as gp:
                    for s in range(2):
                        pair(b * AP_ + gp * 2 + s, b * (AP_ // 2) + gp, s, True)
                pair(b * AP_ + (AP_ - 2), b * (AP_ // 2) + (AP_ // 2 - 1), 0, True)
                pair(b * AP_ + (AP_ - 1), b * (AP_ // 2) + (AP_ // 2 - 1), 1, False)
                e.wait_ge(S["ctx"], (b + 1) * AP_ + 2)
                for t in range(TPB):
                    x = e.transpose(EXP[0][:, P * t:P * t + P], CX[:, t, :], IDN[:, :])
                x.then_inc(S["cT_ps"], 1)
                e.wait_ge(S["cT_ready"], b + 1)
                for t in range(TPB):
                    o = EXP[1][:, P * t:P * t + P]
                    e.matmul(o, CT[:, t, :], WOUT[:, :], start=True, stop=False)
                    x = e.matmul(o, ONR[:, :], ROWS[:, 2 * P:3 * P], start=False, stop=True)
                x.then_inc(S["dense_ps"], 1)
                for t in range(TPB):
                    e.wait_ge(S["w_ready"], b * TPB + t + 1)
                    for k in range(TPB):
                        x = e.transpose(EXP[0][:, P * k:P * k + P], W[:, P * k:P * k + P], IDN[:, :])
                    x.then_inc(S["wT_ps"], 1)
                    e.wait_ge(S["wT_ready"], b * TPB + t + 1)
                    if t >= 1:
                        e.wait_ge(S["r1"], b * TPB + t)
                    for k in range(TPB):
                        x = e.matmul(OP[:, 0:P], WT[:, k, :], SV[:, k, :], start=(k == 0), stop=(k == TPB - 1))
                    x.then_inc(S["sp_ps"], 1)
                e.wait_ge(S["x1"], b + 1)
                for t in range(TPB):
                    x = e.transpose(EXP[0][:, P * t:P * t + P], R1[:, t, :], IDN[:, :])
                x.then_inc(S["x1T_ps"], 1)
                e.wait_ge(S["x1T_ready"], b + 1)
                for j in range(4):
                    if j >= 2:
                        e.wait_ge(S["h_ready"], b * 4 + j - 1)
                    for c in range(2):
                        x = e.matmul(EXP[j % 2][:, 512 * c:512 * c + 512], WF1[:, P * j:P * j + P],
                                     X1T[:, 512 * c:512 * c + 512], start=True, stop=True)
                    x.then_inc(S["h_ps"], 1)
                e.wait_ge(S["h_ready"], b * 4 + 4)
                for t in range(TPB):
                    o = EXP[1][:, P * t:P * t + P] if 0 else (MXP[t // 4][:, P * (t % 4):P * (t % 4) + P])
                    for j in range(4):
                        e.matmul(o, HT[:, j, P * t:P * t + P], WF2[:, j, :], start=(j == 0), stop=False)
                    x = e.matmul(o, ONR[:, :], ROWS[:, 3 * P:4 * P], start=False, stop=True)
                x.then_inc(S["ff_ps"], 1)

        @block.scalar
        def _(e):
            e.wait_ge(S["loaded"], NL * 16)
            e.activation(SG[:, 0:1], LAM[:, :], ACT.Exp, scale=-1.0).then_inc(S["lam_e"], 1)

            def v9_copy(N, s, p):
                e.activation(V9[s][:, :, :, 0:AD], V8[:, :, bass.ds(p * 2, 2), :], ACT.Copy).then_inc(S["v9"], 1)

            def exps(N):
                for u in range(16):
                    a = u % 2
                    e.wait_ge(S["st_ps"], N * 16 + (u + 1))
                    e.activation(PX[a][:, :], EXP[a][:, :], ACT.Exp, scale=AD ** -0.5).then_inc(S["exp"], 1)

            with e.Fori(0, BATCH) as b:
                e.wait_ge(S["xT_ps"], b + 1)
                e.activation(XT[:, :], EXP[0][:, :], ACT.Copy).then_inc(S["xT_ready"], 1)
                for i, dst in enumerate((SQ, SK)):
                    for c in range(2):
                        e.wait_ge(S["s_ps"], b * 4 + 2 * i + c + 1)
                        e.activation(dst[:, 512 * c:512 * c + 512], MXP[c][0:RANK, :], ACT.Identity,
                                     bias=COLS[0:RANK, 2 + i:3 + i]).then_inc(S["s_ready"], 1)
                for i in range(2):
                    e.wait_ge(S["v_ps"], b * 2 + i + 1)
                    v = EXP[i][:, :].rearrange("p (t x) -> p t x", t=4)
                    e.activation(V8[:, 4 * i:4 * i + 4, :, :].rearrange("p t h d -> p t (h d)"), v[:, :, 0:P], ACT.Copy)
                    e.activation(SV[:, 4 * i:4 * i + 4, :], v[:, :, P:2 * P], ACT.Copy)
                    e.drain().then_inc(S["v_ready"], 1)
                for t in range(TPB):
                    e.wait_ge(S["ssm_ready"], b * TPB + t + 1)
                    e.activation(E[:, t, :], EXP[t % 2][:, :], ACT.Exp, bias=SMS[:, t:t + 1], scale=RANK ** -0.5,
                                 accum_out=Z[:, t:t + 1]).then_inc(S["e_ready"], 1)
                with e.Fori(0, AP_ // 2) as gp:
                    for s in range(2):
                        N = b * AP_ + gp * 2 + s
                        v9_copy(N, s, gp * 2 + s)
                        exps(N)
                e.wait_ge(S["cT_ps"], b + 1)
                e.activation(CT[:, :, :].rearrange("p t d -> p (t d)"), EXP[0][:, :], ACT.Copy).then_inc(S["cT_ready"], 1)
                for t in range(TPB):
                    e.wait_ge(S["wT_ps"], b * TPB + t + 1)
                    e.activation(WT[:, :, :].rearrange("p t d -> p (t d)"), EXP[0][:, :], ACT.Copy)\
                        .then_inc(S["wT_ready"], 1)
                e.wait_ge(S["x1T_ps"], b + 1)
                e.activation(X1T[:, :], EXP[0][:, :], ACT.Copy).then_inc(S["x1T_ready"], 1)
                for j in range(4):
                    e.wait_ge(S["h_ps"], b * 4 + j + 1)
                    e.activation(HT[:, j, :], EXP[j % 2][:, :], ACT.Relu, bias=COLS[:, 4 + j:5 + j])\
                        .then_inc(S["h_ready"], 1)

        @block.vector
        def _(e):
            e.wait_ge(S["loaded"], NL * 16)
            e.wait_ge(S["lam_e"], 1)
            e.tensor_scalar(SG[:, 1:2], SG[:, 0:1], 1.0, None, ALU.add)
            e.drain()
            e.reciprocal(SG[:, 2:3], SG[:, 1:2])
            e.drain()
            e.tensor_scalar(SG[:, 3:4], SG[:, 2:3], -1.0, 1.0, ALU.mult, ALU.add)
            e.tensor_copy(IDB[:, :], IDN[:, :])
            for s in range(2):
                e.tensor_scalar(KPK[s][:, :], KPK[s][:, :], COLS[:, 8:9], None, ALU.add)
            e.drain().then_inc(S["sig"], 1)
            e.sem_inc(S["ctx"], 2)
            e.sem_inc(S["qm"], 1)

            def layernorm(get, put, nth, b):
                for t in range(TPB):
                    e.bn_stats(ST[:, t, :], get(t))
                e.drain()
                for t in range(TPB):
                    e.bn_aggr(MV[:, t, :], ST[:, t, :])
                e.drain()
                e.tensor_scalar(VE[:, :], MV[:, :, 1], EPS, None, ALU.add).then_inc(S["var"], 1)
                e.wait_ge(S["rstd"], b * 3 + nth + 1)
                for t in range(TPB):
                    x = e.tensor_scalar(put(t), get(t), MV[:, t, 0:1], RS[:, t:t + 1], ALU.subtract, ALU.mult)
                return x

            def maxima(N, s):
                for u in range(16):
                    qt, a = u // 2, u % 2
                    for h in range(2):
                        e.wait_ge(S["mx_ps"], N * 32 + (2 * u + h + 1))
                        e.tensor_reduce(MX[:, a, qt, h:h + 1], MXP[h][:, :], AX.X, ALU.max).then_inc(S["mx_red"], 1)
                e.drain()
                e.tensor_reduce(NM[:, :, :], MX[:, :, :, :], AX.X, ALU.max, negate=True)
                e.drain()
                mt = MT[:, :, :].rearrange("p t (a r) -> p a t r", a=2)
                for k in range(3):
                    e.tensor_copy(mt[:, :, :, MROW + k], NM[:, :, :])
                    e.drain()
                    if k < 2:
                        e.tensor_tensor(NM[:, :, :], NM[:, :, :], mt[:, :, :, MROW + k], ALU.subtract)
                        e.drain()
                e.drain().then_inc(S["nm"], 1)

            def add_m(N, s):
                e.wait_ge(S["mt_ps"], N + 1)
                e.tensor_tensor(QM[s][:, :], QPK[s][:, :], MIB, ALU.add).then_inc(S["qm"], 1)

            def context(N, s, p, nxt):
                if nxt:
                    maxima(N + 1, 1 - s)
                e.wait_ge(S["pv_ps"], N * 16 + 16)
                e.tensor_copy(OE[:, :], OP[:, :]).then_inc(S["oe"], 1)
                if nxt:
                    add_m(N + 1, 1 - s)
                e.wait_ge(S["ot_ps"], N + 1)
                o = MI[:, :].rearrange("p (t a c r) -> p a c t r", t=4, a=2, c=2)
                for a in range(2):
                    e.reciprocal(RC[:, a, :, :], o[:, a, :, :, AD])
                e.drain()
                for a in range(2):
                    x = e.tensor_tensor(CX[:, :, bass.ds(p * 16 + 8 * a, AD)].rearrange("p (c t) d -> p c t d", c=2),
                                        o[:, a, :, :, 0:AD], RC[:, a, :, :].unsqueeze(3).to_broadcast([P, 2, 4, AD]),
                                        ALU.mult)
                e.drain().then_inc(S["ctx"], 1)

            with e.Fori(0, BATCH) as b:
                xt = lambda t: X[:, bass.ds(b * TPB + t, 1), :].rearrange("p a d -> p (a d)")
                layernorm(xt, lambda t: XNa[:, t, :], 0, b)
                e.drain().then_inc(S["xn"], 1)
                for i in range(2):
                    e.wait_ge(S["q_ps"], b * 2 + i + 1)
                    e.tensor_scalar(Q32[:, :], EXP[i][:, :], COLS[:, i:i + 1], None, ALU.add)
                    e.drain()
                    e.tensor_copy(QP3[:, i, 0, :], Q32[:, :])
                    e.drain()
                    e.tensor_tensor(QR[:, :], Q32[:, :], QP3[:, i, 0, :], ALU.subtract)
                    e.drain()
                    e.tensor_copy(QP3[:, i, 1, :], QR[:, :])
                    e.drain()
                    e.tensor_tensor(QP3[:, i, 2, :], QR[:, :], QP3[:, i, 1, :], ALU.subtract).then_inc(S["split"], 1)
                for t in range(TPB):
                    e.wait_ge(S["ss_ps"], b * TPB + t + 1)
                    e.tensor_reduce(SM[:, t:t + 1], EXP[t % 2][:, :], AX.X, ALU.max, negate=True)
                    e.drain()
                    e.tensor_scalar(SMS[:, t:t + 1], SM[:, t:t + 1], RANK ** -0.5, None, ALU.mult).then_inc(S["ssm_ready"], 1)
                maxima(b * AP_, 0)
                add_m(b * AP_, 0)
                with e.Fori(0, AP_ // 2 - 1) as gp:
                    for s in range(2):
                        context(b * AP_ + gp * 2 + s, s, gp * 2 + s, True)
                context(b * AP_ + (AP_ - 2), 0, AP_ - 2, True)
                context(b * AP_ + (AP_ - 1), 1, AP_ - 1, False)
                e.wait_ge(S["e_ready"], b * TPB + TPB)
                e.memset(THR[:, :], 0)
                e.memset(BIT[:, :], 1 << 29)
                e.drain()
                with e.Fori(0, 30) as it:
                    e.tensor_tensor(CND[:, :], THR[:, :], BIT[:, :], ALU.bitwise_or)
                    e.drain()
                    for t in range(TPB):
                        e.tensor_scalar(J[:, t, :], E[:, t, :], CND[:, t:t + 1].bitcast(F32), 0.0, ALU.is_ge, ALU.add,
                                        accum_out=CNT[:, t:t + 1])
                    e.drain()
                    e.tensor_scalar(MSK[:, :], CNT[:, :], float(KEEP), None, ALU.is_ge)
                    e.tensor_scalar(BIT[:, :], BIT[:, :], 1, None, ALU.logical_shift_right)
                    e.drain()
                    e.copy_predicated(THR[:, :], MSK[:, :], CND[:, :])
                    e.drain()
                for t in range(TPB):
                    th = THR[:, t:t + 1].bitcast(F32)
                    e.tensor_scalar(GT[:, :], E[:, t, :], th, 0.0, ALU.is_gt, ALU.add, accum_out=CNT[:, t:t + 1])
                    e.tensor_scalar(EQ[:, :], E[:, t, :], th, None, ALU.is_equal)
                    e.drain()
                    e.tensor_scalar(REM[:, t:t + 1], CNT[:, t:t + 1], -1.0, float(KEEP), ALU.mult, ALU.add)
                    e.tensor_tensor_scan(RK[:, :], EQ[:, :], EQ[:, :], 0.0, ALU.add, ALU.max)
                    e.drain()
                    e.scalar_tensor_tensor(EQ[:, :], RK[:, :], REM[:, t:t + 1], EQ[:, :], ALU.is_le, ALU.mult)
                    e.drain()
                    e.tensor_tensor(GT[:, :], GT[:, :], EQ[:, :], ALU.add)
                    e.drain()
                    if t >= 1:
                        e.wait_ge(S["wT_ps"], b * TPB + t)
                    e.scalar_tensor_tensor(W[:, :], E[:, t, :], 1.0, GT[:, :], ALU.mult, ALU.mult,
                                           accum_out=TOP[:, t:t + 1]).then_inc(S["w_ready"], 1)
                    e.drain()
                    e.scalar_tensor_tensor(DEN[:, t:t + 1], Z[:, t:t + 1], 1e-9, TOP[:, t:t + 1], ALU.mult, ALU.add)
                    e.drain()
                    e.reciprocal(RDN[:, t:t + 1], DEN[:, t:t + 1])
                    e.drain()
                    e.wait_ge(S["sp_ps"], b * TPB + t + 1)
                    e.tensor_scalar(SP_[:, t, :], OP[:, 0:P], RDN[:, t:t + 1], SG[:, 3:4], ALU.mult, ALU.mult)\
                        .then_inc(S["r1"], 1)
                e.drain()
                e.wait_ge(S["dense_ps"], b + 1)
                sp = SP_[:, :, :].rearrange("p t d -> p (t d)")
                e.scalar_tensor_tensor(sp, EXP[1][:, :], SG[:, 2:3], sp, ALU.mult, ALU.add)
                e.drain()
                e.tensor_tensor(SP_[:, :, :], SP_[:, :, :], XNa[:, :, :], ALU.add)
                e.drain()

                def affine(i):
                    e.drain()
                    e.tensor_tensor(R1[:, :, :], R1[:, :, :], GB[:, i, :].unsqueeze(1).to_broadcast([P, TPB, P]), ALU.mult)
                    e.drain()
                    return e.tensor_tensor(R1[:, :, :], R1[:, :, :], GB[:, i + 1, :].unsqueeze(1).to_broadcast([P, TPB, P]),
                                           ALU.add)

                layernorm(lambda t: SP_[:, t, :], lambda t: R1[:, t, :], 1, b)
                affine(0).then_inc(S["x1"], 1)
                e.wait_ge(S["ff_ps"], b + 1)
                for i in range(2):
                    x = e.tensor_tensor(SP_[:, 4 * i:4 * i + 4, :].rearrange("p t d -> p (t d)"),
                                        R1[:, 4 * i:4 * i + 4, :].rearrange("p t d -> p (t d)"), MXP[i][:, :], ALU.add)
                e.drain()
                layernorm(lambda t: SP_[:, t, :], lambda t: R1[:, t, :], 2, b)
                affine(2)
                e.drain()
                xb = X[:, bass.ds(b * TPB, TPB), :]
                e.tensor_tensor(xb, xb, R1[:, :, :], ALU.add).then_inc(S["xo"], 1)
                e.drain()
            e.drain().then_inc(S["xout"], 1)


def encoder_inputs(f):
    t = lambda n: np.ascontiguousarray(f(n).T)
    w = f('L0_attn_in_proj_w')
    b = f('L0_attn_in_proj_b')
    cols = np.zeros((P, 9), np.float32)
    cols[:, 0], cols[:, 1] = b[0:P], b[P:2 * P]
    cols[:RANK, 2], cols[:RANK, 3] = f('L0_attn_Qp_b'), f('L0_attn_Kp_b')
    cols[:, 4:8] = f('L0_attn_ff1_b').reshape(4, P).T
    rows = np.concatenate([b[2 * P:], f('L0_attn_Vp_b'), f('L0_attn_out_proj_b'), f('L0_attn_ff2_b'),
                           f('L0_attn_ln1_g'), f('L0_attn_ln1_b'), f('L0_attn_ln2_g'), f('L0_attn_ln2_b')])[None]
    for a in range(2):
        cols[64 * a + MROW:64 * a + MROW + 3, 8] = 1
    return dict(
        wqk=np.ascontiguousarray(w[:2 * P].reshape(2, P, P).transpose(2, 0, 1)), wqs=t('L0_attn_Qp_w'), wks=t('L0_attn_Kp_w'),
        wv2=np.ascontiguousarray(np.concatenate([w[2 * P:], f('L0_attn_Vp_w')], 0).T), wout=t('L0_attn_out_proj_w'),
        wf1=t('L0_attn_ff1_w'), wf2=np.ascontiguousarray(f('L0_attn_ff2_w').T.reshape(4, P, P).transpose(1, 0, 2)),
        rows=np.ascontiguousarray(rows), cols=cols, lam=np.ascontiguousarray(f('L0_attn_lam').reshape(1, 1)))


def stage_b(nc, X, wqkv, wo, w1, w2, b1, b2, lngb, scales, rope, mask, ident, shift, edge, onesrow, out):
    ctx = ExitStack()
    with ctx:
        def sb(name, shape, dt=F32):
            return ctx.enter_context(nc.sbuf_tensor("b_" + name, shape, dt))

        def pb(name, shape, dt=F32):
            return ctx.enter_context(nc.psum_tensor("b_" + name, shape, dt))

        def sem(name):
            return ctx.enter_context(nc.semaphore("b_" + name))

        H = sb("H", [P, TILES, P])
        IDN = sb("IDN", [P, P])
        SH = sb("SH", [P, P])
        ED = sb("ED", [P, P])
        ONR = sb("ONR", [P, P])
        IDB = sb("IDB", [P, P], BF16)
        MSK = sb("MSK", [P, TPB // 2, 512], BF16)
        Wqkv = sb("Wqkv", [P, 3 * INNER])
        Wo = sb("Wo", [P, PAIRS, P])
        W1 = sb("W1", [P, 2 * FF])
        W2 = sb("W2", [P, 3, P])
        BI = sb("BI", [P, 2 * FF + P])
        GB = sb("GB", [P, 2])
        SC = sb("SC", [P, 4, DH])
        RT = sb("RT", [P, 4, TPB, DH])
        RL = sb("RL", [P, 4, TPB, DH])
        HS = [sb(f"HS{i}", [P, P]) for i in range(2)]
        HM = [sb(f"HM{i}", [P, P]) for i in range(2)]
        xsT = [sb(f"xsT{i}", [P, WIN + P]) for i in range(2)]
        SQ = sb("SQ", [P, 2, INNER])
        SS = sb("SS", [P, 2, HEADS])
        RN = sb("RN", [P, 2, HEADS])
        NHALF = sb("NHALF", [P, HEADS])
        T1 = sb("T1", [P, 2, INNER])
        T2 = sb("T2", [P, 2, INNER])
        QH = sb("QH", [P, 2, INNER])
        qT = sb("qT", [P, PAIRS, P])
        kT = [sb(f"kT{i}", [P, PAIRS, WIN + P]) for i in range(2)]
        V2 = [sb(f"V2{i}", [P, NWIN, 512]) for i in range(2)]
        M = sb("M", [P, HEADS])
        PD = sb("PD", [P, PAIRS, 2, SPAN])
        PE_ = sb("PE_", [P, PAIRS, 2, SPAN])
        RS = sb("RS", [P, HEADS])
        RR = sb("RR", [P, HEADS])
        PTr = sb("PTr", [P, PAIRS, P])
        ON = sb("ON", [P, PAIRS, 2, DH])
        OT = sb("OT", [P, PAIRS, P])
        XJ = sb("XJ", [P, P])
        ST = sb("ST", [P, 6])
        MV = sb("MV", [P, 2])
        VE = sb("VE", [P, 1])
        RSTD = sb("RSTD", [P, 1])
        XN = sb("XN", [P, P])
        XNT = sb("XNT", [P, P])
        G = sb("G", [P, FF])
        HP = sb("HP", [P, FF])
        HPT = sb("HPT", [P, 3, P])
        ST0 = sb("ST0", [P, TILES, 6])
        MV0 = sb("MV0", [P, TILES, 2])
        VE0 = sb("VE0", [P, TILES])
        RS0 = sb("RS0", [P, TILES])
        NH0 = sb("NH0", [P, TILES])

        PA = pb("PA", [P, 1024])
        PB = pb("PB", [P, 1024])
        PV = [pb(f"PV{i}", [P, 512]) for i in range(2)]
        PT = [pb(f"PT{i}", [P, 512]) for i in range(2)]

        names = """loaded consts wload tab ln0_var ln0_rstd ln0_done
            hs_ready xsT_ps xsT_ready qk_ps v_ps v_ready sq_ready ss_ready rn_ready rope_ready
            tr_ps qkT_ready s_ps sub_ready p_ready sum_ready pt_ps pt_ready o_ps o_ready ot_ps ot_ready
            wo_ps hm_ready shift_ps var_ready rstd_ready xn_ready xnT_ps xnT_ready hg_ps gelu_ready
            hp_ready hpT_ps hpT_ready ff_ps h_ready out_ready stored pe_step pool_step zeroed idb_ready""".split()
        S = {n: sem(n) for n in names}
        NCONST = 8
        NW = 10

        def pe_front(e, T, s):
            o = 1 - s
            e.wait_ge(S["hs_ready"], T + 1)
            e.matmul(PT[1][0:64, 0:P], HS[s][:, 0:64], IDN[:, :], start=True, stop=True)
            e.matmul(PT[1][64:128, 0:P], HS[s][:, 64:128], SH[:, :], start=True, stop=False)
            e.matmul(PT[1][64:128, 0:P], HS[o][:, 64:128], ED[:, :], start=False, stop=True).then_inc(S["xsT_ps"], 1)
            e.wait_ge(S["xsT_ready"], T + 1)
            for i, ps in enumerate((PA, PB)):
                for j in range(2):
                    col = (2 * i + j) * 512
                    x = e.matmul(ps[:, 512 * j:512 * j + 512], xsT[s][:, WIN:], Wqkv[:, col:col + 512],
                                 start=True, stop=True)
                x.then_inc(S["qk_ps"], 1)
            e.wait_ge(S["h_ready"], T + 1)
            for w in range(NWIN):
                if w >= 2:
                    e.wait_ge(S["v_ready"], T * NWIN + w - 1)
                for a in range(2):
                    x = e.matmul(PV[w % 2][64 * a:64 * a + 64, :], xsT[s][:, WIN * w:WIN * w + SPAN],
                                 Wqkv[:, 2 * INNER + 512 * a:2 * INNER + 512 * a + 512], start=True, stop=True)
                x.then_inc(S["v_ps"], 1)
            for i in range(2):
                e.wait_ge(S["rope_ready"], 2 * T + i + 1)
                for hb in range(2):
                    n = 2 * i + hb
                    if n >= 2:
                        e.wait_ge(S["qkT_ready"], 4 * T + n - 1)
                    for j in range(4):
                        c = (4 * hb + j) * P
                        x = e.transpose(PT[hb][:, P * j:P * j + P], QH[:, i, c:c + P], IDN[:, :])
                    x.then_inc(S["tr_ps"], 1)

        def pe_attend(e, T, s, g):
            e.wait_ge(S["qkT_ready"], 4 * T + 4)
            e.sem_inc(S["pe_step"], 1)
            for a in range(2):
                mk = MSK[:, g, :] if s == 0 else MSK[:, 1, :]
                e.matmul(PA[:, 512 * a:512 * a + 512], IDB[:, :], mk, start=True, stop=False,
                         skip_group_check=True)
            for p in range(PAIRS):
                for w in range(NWIN):
                    for a in range(2):
                        x = e.matmul(PA[WIN * w:WIN * w + WIN, 512 * a + SPAN * p:512 * a + SPAN * p + SPAN],
                                     qT[64 * a:64 * a + 64, p, WIN * w:WIN * w + WIN],
                                     kT[s][64 * a:64 * a + 64, p, WIN * w:WIN * w + SPAN],
                                     start=False, stop=True, skip_group_check=True)
            x.then_inc(S["s_ps"], 1)
            e.wait_ge(S["p_ready"], T + 1)
            for hb in range(2):
                for j in range(4):
                    x = e.transpose(PT[hb][:, P * j:P * j + P],
                                    PE_[:, 4 * hb + j, :, :].rearrange("p a k -> p (a k)"), IDN[:, :])
                x.then_inc(S["pt_ps"], 1)
            e.wait_ge(S["v_ready"], T * NWIN + NWIN)
            for hb in range(2):
                e.wait_ge(S["pt_ready"], 2 * T + hb + 1)
                e.sem_inc(S["pe_step"], 1)
                for p in range(4 * hb, 4 * hb + 4):
                    for w in range(NWIN):
                        for a in range(2):
                            x = e.matmul(PB[WIN * w:WIN * w + WIN, 512 * a + DH * p:512 * a + DH * p + DH],
                                         PTr[64 * a:64 * a + 64, p, WIN * w:WIN * w + WIN],
                                         V2[s][64 * a:64 * a + 64, w, DH * p:DH * p + DH],
                                         start=True, stop=True)
            x.then_inc(S["o_ps"], 1)
            e.wait_ge(S["o_ready"], T + 1)
            for hb in range(2):
                for j in range(4):
                    x = e.transpose(PT[hb][:, P * j:P * j + P],
                                    ON[:, 4 * hb + j, :, :].rearrange("p a k -> p (a k)"), IDN[:, :])
                x.then_inc(S["ot_ps"], 1)
            for hb in range(2):
                e.wait_ge(S["ot_ready"], 2 * T + hb + 1)
                for j in range(4 * hb, 4 * hb + 4):
                    x = e.matmul(PV[0][:, 0:P], OT[:, j, :], Wo[:, j, :], start=(j == 0), stop=(j == 7))
            x.then_inc(S["wo_ps"], 1)

        def pe_ffn(e, T, s):
            o = 1 - s
            e.wait_ge(S["hm_ready"], T + 1)
            e.matmul(PV[1][:, 0:64], SH[:, :], HM[s][:, 64:128], start=True, stop=False)
            e.matmul(PV[1][:, 0:64], ED[:, :], HM[o][:, 64:128], start=False, stop=True).then_inc(S["shift_ps"], 1)
            e.wait_ge(S["xn_ready"], T + 1)
            e.transpose(PV[1][:, 0:P], XN[:, :], IDN[:, :]).then_inc(S["xnT_ps"], 1)
            e.wait_ge(S["xnT_ready"], T + 1)
            for i in range(2):
                ps = PA[:, 512 * i:512 * i + FF]
                e.matmul(ps, XNT[:, :], W1[:, FF * i:FF * i + FF], start=True, stop=False)
                x = e.matmul(ps, ONR[:, :], BI[:, FF * i:FF * i + FF], start=False, stop=True)
            x.then_inc(S["hg_ps"], 1)
            e.wait_ge(S["hp_ready"], T + 1)
            for j, (c, n) in enumerate(FFC):
                x = e.transpose(PT[0][0:n, P * j:P * j + P], HP[:, c:c + n], IDN[:, :])
            x.then_inc(S["hpT_ps"], 1)
            e.wait_ge(S["hpT_ready"], T + 1)
            for j in range(2):
                e.matmul(PV[1][:, 0:P], HPT[:, j, :], W2[:, j, :], start=(j == 0), stop=False)
            e.matmul(PV[1][:, 0:P], HPT[:, 2, :], W2[:, 2, :], start=False, stop=False)
            e.matmul(PV[1][:, 0:P], ONR[:, :], BI[:, 2 * FF:2 * FF + P], start=False, stop=True)\
                .then_inc(S["ff_ps"], 1)

        def act_front(e, T, s, tile):
            o = 1 - s
            e.activation(HS[s][:, :], H[:, tile, :].rearrange("p a d -> p (a d)"), ACT.Copy).then_inc(S["hs_ready"], 1)
            e.wait_ge(S["xsT_ps"], T + 1)
            e.activation(xsT[s][:, 0:WIN], xsT[o][:, P:P + WIN], ACT.Copy)
            e.activation(xsT[s][:, WIN:], PT[1][:, 0:P], ACT.Copy)
            e.drain().then_inc(S["xsT_ready"], 1)
            for i, ps in enumerate((PA, PB)):
                e.wait_ge(S["qk_ps"], 2 * T + i + 1)
                e.activation(SQ[:, i, :], ps[:, :], ACT.Square).then_inc(S["sq_ready"], 1)
            for w in range(NWIN):
                e.wait_ge(S["v_ps"], NWIN * T + w + 1)
                e.activation(V2[s][:, w, :], PV[w % 2][:, :], ACT.Copy).then_inc(S["v_ready"], 1)
            e.activation(kT[s][:, :, 0:WIN], kT[o][:, :, P:P + WIN], ACT.Copy)
            for i in range(2):
                for hb in range(2):
                    e.wait_ge(S["tr_ps"], 4 * T + 2 * i + hb + 1)
                    dst = qT[:, 4 * hb:4 * hb + 4, :] if i == 0 else kT[s][:, 4 * hb:4 * hb + 4, WIN:]
                    e.activation(dst, PT[hb][:, :].rearrange("p (j t) -> p j t", t=P), ACT.Copy)\
                        .then_inc(S["qkT_ready"], 1)

        def act_attend(e, T, s):
            e.wait_ge(S["sub_ready"], T + 1)
            e.activation(PE_[:, :, :, :], PD[:, :, :, :], ACT.Exp, scale=QK_SCALE).then_inc(S["p_ready"], 1)
            for hb in range(2):
                e.wait_ge(S["pt_ps"], 2 * T + hb + 1)
                e.activation(PTr[:, 4 * hb:4 * hb + 4, :], PT[hb][:, :].rearrange("p (j t) -> p j t", t=P),
                             ACT.Copy).then_inc(S["pt_ready"], 1)
            for hb in range(2):
                e.wait_ge(S["ot_ps"], 2 * T + hb + 1)
                e.activation(OT[:, 4 * hb:4 * hb + 4, :], PT[hb][:, :].rearrange("p (j t) -> p j t", t=P),
                             ACT.Copy).then_inc(S["ot_ready"], 1)

        def act_ffn(e, T, s):
            e.wait_ge(S["hg_ps"], T + 1)
            e.activation(G[:, :], PA[:, 512:512 + FF], ACT.Gelu).then_inc(S["gelu_ready"], 1)
            e.wait_ge(S["hpT_ps"], T + 1)
            n = FFC[2][1]
            e.activation(HPT[:, 0:2, :], PT[0][:, 0:2 * P].rearrange("p (j t) -> p j t", t=P), ACT.Copy)
            e.activation(HPT[0:n, 2, :], PT[0][0:n, 2 * P:3 * P], ACT.Copy)
            e.drain().then_inc(S["hpT_ready"], 1)

        def dve_front(e, T, s, tp):
            for i, ps in enumerate((PA, PB)):
                v = ps[:, :].rearrange("p (h d) -> p h d", d=DH)
                t1 = T1[:, i, :].rearrange("p (h d) -> p h d", d=DH)
                t2 = T2[:, i, :].rearrange("p (h d) -> p h d", d=DH)
                cs = RL[:, 2 * i, tp, :].to_broadcast([P, HEADS, DH])
                e.wait_ge(S["sq_ready"], 2 * T + i + 1)
                e.tensor_reduce(SS[:, i, :], SQ[:, i, :].rearrange("p (h d) -> p h d", d=DH), AX.X, ALU.add)\
                    .then_inc(S["ss_ready"], 1)
                e.tensor_tensor(t1, v, cs, ALU.mult)
                for hf in range(2):
                    sn = RL[:, 2 * i + 1, tp, WIN * hf:WIN * hf + WIN].to_broadcast([P, HEADS, WIN])
                    e.tensor_tensor(t2[:, :, WIN * hf:WIN * hf + WIN],
                                    v[:, :, WIN * (1 - hf):WIN * (1 - hf) + WIN], sn, ALU.mult)
                e.drain()
                e.tensor_tensor(T1[:, i, :], T1[:, i, :], T2[:, i, :], ALU.add)
                e.drain()
                e.wait_ge(S["rn_ready"], 2 * T + i + 1)
                e.tensor_tensor(QH[:, i, :].rearrange("p (h d) -> p h d", d=DH), t1,
                                RN[:, i, :].unsqueeze(2).to_broadcast([P, HEADS, DH]), ALU.mult)\
                    .then_inc(S["rope_ready"], 1)

        def dve_attend(e, T, s):
            v = PA[:, :].rearrange("p (a j k) -> p a j k", a=2, k=SPAN)
            e.wait_ge(S["s_ps"], T + 1)
            e.tensor_reduce(M[:, :], PA[:, :].rearrange("p (h k) -> p h k", k=SPAN), AX.X, ALU.max)
            e.drain()
            e.tensor_tensor(PD[:, :, :, :].rearrange("p j a k -> p a j k"), v,
                            M[:, :].rearrange("p (a j) -> p a j", a=2).unsqueeze(3).to_broadcast([P, 2, PAIRS, SPAN]),
                            ALU.subtract).then_inc(S["sub_ready"], 1)
            e.wait_ge(S["p_ready"], T + 1)
            e.tensor_reduce(RS[:, :], PE_[:, :, :, :].rearrange("p j a k -> p (j a) k"), AX.X, ALU.add)
            e.drain()
            e.reciprocal(RR[:, :], RS[:, :])
            e.drain()
            e.wait_ge(S["o_ps"], T + 1)
            e.tensor_tensor(ON[:, :, :, :].rearrange("p j a k -> p a j k"),
                            PB[:, :].rearrange("p (a j k) -> p a j k", a=2, k=DH),
                            RR[:, :].rearrange("p (j a) -> p a j", a=2).unsqueeze(3).to_broadcast([P, 2, PAIRS, DH]),
                            ALU.mult).then_inc(S["o_ready"], 1)
            e.wait_ge(S["wo_ps"], T + 1)
            e.tensor_tensor(HM[s][:, :], HS[s][:, :], PV[0][:, 0:P], ALU.add).then_inc(S["hm_ready"], 1)

        def dve_ffn(e, T, s, tile):
            e.wait_ge(S["shift_ps"], T + 1)
            e.tensor_copy(XJ[:, 0:64], HM[s][:, 0:64])
            e.tensor_copy(XJ[:, 64:128], PV[1][:, 0:64])
            e.drain()
            e.bn_stats(ST[:, :], XJ[:, :])
            e.drain()
            e.bn_aggr(MV[:, :], ST[:, :])
            e.drain()
            e.tensor_scalar(VE[:, :], MV[:, 1:2], EPS, None, ALU.add).then_inc(S["var_ready"], 1)
            e.wait_ge(S["rstd_ready"], T + 1)
            e.tensor_scalar(XN[:, :], XJ[:, :], MV[:, 0:1], RSTD[:, :], ALU.subtract, ALU.mult)\
                .then_inc(S["xn_ready"], 1)
            e.wait_ge(S["xnT_ps"], T + 1)
            e.tensor_scalar(XNT[:, :], PV[1][:, 0:P], GB[:, 0:1], GB[:, 1:2], ALU.mult, ALU.add)\
                .then_inc(S["xnT_ready"], 1)
            e.wait_ge(S["gelu_ready"], T + 1)
            e.tensor_tensor(HP[:, :], PA[:, 0:FF], G[:, :], ALU.mult).then_inc(S["hp_ready"], 1)
            e.wait_ge(S["ff_ps"], T + 1)
            e.tensor_tensor(H[:, tile, :].rearrange("p a d -> p (a d)"), HM[s][:, :], PV[1][:, 0:P], ALU.add)\
                .then_inc(S["h_ready"], 1)

        def pool_tile(e, T):
            for i in range(2):
                e.wait_ge(S["ss_ready"], 2 * T + i + 1)
                e.sem_inc(S["pool_step"], 1)
                e.tensor_scalar(SS[:, i, :], SS[:, i, :], 1e-24, None, ALU.max)
                e.drain()
                e.tensor_tensor(RN[:, i, :], SS[:, i, :], NHALF[:, :], ALU.pow).then_inc(S["rn_ready"], 1)
            e.wait_ge(S["var_ready"], T + 1)
            e.tensor_tensor(RSTD[:, :], VE[:, :], NHALF[:, 0:1], ALU.pow).then_inc(S["rstd_ready"], 1)

        LOADS = [(X, "x")]
        block = ctx.enter_context(nc.Block())

        @block.sync
        def _(e):
            for dst, s_ in ((IDN[:, :], ident), (SH[:, :], shift), (ED[:, :], edge), (ONR[:, :], onesrow),
                            (T1[:, :, :].rearrange("p i (v x) -> p (i v) x", v=2), mask), (RT[:, :, :, :], rope)):
                e.dma_start(dst, s_).then_inc(S["consts"], 16)
            with e.Fori(0, DEPTH) as L:
                e.wait_ge(S["h_ready"], L * TILES + 1)
                e.wait_ge(S["zeroed"], 1)
                ly = lambda t: t[bass.ds(L, 1)].squeeze(0)
                for dst, s_ in ((Wqkv[:, :], ly(wqkv)),
                                (Wo[:, :, :], ly(wo).rearrange("(j p) n -> p j n", p=P)),
                                (W1[:, :], ly(w1)),
                                (W2[:, 0:2, :], ly(w2)[0:2 * P, :].rearrange("(j p) n -> p j n", p=P)),
                                (W2[0:FF - 2 * P, 2, :], ly(w2)[2 * P:FF, :]),
                                (BI[0:1, 0:2 * FF], b1[bass.ds(L, 1), :]),
                                (BI[0:1, 2 * FF:], b2[bass.ds(L, 1), :]),
                                (GB[:, :], ly(lngb)),
                                (SC[:, :, :].rearrange("p a d -> p (a d)"), scales[bass.ds(L, 1), :].to_broadcast([P, 4 * DH]))):
                    e.dma_start(dst, s_).then_inc(S["wload"], 16)
            e.wait_ge(S["out_ready"], 1)
            e.dma_start(out.rearrange("b (t p) d -> p (b t) d", p=P), X[:, :, :]).then_inc(S["stored"], 16)
            e.wait_ge(S["stored"], 16)

        @block.gpsimd
        def _(e):
            e.memset(NHALF[:, :], -0.5)
            e.memset(NH0[:, :], -0.5)
            e.memset(BI[:, :], 0.0)
            e.memset(W2[:, :, :], 0.0)
            e.memset(HPT[:, :, :], 0.0)
            for t in (*kT, *xsT, *HS, *HM):
                e.memset(t[:], 0.0)
            e.drain().then_inc(S["zeroed"], 1)
            e.wait_ge(S["ln0_var"], 1)
            e.tensor_tensor(RS0[:, :], VE0[:, :], NH0[:, :], ALU.pow).then_inc(S["ln0_rstd"], 1)
            with e.Fori(0, DEPTH) as L:
                with e.Fori(0, BATCH) as b:
                    with e.Fori(0, TPB // 2) as g:
                        for s in range(2):
                            pool_tile(e, ((L * BATCH + b) * (TPB // 2) + g) * 2 + s)

        @block.scalar
        def _(e):
            e.wait_ge(S["ln0_done"], 1)
            with e.Fori(0, DEPTH) as L:
                with e.Fori(0, BATCH) as b:
                    e.wait_ge(S["h_ready"], (L * BATCH + b) * TPB + 1)
                    e.memzero(HS[1][:, :])
                    e.memzero(kT[1][:, :, P:])
                    e.drain()
                    with e.Fori(0, TPB // 2) as g:
                        for s in range(2):
                            T = ((L * BATCH + b) * (TPB // 2) + g) * 2 + s
                            e.wait_ge(S["h_ready"], T + 1)
                            act_front(e, T, s, bass.ds(b * TPB + g * 2 + s, 1))
                            act_attend(e, T, s)
                            act_ffn(e, T, s)
                            e.drain()

        @block.vector
        def _(e):
            e.wait_ge(S["zeroed"], 1)
            for t in range(TILES):
                e.bn_stats(ST0[:, t, :], X[:, t, :])
            e.drain()
            for t in range(TILES):
                e.bn_aggr(MV0[:, t, :], ST0[:, t, :])
            e.drain()
            e.tensor_scalar(VE0[:, :], MV0[:, :, 1], EPS, None, ALU.add).then_inc(S["ln0_var"], 1)
            e.wait_ge(S["ln0_rstd"], 1)
            for t in range(TILES):
                e.tensor_scalar(H[:, t, :], X[:, t, :], MV0[:, t, 0:1], RS0[:, t:t + 1], ALU.subtract, ALU.mult)
            e.drain().then_inc(S["ln0_done"], 1)
            e.wait_ge(S["consts"], 16 * 6)
            e.tensor_copy(MSK[:, :, :], T1[:, :, :].rearrange("p i (v x) -> p (i v) x", v=2))
            e.tensor_copy(IDB[:, :], IDN[:, :])
            e.drain().then_inc(S["h_ready"], 1)
            with e.Fori(0, DEPTH) as L:
                e.wait_ge(S["wload"], (L + 1) * (16 * 9))
                for i in range(4):
                    e.tensor_tensor(RL[:, i, :, :], RT[:, i, :, :],
                                    SC[:, i, :].unsqueeze(1).to_broadcast([P, TPB, DH]), ALU.mult)
                e.drain()
                with e.Fori(0, BATCH) as b:
                    e.memset(HM[1][:, :], 0.0)
                    e.drain()
                    with e.Fori(0, TPB // 2) as g:
                        for s in range(2):
                            T = ((L * BATCH + b) * (TPB // 2) + g) * 2 + s
                            dve_front(e, T, s, bass.ds(g * 2 + s, 1))
                            dve_attend(e, T, s)
                            dve_ffn(e, T, s, bass.ds(b * TPB + g * 2 + s, 1))
                            e.drain()
            e.tensor_tensor(X[:, :, :], X[:, :, :], H[:, :, :], ALU.add).then_inc(S["out_ready"], 1)

        @block.tensor
        def _(e):
            e.wait_ge(S["consts"], 16 * 6)
            e.wait_ge(S["h_ready"], 1)
            with e.Fori(0, DEPTH) as L:
                e.wait_ge(S["wload"], (L + 1) * (16 * 9))
                e.sem_inc(S["pe_step"], 1)
                with e.Fori(0, BATCH) as b:
                    with e.Fori(0, TPB // 2) as g:
                        for s in range(2):
                            T = ((L * BATCH + b) * (TPB // 2) + g) * 2 + s
                            pe_front(e, T, s)
                            pe_attend(e, T, s, bass.ds(g, 1))
                            pe_ffn(e, T, s)


def rope_tables():
    half = np.arange(0, DH, 2, dtype=np.float32)
    inv_freq = (np.float32(1.0) / np.float32(10000.0) ** (half / np.float32(DH))).astype(np.float32)
    t = np.arange(SEQ, dtype=np.float32)
    fr = t[:, None] * inv_freq[None, :]
    fr = np.concatenate([fr, fr], -1).astype(np.float32)
    base = ((half + np.float32(0.4 * DH)) / np.float32(1.4 * DH)).astype(np.float32)
    power = ((t - SEQ // 2) / np.float32(WIN // 2)).astype(np.float32)
    scale = (base[None, :] ** power[:, None]).astype(np.float32)
    scale = np.concatenate([scale, scale], -1)
    sign = np.where(np.arange(DH) < DH // 2, -1.0, 1.0).astype(np.float32)
    cos, sin = np.cos(fr), np.sin(fr) * sign
    tabs = np.stack([cos * scale, sin * scale, cos / scale, sin / scale]).astype(np.float32)
    return np.ascontiguousarray(tabs.reshape(4, TPB, P, DH).transpose(2, 0, 1, 3))


def masks():
    i = np.arange(P)[:, None] % WIN
    j = np.arange(SPAN)[None, :]
    seen = (i <= j) & (j <= i + WIN)
    first = seen & ~((np.arange(P)[:, None] < WIN) & (j < WIN))
    tab = np.stack([first] + [seen] * (TPB // 2 - 1), 1)
    tab = np.where(tab, 0.0, -1e30)
    return np.tile(tab, (1, 1, 8)).astype(np.float32)


def build(nc, enc, stk, scratch, out):
    with nc.sbuf_tensor("X", [P, TILES, P], F32) as X:
        stage_a(nc, X, scratch=scratch, **enc)
        stage_b(nc, X, out=out, **stk)


def stack_inputs(f):
    rot = np.r_[DH // 2:DH, 0:DH // 2]
    heads = [np.arange(a, HEADS, 2) for a in range(2)]
    vcols = [(2 * INNER + h[:, None] * DH + np.arange(DH)).ravel() for h in heads]
    order = np.concatenate([np.arange(2 * INNER)] + vcols)
    qs, ks = f('L0_ffn_q_scale'), f('L0_ffn_k_scale')
    edge = np.zeros((P, P), np.float32)
    edge[P - 1, 0] = 1
    return dict(
        wqkv=np.ascontiguousarray(f('L0_ffn_Wqkv')[:, :, order]), wo=f('L0_ffn_Wo'), w1=f('L0_ffn_W1'),
        w2=f('L0_ffn_W2'), b1=f('L0_ffn_b1'), b2=f('L0_ffn_b2'),
        lngb=np.ascontiguousarray(np.stack([f('L0_ffn_ln_g'), f('L0_ffn_ln_b')], -1)),
        scales=np.ascontiguousarray(np.concatenate([qs, qs[:, rot], ks, ks[:, rot]], -1)),
        rope=rope_tables(), mask=masks(), shift=np.eye(P, k=1, dtype=np.float32), edge=edge)


def kernel(**inputs):
    import concourse.bacc as bacc
    from concourse.bass_utils import run_bass_kernel_spmd as run
    f = lambda n: np.ascontiguousarray(inputs[n])
    onesrow = np.zeros((P, P), np.float32)
    onesrow[0] = 1
    both = dict(ident=np.eye(P, dtype=np.float32), onesrow=onesrow)
    enc = dict(src=f('L0_attn_src'), **encoder_inputs(f))
    stk = stack_inputs(f)
    nc = bacc.Bacc("TRN2", target_bir_lowering=False, num_devices=1)
    arrays = {**both, **enc, **stk}
    dram = {n: nc.dram_tensor(n + "_dram", a.shape, mybir.dt.from_np(a.dtype), kind="ExternalInput").ap()
            for n, a in arrays.items()}
    out = nc.dram_tensor("out_dram", (BATCH, SEQ, P), F32, kind="ExternalOutput").ap()
    scratch = nc.dram_tensor("parts_dram", (2, 3, P, SEQ), BF16, kind="Internal").ap()
    build(nc, {n: dram[n] for n in (*both, *enc)}, {n: dram[n] for n in (*both, *stk)}, scratch, out)
    r = run(nc, [{n + "_dram": a for n, a in arrays.items()}], core_ids=[0])
    return r.results[0]["out_dram"]
```

```python
import concourse.bass as bass
from concourse import mybir
from contextlib import ExitStack
import numpy as np

F32 = mybir.dt.float32
BF16 = mybir.dt.bfloat16
I32 = mybir.dt.int32
ACT = mybir.ActivationFunctionType
ALU = mybir.AluOpType
AX = mybir.AxisListType

P = 128
BATCH, SEQ = 4, 1024
TPB = SEQ // P
TILES = BATCH * TPB
EPS = 1e-5
AH, AD = 16, 8
AP_ = AH // 2
RANK = 64
KEEP = int(SEQ * 0.2)
AFF = 512
PARTS_Q = (0, 0, 1, 0, 2, 1)
PARTS_K = (0, 1, 0, 2, 0, 1)
MROW = 48


DEPTH, HEADS, DH = 6, 16, 64
PAIRS = HEADS // 2
INNER = HEADS * DH
WIN = 32
NWIN = P // WIN
SPAN = 2 * WIN
FF = 341
FFC = [(0, 128), (128, 128), (256, FF - 256)]
QK_SCALE = 8.0


def stage_a(nc, X, src, scratch, wqk, wqs, wks, wv2, wout, wf1, wf2, rows, cols, ident, onesrow, lam):
    ctx = ExitStack()
    with ctx:
        def sb(name, shape, dt=F32):
            return ctx.enter_context(nc.sbuf_tensor("a_" + name, shape, dt))

        def pb(name, shape, dt=F32):
            return ctx.enter_context(nc.psum_tensor("a_" + name, shape, dt))

        def sem(name):
            return ctx.enter_context(nc.semaphore("a_" + name))

        IDN = sb("IDN", [P, P])
        IDB = sb("IDB", [P, P], BF16)
        ONR = sb("ONR", [P, P])
        WQK = sb("WQK", [P, 2, P])
        WQS = sb("WQS", [P, RANK])
        WKS = sb("WKS", [P, RANK])
        WV2 = sb("WV2", [P, 2 * P])
        WOUT = sb("WOUT", [P, P])
        WF1 = sb("WF1", [P, AFF])
        WF2 = sb("WF2", [P, 4, P])
        ROWS = sb("ROWS", [P, 4 * P])
        GB = sb("GB", [P, 4, P])
        COLS = sb("COLS", [P, 9])
        LAM = sb("LAM", [P, 1])
        SG = sb("SG", [P, 4])
        ST = sb("ST", [P, TPB, 6])
        MV = sb("MV", [P, TPB, 2])
        VE = sb("VE", [P, TPB])
        RS = sb("RS", [P, TPB])
        NHf = sb("NHf", [P, TPB])
        XNa = sb("XNa", [P, TPB, P])
        XT = sb("XT", [P, SEQ])
        Q32 = sb("Q32", [P, SEQ])
        QR = sb("QR", [P, SEQ])
        QP3 = sb("QP3", [P, 2, 3, SEQ], BF16)
        QPK = [sb(f"QPK{i}", [P, SEQ], BF16) for i in range(2)]
        KPK = [sb(f"KPK{i}", [P, SEQ], BF16) for i in range(2)]
        QM = [sb(f"QM{i}", [P, SEQ], BF16) for i in range(2)]
        V8 = sb("V8", [P, TPB, AH, AD])
        V9 = [sb(f"V9{i}", [P, TPB, 2, 32]) for i in range(2)]
        SQ = sb("SQ", [RANK, SEQ])
        SK = sb("SK", [RANK, SEQ])
        SV = sb("SV", [P, TPB, P])
        E = sb("E", [P, TPB, SEQ])
        Z = sb("Z", [P, TPB])
        SM = sb("SM", [P, TPB])
        SMS = sb("SMS", [P, TPB])
        J = sb("J", [P, TPB, SEQ], BF16)
        THR = sb("THR", [P, TPB], I32)
        CND = sb("CND", [P, TPB], I32)
        BIT = sb("BIT", [P, TPB], I32)
        CNT = sb("CNT", [P, TPB])
        MSK = sb("MSK", [P, TPB], I32)
        REM = sb("REM", [P, TPB])
        TOP = sb("TOP", [P, TPB])
        DEN = sb("DEN", [P, TPB])
        RDN = sb("RDN", [P, TPB])
        EQ = sb("EQ", [P, SEQ])
        RK = sb("RK", [P, SEQ])
        GT = sb("GT", [P, SEQ])
        W = sb("W", [P, SEQ])
        WT = sb("WT", [P, TPB, P])
        MX = sb("MX", [P, 2, TPB, 2])
        NM = sb("NM", [P, 2, TPB])
        NR = sb("NR", [P, 2, TPB])
        MT = sb("MT", [P, TPB, P], BF16)
        PX = [sb(f"PX{i}", [P, SEQ]) for i in range(2)]
        OE = sb("OE", [P, 512])
        RC = sb("RC", [P, 2, 2, 4])
        CX = sb("CX", [P, TPB, P])
        CT = sb("CT", [P, TPB, P])
        SP_ = sb("SP", [P, TPB, P])
        R1 = sb("R1", [P, TPB, P])
        X1T = sb("X1T", [P, SEQ])
        HT = sb("HT", [P, 4, SEQ])

        MXP = [pb(f"MXP{i}", [P, 512]) for i in range(2)]
        EXP = [pb(f"EXP{i}", [P, 1024]) for i in range(2)]
        OP = pb("OP", [P, 512])
        MI = pb("MI", [P, 512])
        MIB = MI[:, :].bitcast(BF16)

        names = """loaded zeroed var rstd xn xT_ps xT_ready q_ps split parts_stored pack0 pack1 s_ps s_ready v_ps v_ready
            ss_ps ssm_ready e_ready v9 mx_ps mx_red nm mt_ps qm st_ps exp pv_ps oe ot_ps ctx cT_ps cT_ready
            dense_ps w_ready wT_ps wT_ready sp_ps r1 x1 x1T_ps x1T_ready h_ps h_ready ff_ps ff_ready r2 xo lam_e
            sig pe_step sp_step thr xout""".split()
        S = {n: sem(n) for n in names}
        NL = 14

        def at(N, n, k):
            return N * n + k

        block = ctx.enter_context(nc.Block())

        @block.sync
        def _(e):
            e.dma_start(X[:, :, :], src.rearrange("b (t p) d -> p (b t) d", p=P)).then_inc(S["loaded"], 16)
            e.wait_ge(S["zeroed"], 1)
            for dst, s_ in ((IDN[:, :], ident), (ONR[:, :], onesrow), (WQK[:, :, :], wqk), (WQS[:, :], wqs),
                            (WKS[:, :], wks), (WV2[:, :], wv2), (WOUT[:, :], wout), (WF1[:, :], wf1),
                            (WF2[:, :, :], wf2), (ROWS[0:1, :], rows[0:1, 0:4 * P]),
                            (GB[:, :, :].rearrange("p a d -> p (a d)"), rows[0:1, 4 * P:8 * P].to_broadcast([P, 4 * P])),
                            (COLS[:, :], cols), (LAM[:, :], lam.to_broadcast([P, 1]))):
                e.dma_start(dst, s_).then_inc(S["loaded"], 16)
            e.wait_ge(S["sig"], 1)
            e.sem_inc(S["sp_step"], 1)
            with e.Fori(0, BATCH) as b:
                for i in range(2):
                    e.wait_ge(S["split"], b * 2 + i + 1)
                    for k in range(3):
                        e.dma_start(scratch[i, k], QP3[:, i, k, :]).then_inc(S["parts_stored"], 16)
                e.wait_ge(S["parts_stored"], (b + 1) * (16 * 6))
                e.sem_inc(S["sp_step"], 1)
                with e.Fori(0, AP_ // 2) as gp:
                    for s in range(2):
                        e.wait_ge(S["ctx"], b * AP_ + gp * 2 + s + 1)
                        p = gp * 2 + s
                        for i, (dst, parts) in enumerate(((QPK[s], PARTS_Q), (KPK[s], PARTS_K))):
                            for a in range(2):
                                for g, k in enumerate(parts):
                                    e.dma_start(dst[64 * a + 8 * g:64 * a + 8 * g + 8, :],
                                                scratch[i, k, bass.ds(p * 16 + 8 * a, 8), :]).then_inc(S["pack%d" % s], 16)
            e.wait_ge(S["xout"], 1)

        NPACK = 16 * 24

        @block.gpsimd
        def _(e):
            e.memset(NHf[:, :], -0.5)
            e.memset(ROWS[:, :], 0.0)
            e.memset(MT[:, :, :], 0.0)
            for s in range(2):
                e.memset(QPK[s][:, :], 0.0)
                e.memset(KPK[s][:, :], 0.0)
                e.memset(V9[s][:, :, :, :], 0.0)
            e.drain()
            for s in range(2):
                e.memset(V9[s][:, :, :, AD:AD + 1], 1.0)
            e.drain().then_inc(S["zeroed"], 1)
            with e.Fori(0, BATCH) as b:
                for k in range(3):
                    e.wait_ge(S["var"], b * 3 + k + 1)
                    e.tensor_tensor(RS[:, :], VE[:, :], NHf[:, :], ALU.pow).then_inc(S["rstd"], 1)

        @block.tensor
        def _(e):
            LD = NL * 16

            def max_unit(N, s, u):
                qt, a = u // 2, u % 2
                for h in range(2):
                    if u >= 1:
                        e.wait_ge(S["mx_red"], N * 32 + (2 * u + h - 1))
                        e.sem_inc(S["pe_step"], 1)
                    e.matmul(MXP[h][:, :], QPK[s][64 * a:64 * a + 64, P * qt:P * qt + P],
                             KPK[s][64 * a:64 * a + 64, 512 * h:512 * h + 512], start=True, stop=True)\
                        .then_inc(S["mx_ps"], 1)

            def m_transposes(N, s):
                e.wait_ge(S["nm"], N + 1)
                e.wait_ge(S["ctx"], N + 1)
                for t in range(TPB):
                    x = e.transpose(MIB[:, P * t:P * t + P], MT[:, t, :], IDB[:, :])
                x.then_inc(S["mt_ps"], 1)

            def pv(N, s, u):
                c, kp, a = u // 8, (u // 2) % 4, u % 2
                q = 2 * a + c
                e.wait_ge(S["exp"], N * 16 + (u + 1))
                for j in range(2):
                    x = e.matmul(OP[32 * q:32 * q + 32, :], V9[s][:, 2 * kp + j, a, :],
                                 PX[a][:, 512 * j:512 * j + 512], start=(kp == 0 and j == 0),
                                 stop=(kp == 3 and j == 1))
                x.then_inc(S["pv_ps"], 1)

            def pair(N, h, s, nxt):
                e.wait_ge(S["qm"], N + 2)
                e.sem_inc(S["pe_step"], 1)
                if nxt:
                    e.wait_ge(S["pack%d" % (1 - s)], (h + 1 + s) * NPACK)
                    e.sem_inc(S["pe_step"], 1)
                e.wait_ge(S["v9"], N + 1)
                e.sem_inc(S["pe_step"], 1)
                for u in range(17):
                    if u < 16:
                        c, kp, a = u // 8, (u // 2) % 4, u % 2
                        if u >= 2:
                            e.wait_ge(S["exp"], N * 16 + (u - 1))
                            e.sem_inc(S["pe_step"], 1)
                        for j in range(2):
                            x = e.matmul(EXP[a][:, 512 * j:512 * j + 512],
                                         KPK[s][64 * a:64 * a + 64, P * (2 * kp + j):P * (2 * kp + j) + P],
                                         QM[s][64 * a:64 * a + 64, 512 * c:512 * c + 512], start=True, stop=True)
                        x.then_inc(S["st_ps"], 1)
                        if nxt:
                            max_unit(N + 1, 1 - s, u)
                    if u >= 1:
                        pv(N, s, u - 1)
                if nxt:
                    m_transposes(N + 1, 1 - s)
                    e.wait_ge(S["qm"], N + 3)
                else:
                    e.wait_ge(S["ctx"], N + 2)
                e.wait_ge(S["oe"], N + 1)
                for t in range(4):
                    x = e.transpose(MI[:, P * t:P * t + P], OE[:, P * t:P * t + P], IDN[:, :])
                x.then_inc(S["ot_ps"], 1)

            e.wait_ge(S["loaded"], LD)
            e.wait_ge(S["sig"], 1)
            with e.Fori(0, BATCH) as b:
                e.wait_ge(S["xn"], b + 1)
                for t in range(TPB):
                    x = e.transpose(EXP[0][:, P * t:P * t + P], XNa[:, t, :], IDN[:, :])
                x.then_inc(S["xT_ps"], 1)
                e.wait_ge(S["xT_ready"], b + 1)
                for i in range(2):
                    for c in range(2):
                        x = e.matmul(EXP[i][:, 512 * c:512 * c + 512], WQK[:, i, :], XT[:, 512 * c:512 * c + 512],
                                     start=True, stop=True)
                    x.then_inc(S["q_ps"], 1)
                for i, w in enumerate((WQS, WKS)):
                    for c in range(2):
                        if i == 1:
                            e.wait_ge(S["s_ready"], b * 4 + c + 1)
                        e.matmul(MXP[c][0:RANK, :], w[:, :], XT[:, 512 * c:512 * c + 512],
                                 start=True, stop=True).then_inc(S["s_ps"], 1)
                for t in range(TPB):
                    if t % 4 == 0:
                        e.wait_ge(S["split"], b * 2 + t // 4 + 1)
                    o = EXP[t // 4][:, 256 * (t % 4):256 * (t % 4) + 256]
                    e.matmul(o, XT[:, P * t:P * t + P], WV2[:, :], start=True, stop=False)
                    x = e.matmul(o, ONR[:, :], ROWS[:, 0:256], start=False, stop=True)
                    if t % 4 == 3:
                        x.then_inc(S["v_ps"], 1)
                e.wait_ge(S["s_ready"], b * 4 + 4)
                for t in range(TPB):
                    if t < 2:
                        e.wait_ge(S["v_ready"], b * 2 + t + 1)
                    else:
                        e.wait_ge(S["e_ready"], b * TPB + t - 1)
                    e.sem_inc(S["pe_step"], 1)
                    for c in range(2):
                        x = e.matmul(EXP[t % 2][:, 512 * c:512 * c + 512], SQ[:, P * t:P * t + P],
                                     SK[:, 512 * c:512 * c + 512], start=True, stop=True)
                    x.then_inc(S["ss_ps"], 1)
                e.wait_ge(S["pack0"], b * (AP_ // 2 * NPACK) + NPACK)
                e.sem_inc(S["pe_step"], 1)
                e.wait_ge(S["e_ready"], b * TPB + TPB)
                e.sem_inc(S["pe_step"], 1)
                for u in range(16):
                    max_unit(b * AP_, 0, u)
                m_transposes(b * AP_, 0)
                with e.Fori(0, AP_ // 2 - 1) as gp:
                    for s in range(2):
                        pair(b * AP_ + gp * 2 + s, b * (AP_ // 2) + gp, s, True)
                pair(b * AP_ + (AP_ - 2), b * (AP_ // 2) + (AP_ // 2 - 1), 0, True)
                pair(b * AP_ + (AP_ - 1), b * (AP_ // 2) + (AP_ // 2 - 1), 1, False)
                e.wait_ge(S["ctx"], (b + 1) * AP_ + 2)
                for t in range(TPB):
                    x = e.transpose(EXP[0][:, P * t:P * t + P], CX[:, t, :], IDN[:, :])
                x.then_inc(S["cT_ps"], 1)
                e.wait_ge(S["cT_ready"], b + 1)
                for t in range(TPB):
                    o = EXP[1][:, P * t:P * t + P]
                    e.matmul(o, CT[:, t, :], WOUT[:, :], start=True, stop=False)
                    x = e.matmul(o, ONR[:, :], ROWS[:, 2 * P:3 * P], start=False, stop=True)
                x.then_inc(S["dense_ps"], 1)
                for t in range(TPB):
                    e.wait_ge(S["w_ready"], b * TPB + t + 1)
                    for k in range(TPB):
                        x = e.transpose(EXP[0][:, P * k:P * k + P], W[:, P * k:P * k + P], IDN[:, :])
                    x.then_inc(S["wT_ps"], 1)
                    e.wait_ge(S["wT_ready"], b * TPB + t + 1)
                    if t >= 1:
                        e.wait_ge(S["r1"], b * TPB + t)
                    for k in range(TPB):
                        x = e.matmul(OP[:, 0:P], WT[:, k, :], SV[:, k, :], start=(k == 0), stop=(k == TPB - 1))
                    x.then_inc(S["sp_ps"], 1)
                e.wait_ge(S["x1"], b + 1)
                for t in range(TPB):
                    x = e.transpose(EXP[0][:, P * t:P * t + P], R1[:, t, :], IDN[:, :])
                x.then_inc(S["x1T_ps"], 1)
                e.wait_ge(S["x1T_ready"], b + 1)
                for j in range(4):
                    if j >= 2:
                        e.wait_ge(S["h_ready"], b * 4 + j - 1)
                    for c in range(2):
                        x = e.matmul(EXP[j % 2][:, 512 * c:512 * c + 512], WF1[:, P * j:P * j + P],
                                     X1T[:, 512 * c:512 * c + 512], start=True, stop=True)
                    x.then_inc(S["h_ps"], 1)
                e.wait_ge(S["h_ready"], b * 4 + 4)
                for t in range(TPB):
                    o = EXP[1][:, P * t:P * t + P] if 0 else (MXP[t // 4][:, P * (t % 4):P * (t % 4) + P])
                    for j in range(4):
                        e.matmul(o, HT[:, j, P * t:P * t + P], WF2[:, j, :], start=(j == 0), stop=False)
                    x = e.matmul(o, ONR[:, :], ROWS[:, 3 * P:4 * P], start=False, stop=True)
                x.then_inc(S["ff_ps"], 1)

        @block.scalar
        def _(e):
            e.wait_ge(S["loaded"], NL * 16)
            e.activation(SG[:, 0:1], LAM[:, :], ACT.Exp, scale=-1.0).then_inc(S["lam_e"], 1)

            def v9_copy(N, s, p):
                e.activation(V9[s][:, :, :, 0:AD], V8[:, :, bass.ds(p * 2, 2), :], ACT.Copy).then_inc(S["v9"], 1)

            def exps(N):
                for u in range(16):
                    a = u % 2
                    e.wait_ge(S["st_ps"], N * 16 + (u + 1))
                    e.activation(PX[a][:, :], EXP[a][:, :], ACT.Exp, scale=AD ** -0.5).then_inc(S["exp"], 1)

            with e.Fori(0, BATCH) as b:
                e.wait_ge(S["xT_ps"], b + 1)
                e.activation(XT[:, :], EXP[0][:, :], ACT.Copy).then_inc(S["xT_ready"], 1)
                for i, dst in enumerate((SQ, SK)):
                    for c in range(2):
                        e.wait_ge(S["s_ps"], b * 4 + 2 * i + c + 1)
                        e.activation(dst[:, 512 * c:512 * c + 512], MXP[c][0:RANK, :], ACT.Identity,
                                     bias=COLS[0:RANK, 2 + i:3 + i]).then_inc(S["s_ready"], 1)
                for i in range(2):
                    e.wait_ge(S["v_ps"], b * 2 + i + 1)
                    v = EXP[i][:, :].rearrange("p (t x) -> p t x", t=4)
                    e.activation(V8[:, 4 * i:4 * i + 4, :, :].rearrange("p t h d -> p t (h d)"), v[:, :, 0:P], ACT.Copy)
                    e.activation(SV[:, 4 * i:4 * i + 4, :], v[:, :, P:2 * P], ACT.Copy)
                    e.drain().then_inc(S["v_ready"], 1)
                for t in range(TPB):
                    e.wait_ge(S["ssm_ready"], b * TPB + t + 1)
                    e.activation(E[:, t, :], EXP[t % 2][:, :], ACT.Exp, bias=SMS[:, t:t + 1], scale=RANK ** -0.5,
                                 accum_out=Z[:, t:t + 1]).then_inc(S["e_ready"], 1)
                with e.Fori(0, AP_ // 2) as gp:
                    for s in range(2):
                        N = b * AP_ + gp * 2 + s
                        v9_copy(N, s, gp * 2 + s)
                        exps(N)
                e.wait_ge(S["cT_ps"], b + 1)
                e.activation(CT[:, :, :].rearrange("p t d -> p (t d)"), EXP[0][:, :], ACT.Copy).then_inc(S["cT_ready"], 1)
                for t in range(TPB):
                    e.wait_ge(S["wT_ps"], b * TPB + t + 1)
                    e.activation(WT[:, :, :].rearrange("p t d -> p (t d)"), EXP[0][:, :], ACT.Copy)\
                        .then_inc(S["wT_ready"], 1)
                e.wait_ge(S["x1T_ps"], b + 1)
                e.activation(X1T[:, :], EXP[0][:, :], ACT.Copy).then_inc(S["x1T_ready"], 1)
                for j in range(4):
                    e.wait_ge(S["h_ps"], b * 4 + j + 1)
                    e.activation(HT[:, j, :], EXP[j % 2][:, :], ACT.Relu, bias=COLS[:, 4 + j:5 + j])\
                        .then_inc(S["h_ready"], 1)

        @block.vector
        def _(e):
            e.wait_ge(S["loaded"], NL * 16)
            e.wait_ge(S["lam_e"], 1)
            e.tensor_scalar(SG[:, 1:2], SG[:, 0:1], 1.0, None, ALU.add)
            e.drain()
            e.reciprocal(SG[:, 2:3], SG[:, 1:2])
            e.drain()
            e.tensor_scalar(SG[:, 3:4], SG[:, 2:3], -1.0, 1.0, ALU.mult, ALU.add)
            e.tensor_copy(IDB[:, :], IDN[:, :])
            for s in range(2):
                e.tensor_scalar(KPK[s][:, :], KPK[s][:, :], COLS[:, 8:9], None, ALU.add)
            e.drain().then_inc(S["sig"], 1)
            e.sem_inc(S["ctx"], 2)
            e.sem_inc(S["qm"], 1)

            def layernorm(get, put, nth, b):
                for t in range(TPB):
                    e.bn_stats(ST[:, t, :], get(t))
                e.drain()
                for t in range(TPB):
                    e.bn_aggr(MV[:, t, :], ST[:, t, :])
                e.drain()
                e.tensor_scalar(VE[:, :], MV[:, :, 1], EPS, None, ALU.add).then_inc(S["var"], 1)
                e.wait_ge(S["rstd"], b * 3 + nth + 1)
                for t in range(TPB):
                    x = e.tensor_scalar(put(t), get(t), MV[:, t, 0:1], RS[:, t:t + 1], ALU.subtract, ALU.mult)
                return x

            def maxima(N, s):
                for u in range(16):
                    qt, a = u // 2, u % 2
                    for h in range(2):
                        e.wait_ge(S["mx_ps"], N * 32 + (2 * u + h + 1))
                        e.tensor_reduce(MX[:, a, qt, h:h + 1], MXP[h][:, :], AX.X, ALU.max).then_inc(S["mx_red"], 1)
                e.drain()
                e.tensor_reduce(NM[:, :, :], MX[:, :, :, :], AX.X, ALU.max, negate=True)
                e.drain()
                mt = MT[:, :, :].rearrange("p t (a r) -> p a t r", a=2)
                for k in range(3):
                    e.tensor_copy(mt[:, :, :, MROW + k], NM[:, :, :])
                    e.drain()
                    if k < 2:
                        e.tensor_tensor(NM[:, :, :], NM[:, :, :], mt[:, :, :, MROW + k], ALU.subtract)
                        e.drain()
                e.drain().then_inc(S["nm"], 1)

            def add_m(N, s):
                e.wait_ge(S["mt_ps"], N + 1)
                e.tensor_tensor(QM[s][:, :], QPK[s][:, :], MIB, ALU.add).then_inc(S["qm"], 1)

            def context(N, s, p, nxt):
                if nxt:
                    maxima(N + 1, 1 - s)
                e.wait_ge(S["pv_ps"], N * 16 + 16)
                e.tensor_copy(OE[:, :], OP[:, :]).then_inc(S["oe"], 1)
                if nxt:
                    add_m(N + 1, 1 - s)
                e.wait_ge(S["ot_ps"], N + 1)
                o = MI[:, :].rearrange("p (t a c r) -> p a c t r", t=4, a=2, c=2)
                for a in range(2):
                    e.reciprocal(RC[:, a, :, :], o[:, a, :, :, AD])
                e.drain()
                for a in range(2):
                    x = e.tensor_tensor(CX[:, :, bass.ds(p * 16 + 8 * a, AD)].rearrange("p (c t) d -> p c t d", c=2),
                                        o[:, a, :, :, 0:AD], RC[:, a, :, :].unsqueeze(3).to_broadcast([P, 2, 4, AD]),
                                        ALU.mult)
                e.drain().then_inc(S["ctx"], 1)

            with e.Fori(0, BATCH) as b:
                xt = lambda t: X[:, bass.ds(b * TPB + t, 1), :].rearrange("p a d -> p (a d)")
                layernorm(xt, lambda t: XNa[:, t, :], 0, b)
                e.drain().then_inc(S["xn"], 1)
                for i in range(2):
                    e.wait_ge(S["q_ps"], b * 2 + i + 1)
                    e.tensor_scalar(Q32[:, :], EXP[i][:, :], COLS[:, i:i + 1], None, ALU.add)
                    e.drain()
                    e.tensor_copy(QP3[:, i, 0, :], Q32[:, :])
                    e.drain()
                    e.tensor_tensor(QR[:, :], Q32[:, :], QP3[:, i, 0, :], ALU.subtract)
                    e.drain()
                    e.tensor_copy(QP3[:, i, 1, :], QR[:, :])
                    e.drain()
                    e.tensor_tensor(QP3[:, i, 2, :], QR[:, :], QP3[:, i, 1, :], ALU.subtract).then_inc(S["split"], 1)
                for t in range(TPB):
                    e.wait_ge(S["ss_ps"], b * TPB + t + 1)
                    e.tensor_reduce(SM[:, t:t + 1], EXP[t % 2][:, :], AX.X, ALU.max, negate=True)
                    e.drain()
                    e.tensor_scalar(SMS[:, t:t + 1], SM[:, t:t + 1], RANK ** -0.5, None, ALU.mult).then_inc(S["ssm_ready"], 1)
                maxima(b * AP_, 0)
                add_m(b * AP_, 0)
                with e.Fori(0, AP_ // 2 - 1) as gp:
                    for s in range(2):
                        context(b * AP_ + gp * 2 + s, s, gp * 2 + s, True)
                context(b * AP_ + (AP_ - 2), 0, AP_ - 2, True)
                context(b * AP_ + (AP_ - 1), 1, AP_ - 1, False)
                e.wait_ge(S["e_ready"], b * TPB + TPB)
                e.memset(THR[:, :], 0)
                e.memset(BIT[:, :], 1 << 29)
                e.drain()
                with e.Fori(0, 30) as it:
                    e.tensor_tensor(CND[:, :], THR[:, :], BIT[:, :], ALU.bitwise_or)
                    e.drain()
                    for t in range(TPB):
                        e.tensor_scalar(J[:, t, :], E[:, t, :], CND[:, t:t + 1].bitcast(F32), 0.0, ALU.is_ge, ALU.add,
                                        accum_out=CNT[:, t:t + 1])
                    e.drain()
                    e.tensor_scalar(MSK[:, :], CNT[:, :], float(KEEP), None, ALU.is_ge)
                    e.tensor_scalar(BIT[:, :], BIT[:, :], 1, None, ALU.logical_shift_right)
                    e.drain()
                    e.copy_predicated(THR[:, :], MSK[:, :], CND[:, :])
                    e.drain()
                for t in range(TPB):
                    th = THR[:, t:t + 1].bitcast(F32)
                    e.tensor_scalar(GT[:, :], E[:, t, :], th, 0.0, ALU.is_gt, ALU.add, accum_out=CNT[:, t:t + 1])
                    e.tensor_scalar(EQ[:, :], E[:, t, :], th, None, ALU.is_equal)
                    e.drain()
                    e.tensor_scalar(REM[:, t:t + 1], CNT[:, t:t + 1], -1.0, float(KEEP), ALU.mult, ALU.add)
                    e.tensor_tensor_scan(RK[:, :], EQ[:, :], EQ[:, :], 0.0, ALU.add, ALU.max)
                    e.drain()
                    e.scalar_tensor_tensor(EQ[:, :], RK[:, :], REM[:, t:t + 1], EQ[:, :], ALU.is_le, ALU.mult)
                    e.drain()
                    e.tensor_tensor(GT[:, :], GT[:, :], EQ[:, :], ALU.add)
                    e.drain()
                    if t >= 1:
                        e.wait_ge(S["wT_ps"], b * TPB + t)
                    e.scalar_tensor_tensor(W[:, :], E[:, t, :], 1.0, GT[:, :], ALU.mult, ALU.mult,
                                           accum_out=TOP[:, t:t + 1]).then_inc(S["w_ready"], 1)
                    e.drain()
                    e.scalar_tensor_tensor(DEN[:, t:t + 1], Z[:, t:t + 1], 1e-9, TOP[:, t:t + 1], ALU.mult, ALU.add)
                    e.drain()
                    e.reciprocal(RDN[:, t:t + 1], DEN[:, t:t + 1])
                    e.drain()
                    e.wait_ge(S["sp_ps"], b * TPB + t + 1)
                    e.tensor_scalar(SP_[:, t, :], OP[:, 0:P], RDN[:, t:t + 1], SG[:, 3:4], ALU.mult, ALU.mult)\
                        .then_inc(S["r1"], 1)
                e.drain()
                e.wait_ge(S["dense_ps"], b + 1)
                sp = SP_[:, :, :].rearrange("p t d -> p (t d)")
                e.scalar_tensor_tensor(sp, EXP[1][:, :], SG[:, 2:3], sp, ALU.mult, ALU.add)
                e.drain()
                e.tensor_tensor(SP_[:, :, :], SP_[:, :, :], XNa[:, :, :], ALU.add)
                e.drain()

                def affine(i):
                    e.drain()
                    e.tensor_tensor(R1[:, :, :], R1[:, :, :], GB[:, i, :].unsqueeze(1).to_broadcast([P, TPB, P]), ALU.mult)
                    e.drain()
                    return e.tensor_tensor(R1[:, :, :], R1[:, :, :], GB[:, i + 1, :].unsqueeze(1).to_broadcast([P, TPB, P]),
                                           ALU.add)

                layernorm(lambda t: SP_[:, t, :], lambda t: R1[:, t, :], 1, b)
                affine(0).then_inc(S["x1"], 1)
                e.wait_ge(S["ff_ps"], b + 1)
                for i in range(2):
                    x = e.tensor_tensor(SP_[:, 4 * i:4 * i + 4, :].rearrange("p t d -> p (t d)"),
                                        R1[:, 4 * i:4 * i + 4, :].rearrange("p t d -> p (t d)"), MXP[i][:, :], ALU.add)
                e.drain()
                layernorm(lambda t: SP_[:, t, :], lambda t: R1[:, t, :], 2, b)
                affine(2)
                e.drain()
                xb = X[:, bass.ds(b * TPB, TPB), :]
                e.tensor_tensor(xb, xb, R1[:, :, :], ALU.add).then_inc(S["xo"], 1)
                e.drain()
            e.drain().then_inc(S["xout"], 1)


def encoder_inputs(f):
    t = lambda n: np.ascontiguousarray(f(n).T)
    w = f('L0_attn_in_proj_w')
    b = f('L0_attn_in_proj_b')
    cols = np.zeros((P, 9), np.float32)
    cols[:, 0], cols[:, 1] = b[0:P], b[P:2 * P]
    cols[:RANK, 2], cols[:RANK, 3] = f('L0_attn_Qp_b'), f('L0_attn_Kp_b')
    cols[:, 4:8] = f('L0_attn_ff1_b').reshape(4, P).T
    rows = np.concatenate([b[2 * P:], f('L0_attn_Vp_b'), f('L0_attn_out_proj_b'), f('L0_attn_ff2_b'),
                           f('L0_attn_ln1_g'), f('L0_attn_ln1_b'), f('L0_attn_ln2_g'), f('L0_attn_ln2_b')])[None]
    for a in range(2):
        cols[64 * a + MROW:64 * a + MROW + 3, 8] = 1
    return dict(
        wqk=np.ascontiguousarray(w[:2 * P].reshape(2, P, P).transpose(2, 0, 1)), wqs=t('L0_attn_Qp_w'), wks=t('L0_attn_Kp_w'),
        wv2=np.ascontiguousarray(np.concatenate([w[2 * P:], f('L0_attn_Vp_w')], 0).T), wout=t('L0_attn_out_proj_w'),
        wf1=t('L0_attn_ff1_w'), wf2=np.ascontiguousarray(f('L0_attn_ff2_w').T.reshape(4, P, P).transpose(1, 0, 2)),
        rows=np.ascontiguousarray(rows), cols=cols, lam=np.ascontiguousarray(f('L0_attn_lam').reshape(1, 1)))


def stage_b(nc, X, wqkv, wo, w1, w2, b1, b2, lngb, scales, rope, mask, ident, shift, edge, out):
    ctx = ExitStack()
    with ctx:
        def sb(name, shape, dt=F32):
            return ctx.enter_context(nc.sbuf_tensor("b_" + name, shape, dt))

        def pb(name, shape, dt=F32):
            return ctx.enter_context(nc.psum_tensor("b_" + name, shape, dt))

        def sem(name):
            return ctx.enter_context(nc.semaphore("b_" + name))

        H = sb("H", [P, TILES, P])
        IDN = sb("IDN", [P, P])
        SH = sb("SH", [P, P])
        ED = sb("ED", [P, P])
        IDB = sb("IDB", [P, P], BF16)
        MSK = sb("MSK", [P, 2, 512], BF16)
        Wqkv = sb("Wqkv", [P, 3 * INNER])
        Wo = sb("Wo", [P, PAIRS, P])
        W1 = sb("W1", [P, 2 * FF])
        W2 = sb("W2", [P, 3, P])
        B1 = sb("B1", [P, 2, 3])
        GB = sb("GB", [P, 2])
        SC = sb("SC", [P, 4, DH])
        RT = sb("RT", [P, 4, TPB, DH])
        RL = sb("RL", [P, 4, TPB, DH])
        HS = [sb(f"HS{i}", [P, P]) for i in range(2)]
        HM = [sb(f"HM{i}", [P, P]) for i in range(2)]
        xsT = [sb(f"xsT{i}", [P, WIN + P]) for i in range(2)]
        SQ = sb("SQ", [P, 2, INNER])
        SS = sb("SS", [P, 2, HEADS])
        RN = sb("RN", [P, 2, HEADS])
        NHALF = sb("NHALF", [P, HEADS])
        T1 = sb("T1", [P, 2, INNER])
        T2 = sb("T2", [P, 2, INNER])
        QH = sb("QH", [P, 2, INNER])
        qT = [sb(f"qT{i}", [P, PAIRS, P]) for i in range(2)]
        kT = [sb(f"kT{i}", [P, PAIRS, WIN + P]) for i in range(2)]
        V2 = [sb(f"V2{i}", [P, NWIN, 512]) for i in range(2)]
        M = sb("M", [P, HEADS])
        PD = sb("PD", [P, PAIRS, 2, SPAN])
        PE_ = sb("PE_", [P, PAIRS, 2, SPAN])
        RS = sb("RS", [P, HEADS])
        RR = sb("RR", [P, HEADS])
        PTr = sb("PTr", [P, PAIRS, P])
        ON = sb("ON", [P, PAIRS, 2, DH])
        OT = sb("OT", [P, PAIRS, P])
        XJ = sb("XJ", [P, P])
        ST = sb("ST", [P, 6])
        MV = sb("MV", [P, 2])
        VE = sb("VE", [P, 1])
        RSTD = sb("RSTD", [P, 1])
        XN = sb("XN", [P, P])
        XNT = sb("XNT", [P, P])
        G = sb("G", [P, 3, P])
        HPT = sb("HPT", [P, 3, P])
        ST0 = sb("ST0", [P, TILES, 6])
        MV0 = sb("MV0", [P, TILES, 2])
        VE0 = sb("VE0", [P, TILES])
        RS0 = sb("RS0", [P, TILES])
        NH0 = sb("NH0", [P, TILES])

        PA = pb("PA", [P, 1024])
        PB = pb("PB", [P, 1024])
        PV = [pb(f"PV{i}", [P, 512]) for i in range(2)]
        PT = [pb(f"PT{i}", [P, 512]) for i in range(2)]

        names = """loaded consts ln0_var ln0_rstd ln0_done
            hs_ready xsT_ps xsT_ready qk_ps v_ps v_ready sq_ready ss_ready rn_ready rope_ready
            tr_ps qkT_ready s_ps sub_ready p_ready sum_ready pt_ps pt_ready o_ps o_ready ot_ps ot_ready
            wo_ps hm_ready shift_ps var_ready rstd_ready xn_ready xnT_ps xnT_ready hg_ps gelu_ready
            hp_ready ff_ps h_ready out_ready stored pe_step pool_step dve_step zeroed sc_load f_load a_load n_load rl_done hm_zeroed turned idb_ready""".split()
        S = {n: sem(n) for n in names}
        NCONST = 8
        NW = 10

        def wait(e, name, value):
            if not isinstance(value, int) or value > 0:
                e.wait_ge(S[name], value)

        def pe_enter(e, TF, sf, first_f):
            wait(e, "hs_ready", TF + 1)
            e.matmul(PV[0][0:64, 3 * P:], HS[sf][:, 0:64], IDN[:, :], start=True, stop=True)
            x = e.matmul(PV[0][64:128, 3 * P:], HS[sf][:, 64:128], SH[:, :], start=True, stop=first_f)
            if not first_f:
                x = e.matmul(PV[0][64:128, 3 * P:], HS[1 - sf][:, 64:128], ED[:, :], start=False, stop=True)
            x.then_inc(S["xsT_ps"], 1)

        def pe_round(e, T, s, n=True, a=True, f=True, first_a=False, first_next=False):
            TA, TF, sa, sf = T + 1, T + 2, 1 - s, s

            def qk():
                wait(e, "ot_ready", 2 * TA)
                wait(e, "qkT_ready", 4 * TA + 4)
                e.sem_inc(S["pe_step"], 1)
                for h in range(2):
                    e.matmul(PA[:, 512 * h:512 * h + 512], IDB[:, :], MSK[:, 0 if first_a else 1, :],
                             start=True, stop=False, skip_group_check=True)
                for p in range(PAIRS):
                    for h in range(2):
                        for w in range(NWIN):
                            x = e.matmul(PA[WIN * w:WIN * w + WIN, 512 * h + SPAN * p:512 * h + SPAN * p + SPAN],
                                         qT[sa][64 * h:64 * h + 64, p, WIN * w:WIN * w + WIN],
                                         kT[sa][64 * h:64 * h + 64, p, WIN * w:WIN * w + SPAN],
                                         start=False, stop=True, skip_group_check=True)
                x.then_inc(S["s_ps"], 1)

            def shift_mid():
                wait(e, "hm_ready", T + 1)
                wait(e, "qkT_ready", 4 * TA + 4)
                e.matmul(PT[0][:, 0:64], SH[:, :], HM[s][:, 64:128], start=True, stop=False)
                e.matmul(PT[0][:, 0:64], ED[:, :], HM[1 - s][:, 64:128], start=False, stop=True)\
                    .then_inc(S["shift_ps"], 1)

            def project(i):
                if i == 0:
                    wait(e, "xsT_ready", TF + 1)
                    wait(e, "turned", 2 * TF)
                else:
                    wait(e, "turned", 2 * TF + 1)
                for j in range(2):
                    col = (2 * i + j) * 512
                    x = e.matmul(PB[:, 512 * j:512 * j + 512], xsT[sf][:, WIN:], Wqkv[:, col:col + 512],
                                 start=True, stop=True)
                x.then_inc(S["qk_ps"], 1)

            def values(w):
                if w == 0:
                    wait(e, "h_ready", T + 1)
                if w == 1:
                    wait(e, "hm_ready", TA)
                if w >= 2:
                    wait(e, "v_ready", TF * NWIN + (w - 1))
                for h in range(2):
                    x = e.matmul(PV[w % 2][64 * h:64 * h + 64, :], xsT[sf][:, WIN * w:WIN * w + SPAN],
                                 Wqkv[:, 2 * INNER + 512 * h:2 * INNER + 512 * h + 512], start=True, stop=True)
                x.then_inc(S["v_ps"], 1)

            def p_transposes():
                wait(e, "p_ready", TA + 1)
                if n:
                    wait(e, "var_ready", T + 1)
                for hb in range(2):
                    for j in range(4):
                        x = e.transpose(PT[hb][:, P * j:P * j + P],
                                        PE_[:, 4 * hb + j, :, :].rearrange("p a k -> p (a k)"), IDN[:, :])
                    x.then_inc(S["pt_ps"], 1)

            def pv():
                wait(e, "v_ready", TA * NWIN + NWIN)
                for hb in range(2):
                    wait(e, "pt_ready", 2 * TA + (hb + 1))
                    e.sem_inc(S["pe_step"], 1)
                    for p in range(4 * hb, 4 * hb + 4):
                        for h in range(2):
                            for w in range(NWIN):
                                x = e.matmul(PA[WIN * w:WIN * w + WIN, 512 * h + DH * p:512 * h + DH * p + DH],
                                             PTr[64 * h:64 * h + 64, p, WIN * w:WIN * w + WIN],
                                             V2[sa][64 * h:64 * h + 64, w, DH * p:DH * p + DH],
                                             start=True, stop=True)
                x.then_inc(S["o_ps"], 1)

            def o_transposes():
                wait(e, "o_ready", TA + 1)
                for hb in range(2):
                    for j in range(4):
                        x = e.transpose(PA[:, 512 * hb + P * j:512 * hb + P * j + P],
                                        ON[:, 4 * hb + j, :, :].rearrange("p a k -> p (a k)"), IDN[:, :])
                    x.then_inc(S["ot_ps"], 1)

            def qk_transposes(i):
                wait(e, "rope_ready", 2 * TF + (i + 1))
                for hb in range(2):
                    if i == 0 and a:
                        wait(e, "pt_ready", 2 * TA + (hb + 1))
                    if i == 1:
                        wait(e, "qkT_ready", 4 * TF + (hb + 1))
                    for j in range(4):
                        c = (4 * hb + j) * P
                        x = e.transpose(PT[hb][:, P * j:P * j + P], QH[:, i, c:c + P], IDN[:, :])
                    x.then_inc(S["tr_ps"], 1)

            def xn_transpose():
                wait(e, "xn_ready", T + 1)
                wait(e, "v_ready", TF * NWIN + 3)
                e.transpose(PV[0][:, 3 * P:], XN[:, :], IDN[:, :]).then_inc(S["xnT_ps"], 1)

            def ff_up():
                wait(e, "xnT_ready", T + 1)
                wait(e, "v_ready", TF * NWIN + NWIN)
                for i in (1, 0):
                    for j, (c, m) in enumerate(FFC):
                        x = e.matmul(PV[i][0:m, P * j:P * j + P], W1[:, FF * i + c:FF * i + c + m], XNT[:, :],
                                     start=True, stop=True)
                    x.then_inc(S["hg_ps"], 1)

            def out_project():
                wait(e, "v_ready", TF * NWIN + NWIN)
                for hb in range(2):
                    wait(e, "ot_ready", 2 * TA + (hb + 1))
                    for j in range(4 * hb, 4 * hb + 4):
                        x = e.matmul(PV[1][:, 3 * P:], OT[:, j, :], Wo[:, j, :], start=(j == 0), stop=(j == 7))
                x.then_inc(S["wo_ps"], 1)

            def ff_down():
                wait(e, "hp_ready", T + 1)
                for j in range(3):
                    x = e.matmul(PV[1][:, 0:P], HPT[:, j, :], W2[:, j, :], start=(j == 0), stop=(j == 2))
                x.then_inc(S["ff_ps"], 1)

            if f:
                project(0)
            if n:
                shift_mid()
            if a:
                qk()
            if f:
                for w in range(NWIN):
                    values(w)
                project(1)
            if n:
                xn_transpose()
            if a:
                p_transposes()
            if n:
                ff_up()
            if a:
                pv()
            if f:
                qk_transposes(0)
            if n:
                ff_down()
            pe_enter(e, TF + 1, 1 - sf, first_next)
            if a:
                o_transposes()
                out_project()
            if f:
                qk_transposes(1)

        quads = lambda t: t.rearrange("p (j t) -> p j t", t=P)

        def act_enter(e, TF, sf, tile):
            wait(e, "xsT_ps", TF)
            e.activation(HS[sf][:, :], H[:, tile, :].rearrange("p a d -> p (a d)"), ACT.Copy)\
                .then_inc(S["hs_ready"], 1)
            e.activation(xsT[sf][:, 0:WIN], xsT[1 - sf][:, P:P + WIN], ACT.Copy)
            wait(e, "xsT_ps", TF + 1)
            e.activation(xsT[sf][:, WIN:], PV[0][:, 3 * P:], ACT.Copy)
            e.drain().then_inc(S["xsT_ready"], 1)

        def act_round(e, T, s, tile_next, n=True, a=True, f=True, first_f=False):
            TA, TF, sa, sf = T + 1, T + 2, 1 - s, s

            def copy_v(w):
                wait(e, "v_ps", NWIN * TF + (w + 1))
                e.activation(V2[sf][:, w, :], PV[w % 2][:, :], ACT.Copy).then_inc(S["v_ready"], 1)

            def copy_qk(i):
                for hb in range(2):
                    wait(e, "tr_ps", 4 * TF + (2 * i + hb + 1))
                    dst = qT[sf][:, 4 * hb:4 * hb + 4, :] if i == 0 else kT[sf][:, 4 * hb:4 * hb + 4, WIN:]
                    e.activation(dst, quads(PT[hb][:, :]), ACT.Copy).then_inc(S["qkT_ready"], 1)

            if f:
                wait(e, "qk_ps", 2 * TF + 1)
                e.activation(SQ[:, 0, :], PB[:, :], ACT.Square).then_inc(S["sq_ready"], 1)
                copy_v(0)
                copy_v(1)
            if a:
                wait(e, "sub_ready", TA + 1)
                e.activation(PE_[:, :, :, :], PD[:, :, :, :], ACT.Exp, scale=QK_SCALE).then_inc(S["p_ready"], 1)
            if f:
                copy_v(2)
                copy_v(3)
                if first_f:
                    e.memzero(kT[sf][:, :, 0:WIN])
                else:
                    e.activation(kT[sf][:, :, 0:WIN], kT[1 - sf][:, :, P:P + WIN], ACT.Copy)
                wait(e, "qk_ps", 2 * TF + 2)
                e.activation(SQ[:, 1, :], PB[:, :], ACT.Square).then_inc(S["sq_ready"], 1)
            if a:
                for hb in range(2):
                    wait(e, "pt_ps", 2 * TA + (hb + 1))
                    e.activation(PTr[:, 4 * hb:4 * hb + 4, :], quads(PT[hb][:, :]), ACT.Copy).then_inc(S["pt_ready"], 1)
            if n:
                wait(e, "hg_ps", 2 * T + 1)
                for j, (c, m) in enumerate(FFC):
                    e.activation(G[0:m, j, :], PV[1][0:m, P * j:P * j + P], ACT.Gelu, bias=B1[0:m, 1, j:j + 1])\
                        .then_inc(S["gelu_ready"], 1)
            if f:
                copy_qk(0)
            act_enter(e, TF + 1, 1 - sf, tile_next)
            if a:
                for hb in range(2):
                    wait(e, "ot_ps", 2 * TA + (hb + 1))
                    e.activation(OT[:, 4 * hb:4 * hb + 4, :], quads(PA[:, 512 * hb:512 * hb + 512]), ACT.Copy)\
                        .then_inc(S["ot_ready"], 1)
            if f:
                copy_qk(1)

        def dve_round(e, T, s, tp, tile, tile_a, n=True, a=True, f=True):
            TA, TF, sa, sf = T + 1, T + 2, 1 - s, s

            def turn(i):
                v = PB[:, :].rearrange("p (h d) -> p h d", d=DH)
                t1 = T1[:, i, :].rearrange("p (h d) -> p h d", d=DH)
                t2 = T2[:, i, :].rearrange("p (h d) -> p h d", d=DH)
                wait(e, "sq_ready", 2 * TF + (i + 1))
                e.tensor_reduce(SS[:, i, :], SQ[:, i, :].rearrange("p (h d) -> p h d", d=DH), AX.X, ALU.add)\
                    .then_inc(S["ss_ready"], 1)
                e.tensor_tensor(t1, v, RL[:, 2 * i, tp, :].to_broadcast([P, HEADS, DH]), ALU.mult)
                for hf in range(2):
                    sn = RL[:, 2 * i + 1, tp, WIN * hf:WIN * hf + WIN].to_broadcast([P, HEADS, WIN])
                    x = e.tensor_tensor(t2[:, :, WIN * hf:WIN * hf + WIN],
                                        v[:, :, WIN * (1 - hf):WIN * (1 - hf) + WIN], sn, ALU.mult)
                x.then_inc(S["turned"], 1)

            def xn():
                wait(e, "rstd_ready", T + 1)
                e.tensor_scalar(XN[:, :], XJ[:, :], MV[:, 0:1], RSTD[:, :], ALU.subtract, ALU.mult)\
                    .then_inc(S["xn_ready"], 1)

            def normed(i):
                e.drain()
                e.tensor_tensor(T1[:, i, :], T1[:, i, :], T2[:, i, :], ALU.add)
                e.drain()
                wait(e, "rn_ready", 2 * TF + (i + 1))
                e.tensor_tensor(QH[:, i, :].rearrange("p (h d) -> p h d", d=DH),
                                T1[:, i, :].rearrange("p (h d) -> p h d", d=DH),
                                RN[:, i, :].unsqueeze(2).to_broadcast([P, HEADS, DH]), ALU.mult)\
                    .then_inc(S["rope_ready"], 1)

            if f:
                turn(0)
            if n:
                wait(e, "shift_ps", T + 1)
                e.tensor_copy(XJ[:, 0:64], HM[s][:, 0:64])
                e.tensor_copy(XJ[:, 64:128], PT[0][:, 0:64])
                e.drain()
                e.bn_stats(ST[:, :], XJ[:, :])
                e.drain()
                e.bn_aggr(MV[:, :], ST[:, :])
                e.drain()
                e.tensor_scalar(VE[:, :], MV[:, 1:2], EPS, None, ALU.add).then_inc(S["var_ready"], 1)
            if a:
                wait(e, "s_ps", TA + 1)
                e.tensor_reduce(M[:, :], PA[:, :].rearrange("p (h k) -> p h k", k=SPAN), AX.X, ALU.max)
                e.drain()
                e.tensor_tensor(PD[:, :, :, :].rearrange("p j a k -> p a j k"),
                                PA[:, :].rearrange("p (a j k) -> p a j k", a=2, k=SPAN),
                                M[:, :].rearrange("p (a j) -> p a j", a=2).unsqueeze(3)
                                .to_broadcast([P, 2, PAIRS, SPAN]),
                                ALU.subtract).then_inc(S["sub_ready"], 1)
            if n:
                xn()
            if f:
                normed(0)
            if n:
                wait(e, "xnT_ps", T + 1)
                e.tensor_scalar(XNT[:, :], PV[0][:, 3 * P:], GB[:, 0:1], GB[:, 1:2], ALU.mult, ALU.add)\
                    .then_inc(S["xnT_ready"], 1)
            if a:
                wait(e, "p_ready", TA + 1)
                e.tensor_reduce(RS[:, :], PE_[:, :, :, :].rearrange("p j a k -> p (j a) k"), AX.X, ALU.add)
                e.drain()
                e.reciprocal(RR[:, :], RS[:, :])
            if f:
                turn(1)
            if n:
                for j, (c, m) in enumerate(FFC):
                    wait(e, "gelu_ready", 3 * T + (j + 1))
                    if j == 0:
                        wait(e, "hg_ps", 2 * T + 2)
                    x = e.scalar_tensor_tensor(HPT[0:m, j, :], PV[0][0:m, P * j:P * j + P], B1[0:m, 0, j:j + 1],
                                               G[0:m, j, :], ALU.add, ALU.mult)
                x.then_inc(S["hp_ready"], 1)
            if a:
                e.drain()
                wait(e, "o_ps", TA + 1)
                e.tensor_tensor(ON[:, :, :, :].rearrange("p j a k -> p a j k"),
                                PA[:, :].rearrange("p (a j k) -> p a j k", a=2, k=DH),
                                RR[:, :].rearrange("p (j a) -> p a j", a=2).unsqueeze(3)
                                .to_broadcast([P, 2, PAIRS, DH]),
                                ALU.mult).then_inc(S["o_ready"], 1)
            if f:
                normed(1)
            if a:
                wait(e, "wo_ps", TA + 1)
                e.tensor_tensor(HM[sa][:, :], H[:, tile_a, :].rearrange("p a d -> p (a d)"), PV[1][:, 3 * P:],
                                ALU.add).then_inc(S["hm_ready"], 1)
            if n:
                wait(e, "ff_ps", T + 1)
                e.tensor_tensor(H[:, tile, :].rearrange("p a d -> p (a d)"), HM[s][:, :], PV[1][:, 0:P], ALU.add)\
                    .then_inc(S["h_ready"], 1)

        def pool_round(e, T, n=True, f=True):
            TF = T + 2

            def norms(i):
                wait(e, "ss_ready", 2 * TF + (i + 1))
                e.sem_inc(S["pool_step"], 1)
                e.tensor_scalar(SS[:, i, :], SS[:, i, :], 1e-24, None, ALU.max)
                e.drain()
                e.tensor_tensor(RN[:, i, :], SS[:, i, :], NHALF[:, :], ALU.pow).then_inc(S["rn_ready"], 1)

            if n:
                wait(e, "var_ready", T + 1)
                e.tensor_tensor(RSTD[:, :], VE[:, :], NHALF[:, 0:1], ALU.pow).then_inc(S["rstd_ready"], 1)
            if f:
                norms(0)
                norms(1)

        HALF = TPB // 2
        block = ctx.enter_context(nc.Block())

        @block.sync
        def _(e):
            for dst, s_ in ((IDN[:, :], ident), (SH[:, :], shift), (ED[:, :], edge),
                            (T1[:, :, :].rearrange("p i (v x) -> p (i v) x", v=2)[:, 0:2, :], mask),
                            (RT[:, :, :, :], rope)):
                e.dma_start(dst, s_).then_inc(S["consts"], 16)
            e.wait_ge(S["zeroed"], 1)

            def load(L, ly):
                if L is not None:
                    e.wait_ge(S["rl_done"], L * BATCH + BATCH)
                e.dma_start(SC[:, :, :].rearrange("p a d -> p (a d)"),
                            scales[ly, :].to_broadcast([P, 4 * DH])).then_inc(S["sc_load"], 16)
                if L is not None:
                    e.wait_ge(S["tr_ps"], (L + 1) * (4 * TILES))
                e.dma_start(Wqkv[:, :], wqkv[ly].squeeze(0)).then_inc(S["f_load"], 16)
                if L is not None:
                    e.wait_ge(S["wo_ps"], (L + 1) * TILES)
                e.dma_start(Wo[:, :, :], wo[ly].squeeze(0).rearrange("(j p) n -> p j n", p=P)).then_inc(S["a_load"], 16)
                if L is not None:
                    e.wait_ge(S["h_ready"], (L + 1) * TILES + 1)
                w2l = w2[ly].squeeze(0)
                for dst, s_ in ((W1[:, :], w1[ly].squeeze(0)),
                                (W2[:, 0:2, :], w2l[0:2 * P, :].rearrange("(j p) n -> p j n", p=P)),
                                (W2[0:FF - 2 * P, 2, :], w2l[2 * P:FF, :]),
                                (B1[:, :, :], b1[ly].squeeze(0)), (W2[FF - 2 * P:FF - 2 * P + 1, 2, :], b2[ly, :]),
                                (GB[:, :], lngb[ly].squeeze(0))):
                    e.dma_start(dst, s_).then_inc(S["n_load"], 16)

            def load_ahead(L):
                e.wait_ge(S["rl_done"], L * BATCH + BATCH)
                for name in ("sc_load", "f_load", "a_load"):
                    e.sem_inc(S[name], 16)

            load(None, slice(0, 1))
            with e.Fori(0, DEPTH - 1) as L:
                load(L, bass.ds(L + 1, 1))
            load_ahead(DEPTH - 1)
            e.wait_ge(S["out_ready"], 1)
            e.dma_start(out.rearrange("b (t p) d -> p (b t) d", p=P), X[:, :, :]).then_inc(S["stored"], 16)
            e.wait_ge(S["stored"], 16)

        N_LOADS = 6 * 16

        def SCW(B):
            return ((B + 1) // BATCH + 1) * 16

        @block.gpsimd
        def _(e):
            e.memset(NHALF[:, :], -0.5)
            e.memset(NH0[:, :], -0.5)
            e.memset(W2[:, :, :], 0.0)
            e.memset(HPT[:, :, :], 1.0)
            for t in (*kT, *xsT, *HS, *HM):
                e.memset(t[:], 0.0)
            e.drain().then_inc(S["zeroed"], 1)
            e.wait_ge(S["ln0_var"], 1)
            e.tensor_tensor(RS0[:, :], VE0[:, :], NH0[:, :], ALU.pow).then_inc(S["ln0_rstd"], 1)
            pool_round(e, -2, n=False)
            pool_round(e, -1, n=False)
            with e.Fori(0, DEPTH * BATCH) as B:
                with e.Fori(0, HALF) as g:
                    for s in range(2):
                        pool_round(e, B * TPB + g * 2 + s)

        @block.scalar
        def _(e):
            e.wait_ge(S["ln0_done"], 1)
            act_enter(e, 0, 0, slice(0, 1))
            act_round(e, -2, 0, slice(1, 2), n=False, a=False, first_f=True)
            act_round(e, -1, 1, slice(2, 3), n=False)
            with e.Fori(0, DEPTH * BATCH) as B:
                with e.Fori(0, HALF - 1) as g:
                    for s in range(2):
                        act_round(e, B * TPB + g * 2 + s, s, bass.ds((B * TPB + g * 2 + (s + 3)) % TILES, 1))
                for s in range(2):
                    act_round(e, B * TPB + (TPB - 2 + s), s, bass.ds(((B + 1) % BATCH) * TPB + (s + 1), 1),
                              first_f=(s == 0))

        @block.vector
        def _(e):
            e.wait_ge(S["zeroed"], 1)
            for t in range(TILES):
                e.bn_stats(ST0[:, t, :], X[:, t, :])
            e.drain()
            for t in range(TILES):
                e.bn_aggr(MV0[:, t, :], ST0[:, t, :])
            e.drain()
            e.tensor_scalar(VE0[:, :], MV0[:, :, 1], EPS, None, ALU.add).then_inc(S["ln0_var"], 1)
            e.wait_ge(S["ln0_rstd"], 1)
            for t in range(TILES):
                e.tensor_scalar(H[:, t, :], X[:, t, :], MV0[:, t, 0:1], RS0[:, t:t + 1], ALU.subtract, ALU.mult)
            e.drain().then_inc(S["ln0_done"], 1)
            e.wait_ge(S["consts"], 16 * 5)
            e.tensor_copy(MSK[:, :, :], T1[:, :, :].rearrange("p i (v x) -> p (i v) x", v=2)[:, 0:2, :])
            e.tensor_copy(IDB[:, :], IDN[:, :])
            e.drain().then_inc(S["h_ready"], 1)

            def rotation_tables():
                for i in range(4):
                    e.tensor_tensor(RL[:, i, :, :], RT[:, i, :, :],
                                    SC[:, i, :].unsqueeze(1).to_broadcast([P, TPB, DH]), ALU.mult)
                e.drain().then_inc(S["rl_done"], 1)

            e.wait_ge(S["sc_load"], 16)
            rotation_tables()
            dve_round(e, -2, 0, slice(0, 1), None, None, n=False, a=False)
            dve_round(e, -1, 1, slice(1, 2), None, slice(0, 1), n=False)
            with e.Fori(0, DEPTH * BATCH) as B:
                e.drain()
                e.memset(HM[1][:, :], 0.0).then_inc(S["hm_zeroed"], 1)
                e.drain()
                e.wait_ge(S["n_load"], (B // BATCH + 1) * N_LOADS)
                e.sem_inc(S["dve_step"], 1)
                with e.Fori(0, HALF - 1) as g:
                    for s in range(2):
                        dve_round(e, B * TPB + g * 2 + s, s, bass.ds(g * 2 + (s + 2), 1),
                                  bass.ds((B % BATCH) * TPB + g * 2 + s, 1),
                                  bass.ds((B % BATCH) * TPB + g * 2 + (s + 1), 1))
                e.drain()
                e.wait_ge(S["sc_load"], SCW(B))
                rotation_tables()
                for s in range(2):
                    dve_round(e, B * TPB + (TPB - 2 + s), s, slice(s, s + 1),
                              bass.ds((B % BATCH) * TPB + (TPB - 2 + s), 1),
                              bass.ds((B * TPB + (TPB - 1 + s)) % TILES, 1))
            e.drain()
            e.tensor_tensor(X[:, :, :], X[:, :, :], H[:, :, :], ALU.add).then_inc(S["out_ready"], 1)

        @block.tensor
        def _(e):
            e.wait_ge(S["consts"], 16 * 5)
            e.wait_ge(S["h_ready"], 1)
            e.wait_ge(S["f_load"], 16)
            e.wait_ge(S["a_load"], 16)
            pe_enter(e, 0, 0, True)
            pe_round(e, -2, 0, n=False, a=False)
            pe_round(e, -1, 1, n=False, first_a=True)
            with e.Fori(0, DEPTH * BATCH) as B:
                e.wait_ge(S["n_load"], (B // BATCH + 1) * N_LOADS)
                e.wait_ge(S["hm_zeroed"], B + 1)
                e.sem_inc(S["pe_step"], 1)
                with e.Fori(0, HALF - 2) as g:
                    for s in range(2):
                        pe_round(e, B * TPB + g * 2 + s, s)
                pe_round(e, B * TPB + (TPB - 4), 0)
                pe_round(e, B * TPB + (TPB - 3), 1, first_next=True)
                e.wait_ge(S["f_load"], SCW(B))
                e.sem_inc(S["pe_step"], 1)
                pe_round(e, B * TPB + (TPB - 2), 0)
                e.wait_ge(S["a_load"], SCW(B))
                e.sem_inc(S["pe_step"], 1)
                pe_round(e, B * TPB + (TPB - 1), 1, first_a=True)


def rope_tables():
    half = np.arange(0, DH, 2, dtype=np.float32)
    inv_freq = (np.float32(1.0) / np.float32(10000.0) ** (half / np.float32(DH))).astype(np.float32)
    t = np.arange(SEQ, dtype=np.float32)
    fr = t[:, None] * inv_freq[None, :]
    fr = np.concatenate([fr, fr], -1).astype(np.float32)
    base = ((half + np.float32(0.4 * DH)) / np.float32(1.4 * DH)).astype(np.float32)
    power = ((t - SEQ // 2) / np.float32(WIN // 2)).astype(np.float32)
    scale = (base[None, :] ** power[:, None]).astype(np.float32)
    scale = np.concatenate([scale, scale], -1)
    sign = np.where(np.arange(DH) < DH // 2, -1.0, 1.0).astype(np.float32)
    cos, sin = np.cos(fr), np.sin(fr) * sign
    tabs = np.stack([cos * scale, sin * scale, cos / scale, sin / scale]).astype(np.float32)
    return np.ascontiguousarray(tabs.reshape(4, TPB, P, DH).transpose(2, 0, 1, 3))


def masks():
    i = np.arange(P)[:, None] % WIN
    j = np.arange(SPAN)[None, :]
    seen = (i <= j) & (j <= i + WIN)
    first = seen & ~((np.arange(P)[:, None] < WIN) & (j < WIN))
    tab = np.stack([first, seen], 1)
    tab = np.where(tab, 0.0, -1e30)
    return np.tile(tab, (1, 1, 8)).astype(np.float32)


def up_biases(b1):
    cols = np.zeros((DEPTH, 2, 3 * P), np.float32)
    cols[:, :, :FF] = b1.reshape(DEPTH, 2, FF)
    return np.ascontiguousarray(cols.reshape(DEPTH, 2, 3, P).transpose(0, 3, 1, 2))


def build(nc, enc, stk, scratch, out):
    with nc.sbuf_tensor("X", [P, TILES, P], F32) as X:
        stage_a(nc, X, scratch=scratch, **enc)
        stage_b(nc, X, out=out, **stk)


def stack_inputs(f):
    rot = np.r_[DH // 2:DH, 0:DH // 2]
    heads = [np.arange(a, HEADS, 2) for a in range(2)]
    vcols = [(2 * INNER + h[:, None] * DH + np.arange(DH)).ravel() for h in heads]
    order = np.concatenate([np.arange(2 * INNER)] + vcols)
    qs, ks = f('L0_ffn_q_scale'), f('L0_ffn_k_scale')
    edge = np.zeros((P, P), np.float32)
    edge[P - 1, 0] = 1
    return dict(
        wqkv=np.ascontiguousarray(f('L0_ffn_Wqkv')[:, :, order]), wo=f('L0_ffn_Wo'), w1=f('L0_ffn_W1'),
        w2=f('L0_ffn_W2'), b1=up_biases(f('L0_ffn_b1')), b2=f('L0_ffn_b2'),
        lngb=np.ascontiguousarray(np.stack([f('L0_ffn_ln_g'), f('L0_ffn_ln_b')], -1)),
        scales=np.ascontiguousarray(np.concatenate([qs, qs[:, rot], ks, ks[:, rot]], -1)),
        rope=rope_tables(), mask=masks(), shift=np.eye(P, k=1, dtype=np.float32), edge=edge)


def kernel(**inputs):
    import concourse.bacc as bacc
    from concourse.bass_utils import run_bass_kernel_spmd as run
    f = lambda n: np.ascontiguousarray(inputs[n])
    onesrow = np.zeros((P, P), np.float32)
    onesrow[0] = 1
    both = dict(ident=np.eye(P, dtype=np.float32))
    enc = dict(onesrow=onesrow, src=f('L0_attn_src'), **encoder_inputs(f))
    stk = stack_inputs(f)
    nc = bacc.Bacc("TRN2", target_bir_lowering=False, num_devices=1)
    arrays = {**both, **enc, **stk}
    dram = {n: nc.dram_tensor(n + "_dram", a.shape, mybir.dt.from_np(a.dtype), kind="ExternalInput").ap()
            for n, a in arrays.items()}
    out = nc.dram_tensor("out_dram", (BATCH, SEQ, P), F32, kind="ExternalOutput").ap()
    scratch = nc.dram_tensor("parts_dram", (2, 3, P, SEQ), BF16, kind="Internal").ap()
    build(nc, {n: dram[n] for n in (*both, *enc)}, {n: dram[n] for n in (*both, *stk)}, scratch, out)
    r = run(nc, [{n + "_dram": a for n, a in arrays.items()}], core_ids=[0])
    return r.results[0]["out_dram"]
```

```python
import concourse.bass as bass
from concourse import mybir
from contextlib import ExitStack
import numpy as np

F32 = mybir.dt.float32
BF16 = mybir.dt.bfloat16
I32 = mybir.dt.int32
ACT = mybir.ActivationFunctionType
ALU = mybir.AluOpType
AX = mybir.AxisListType

P = 128
BATCH, SEQ = 4, 1024
TPB = SEQ // P
TILES = BATCH * TPB
EPS = 1e-5
AH, AD = 16, 8
PAIRS_A = AH // 2
RANK = 64
KEEP = int(SEQ * 0.2)
AFF = 512
PARTS_Q = (0, 0, 1, 0, 2, 1)
PARTS_K = (0, 1, 0, 2, 0, 1)
MROW = 48


DEPTH, HEADS, DH = 6, 16, 64
PAIRS = HEADS // 2
INNER = HEADS * DH
WIN = 32
NWIN = P // WIN
SPAN = 2 * WIN
FF = 341
FFC = [(0, 128), (128, 128), (256, FF - 256)]
QK_SCALE = 8.0


def stage_a(nc, X, src, scratch, wqk, wqs, wks, wv2, wout, wf1, wf2, rows, cols, ident, onesrow, lam):
    ctx = ExitStack()
    with ctx:
        def sb(name, shape, dt=F32):
            return ctx.enter_context(nc.sbuf_tensor("a_" + name, shape, dt))

        def pb(name, shape, dt=F32):
            return ctx.enter_context(nc.psum_tensor("a_" + name, shape, dt))

        def sem(name):
            return ctx.enter_context(nc.semaphore("a_" + name))

        IDENT = sb("IDENT", [P, P])
        IDENT_BF = sb("IDENT_BF", [P, P], BF16)
        ONES_ROW = sb("ONES_ROW", [P, P])
        WQK = sb("WQK", [P, 2, P])
        WQS = sb("WQS", [P, RANK])
        WKS = sb("WKS", [P, RANK])
        WV2 = sb("WV2", [P, 2 * P])
        WOUT = sb("WOUT", [P, P])
        WF1 = sb("WF1", [P, AFF])
        WF2 = sb("WF2", [P, 4, P])
        ROWS = sb("ROWS", [P, 4 * P])
        LN_GB = sb("LN_GB", [P, 4, P])
        COLS = sb("COLS", [P, 9])
        LAM = sb("LAM", [P, 1])
        SIGMOID = sb("SIGMOID", [P, 4])
        STATS = sb("STATS", [P, TPB, 6])
        MEAN_VAR = sb("MEAN_VAR", [P, TPB, 2])
        VAR_EPS = sb("VAR_EPS", [P, TPB])
        RSTD = sb("RSTD", [P, TPB])
        NEG_HALF = sb("NEG_HALF", [P, TPB])
        X_NORM = sb("X_NORM", [P, TPB, P])
        X_NORM_T = sb("X_NORM_T", [P, SEQ])
        QK_FULL = sb("QK_FULL", [P, SEQ])
        QK_REST = sb("QK_REST", [P, SEQ])
        QK_PARTS = sb("QK_PARTS", [P, 2, 3, SEQ], BF16)
        Q_PACK = [sb(f"Q_PACK{i}", [P, SEQ], BF16) for i in range(2)]
        K_PACK = [sb(f"K_PACK{i}", [P, SEQ], BF16) for i in range(2)]
        Q_WITH_MAX = [sb(f"Q_WITH_MAX{i}", [P, SEQ], BF16) for i in range(2)]
        V_DENSE = sb("V_DENSE", [P, TPB, AH, AD])
        V_ONES = [sb(f"V_ONES{i}", [P, TPB, 2, 32]) for i in range(2)]
        SPARSE_Q = sb("SPARSE_Q", [RANK, SEQ])
        SPARSE_K = sb("SPARSE_K", [RANK, SEQ])
        SPARSE_V = sb("SPARSE_V", [P, TPB, P])
        WEIGHTS = sb("WEIGHTS", [P, TPB, SEQ])
        WEIGHT_SUM = sb("WEIGHT_SUM", [P, TPB])
        NEG_SCORE_MAX = sb("NEG_SCORE_MAX", [P, TPB])
        EXP_BIAS = sb("EXP_BIAS", [P, TPB])
        UNUSED_OUT = sb("UNUSED_OUT", [P, TPB, SEQ], BF16)
        THRESHOLD = sb("THRESHOLD", [P, TPB], I32)
        CANDIDATE = sb("CANDIDATE", [P, TPB], I32)
        BIT = sb("BIT", [P, TPB], I32)
        COUNT = sb("COUNT", [P, TPB])
        ENOUGH = sb("ENOUGH", [P, TPB], I32)
        MISSING = sb("MISSING", [P, TPB])
        KEPT_SUM = sb("KEPT_SUM", [P, TPB])
        DENOM = sb("DENOM", [P, TPB])
        DENOM_INV = sb("DENOM_INV", [P, TPB])
        TIED = sb("TIED", [P, SEQ])
        TIE_RANK = sb("TIE_RANK", [P, SEQ])
        ABOVE = sb("ABOVE", [P, SEQ])
        KEPT = sb("KEPT", [P, SEQ])
        KEPT_T = sb("KEPT_T", [P, TPB, P])
        MAX_HALF = sb("MAX_HALF", [P, 2, TPB, 2])
        NEG_MAX = sb("NEG_MAX", [P, 2, TPB])
        NEG_MAX_ROWS = sb("NEG_MAX_ROWS", [P, TPB, P], BF16)
        PROBS_T = [sb(f"PROBS_T{i}", [P, SEQ]) for i in range(2)]
        OUT_T = sb("OUT_T", [P, 512])
        SUM_INV = sb("SUM_INV", [P, 2, 2, 4])
        CONTEXT = sb("CONTEXT", [P, TPB, P])
        CONTEXT_T = sb("CONTEXT_T", [P, TPB, P])
        MIXED = sb("SP", [P, TPB, P])
        NORM_OUT = sb("NORM_OUT", [P, TPB, P])
        NORM_OUT_T = sb("NORM_OUT_T", [P, SEQ])
        HIDDEN_T = sb("HIDDEN_T", [P, 4, SEQ])
        WEIGHTS_HIGH = HIDDEN_T[:, :, :].rearrange("p j s -> p (j s)").bitcast(BF16).rearrange("p (t s) -> p t s", t=TPB)

        PS_MAX = [pb(f"PS_MAX{i}", [P, 512]) for i in range(2)]
        PS_WIDE = [pb(f"PS_WIDE{i}", [P, 1024]) for i in range(2)]
        PS_OUT = pb("PS_OUT", [P, 512])
        PS_TR = pb("PS_TR", [P, 512])
        PS_TR_BF = PS_TR[:, :].bitcast(BF16)

        names = """loaded zeroed var rstd xn xT_ps xT_ready q_ps split parts_stored pack0 pack1 s_ps s_ready v_ps
            v_ready ss_ps ssm_ready e_ready v9 mx_ps mx_red nm mt_ps qm st_ps exp pv_ps oe ot_ps ctx cT_ps
            cT_ready dense_ps w_ready wT_ps wT_ready sp_ps r1 x1 x1T_ps x1T_ready h_ps h_ready ff_ps lam_e
            sig e_high dve_step pe_step sp_step xout""".split()
        S = {n: sem(n) for n in names}
        LOADS = 14

        block = ctx.enter_context(nc.Block())

        @block.sync
        def _(e):
            e.dma_start(X[:, :, :], src.rearrange("b (t p) d -> p (b t) d", p=P)).then_inc(S["loaded"], 16)
            e.wait_ge(S["zeroed"], 1)
            for dst, s_ in ((IDENT[:, :], ident), (ONES_ROW[:, :], onesrow), (WQK[:, :, :], wqk), (WQS[:, :], wqs),
                            (WKS[:, :], wks), (WV2[:, :], wv2), (WOUT[:, :], wout), (WF1[:, :], wf1),
                            (WF2[:, :, :], wf2), (ROWS[0:1, :], rows[0:1, 0:4 * P]),
                            (LN_GB[:, :, :].rearrange("p a d -> p (a d)"), rows[0:1, 4 * P:8 * P].to_broadcast([P, 4 * P])),
                            (COLS[:, :], cols), (LAM[:, :], lam.to_broadcast([P, 1]))):
                e.dma_start(dst, s_).then_inc(S["loaded"], 16)
            e.wait_ge(S["sig"], 1)
            e.sem_inc(S["sp_step"], 1)
            with e.Fori(0, BATCH) as b:
                for i in range(2):
                    e.wait_ge(S["split"], b * 2 + i + 1)
                    for k in range(3):
                        e.dma_start(scratch[i, k], QK_PARTS[:, i, k, :]).then_inc(S["parts_stored"], 16)
                e.wait_ge(S["parts_stored"], (b + 1) * (16 * 6))
                e.sem_inc(S["sp_step"], 1)
                with e.Fori(0, PAIRS_A // 2) as gp:
                    for s in range(2):
                        e.wait_ge(S["ctx"], b * PAIRS_A + gp * 2 + s + 1)
                        p = gp * 2 + s
                        for i, (dst, parts) in enumerate(((Q_PACK[s], PARTS_Q), (K_PACK[s], PARTS_K))):
                            for a in range(2):
                                for g, k in enumerate(parts):
                                    e.dma_start(dst[64 * a + 8 * g:64 * a + 8 * g + 8, :],
                                                scratch[i, k, bass.ds(p * 16 + 8 * a, 8), :]).then_inc(S["pack%d" % s], 16)
            e.wait_ge(S["xout"], 1)

        NPACK = 16 * 24

        @block.gpsimd
        def _(e):
            e.memset(NEG_HALF[:, :], -0.5)
            e.memset(ROWS[:, :], 0.0)
            e.memset(NEG_MAX_ROWS[:, :, :], 0.0)
            for s in range(2):
                e.memset(Q_PACK[s][:, :], 0.0)
                e.memset(K_PACK[s][:, :], 0.0)
                e.memset(V_ONES[s][:, :, :, :], 0.0)
            e.drain()
            for s in range(2):
                e.memset(V_ONES[s][:, :, :, AD:AD + 1], 1.0)
            e.drain().then_inc(S["zeroed"], 1)
            with e.Fori(0, BATCH) as b:
                for k in range(3):
                    e.wait_ge(S["var"], b * 3 + k + 1)
                    e.tensor_tensor(RSTD[:, :], VAR_EPS[:, :], NEG_HALF[:, :], ALU.pow).then_inc(S["rstd"], 1)

        @block.tensor
        def _(e):
            LD = LOADS * 16

            def max_unit(N, s, u):
                qt, a = u // 2, u % 2
                for h in range(2):
                    if u >= 1:
                        e.wait_ge(S["mx_red"], N * 32 + (2 * u + h - 1))
                        e.sem_inc(S["pe_step"], 1)
                    e.matmul(PS_MAX[h][:, :], Q_PACK[s][64 * a:64 * a + 64, P * qt:P * qt + P],
                             K_PACK[s][64 * a:64 * a + 64, 512 * h:512 * h + 512], start=True, stop=True)\
                        .then_inc(S["mx_ps"], 1)

            def m_transposes(N, s):
                e.wait_ge(S["nm"], N + 1)
                e.wait_ge(S["ctx"], N + 1)
                for t in range(TPB):
                    x = e.transpose(PS_TR_BF[:, P * t:P * t + P], NEG_MAX_ROWS[:, t, :], IDENT_BF[:, :])
                x.then_inc(S["mt_ps"], 1)

            def pv(N, s, u):
                c, kp, a = u // 8, (u // 2) % 4, u % 2
                q = 2 * a + c
                e.wait_ge(S["exp"], N * 16 + (u + 1))
                for j in range(2):
                    x = e.matmul(PS_OUT[32 * q:32 * q + 32, :], V_ONES[s][:, 2 * kp + j, a, :],
                                 PROBS_T[a][:, 512 * j:512 * j + 512], start=(kp == 0 and j == 0),
                                 stop=(kp == 3 and j == 1))
                x.then_inc(S["pv_ps"], 1)

            def pair(N, h, s, nxt):
                e.wait_ge(S["qm"], N + 2)
                e.sem_inc(S["pe_step"], 1)
                if nxt:
                    e.wait_ge(S["pack%d" % (1 - s)], (h + 1 + s) * NPACK)
                    e.sem_inc(S["pe_step"], 1)
                e.wait_ge(S["v9"], N + 1)
                e.sem_inc(S["pe_step"], 1)
                for u in range(17):
                    if u < 16:
                        c, kp, a = u // 8, (u // 2) % 4, u % 2
                        if u >= 2:
                            e.wait_ge(S["exp"], N * 16 + (u - 1))
                            e.sem_inc(S["pe_step"], 1)
                        for j in range(2):
                            x = e.matmul(PS_WIDE[a][:, 512 * j:512 * j + 512],
                                         K_PACK[s][64 * a:64 * a + 64, P * (2 * kp + j):P * (2 * kp + j) + P],
                                         Q_WITH_MAX[s][64 * a:64 * a + 64, 512 * c:512 * c + 512], start=True, stop=True)
                        x.then_inc(S["st_ps"], 1)
                        if nxt:
                            max_unit(N + 1, 1 - s, u)
                    if u >= 1:
                        pv(N, s, u - 1)
                if nxt:
                    m_transposes(N + 1, 1 - s)
                    e.wait_ge(S["qm"], N + 3)
                else:
                    e.wait_ge(S["ctx"], N + 2)
                e.wait_ge(S["oe"], N + 1)
                for t in range(4):
                    x = e.transpose(PS_TR[:, P * t:P * t + P], OUT_T[:, P * t:P * t + P], IDENT[:, :])
                x.then_inc(S["ot_ps"], 1)

            e.wait_ge(S["loaded"], LD)
            e.wait_ge(S["sig"], 1)
            with e.Fori(0, BATCH) as b:
                e.wait_ge(S["xn"], b + 1)
                for t in range(TPB):
                    x = e.transpose(PS_WIDE[0][:, P * t:P * t + P], X_NORM[:, t, :], IDENT[:, :])
                x.then_inc(S["xT_ps"], 1)
                e.wait_ge(S["xT_ready"], b + 1)
                for i in range(2):
                    for c in range(2):
                        x = e.matmul(PS_WIDE[i][:, 512 * c:512 * c + 512], WQK[:, i, :], X_NORM_T[:, 512 * c:512 * c + 512],
                                     start=True, stop=True)
                    x.then_inc(S["q_ps"], 1)
                for i, w in enumerate((WQS, WKS)):
                    for c in range(2):
                        if i == 1:
                            e.wait_ge(S["s_ready"], b * 4 + c + 1)
                        e.matmul(PS_MAX[c][0:RANK, :], w[:, :], X_NORM_T[:, 512 * c:512 * c + 512],
                                 start=True, stop=True).then_inc(S["s_ps"], 1)
                for t in range(TPB):
                    if t % 4 == 0:
                        e.wait_ge(S["split"], b * 2 + t // 4 + 1)
                    o = PS_WIDE[t // 4][:, 256 * (t % 4):256 * (t % 4) + 256]
                    e.matmul(o, X_NORM_T[:, P * t:P * t + P], WV2[:, :], start=True, stop=False)
                    x = e.matmul(o, ONES_ROW[:, :], ROWS[:, 0:256], start=False, stop=True)
                    if t % 4 == 3:
                        x.then_inc(S["v_ps"], 1)
                e.wait_ge(S["s_ready"], b * 4 + 4)
                for t in range(TPB):
                    if t < 2:
                        e.wait_ge(S["v_ready"], b * 2 + t + 1)
                    else:
                        e.wait_ge(S["e_ready"], b * TPB + t - 1)
                    e.sem_inc(S["pe_step"], 1)
                    for c in range(2):
                        x = e.matmul(PS_WIDE[t % 2][:, 512 * c:512 * c + 512], SPARSE_Q[:, P * t:P * t + P],
                                     SPARSE_K[:, 512 * c:512 * c + 512], start=True, stop=True)
                    x.then_inc(S["ss_ps"], 1)
                e.wait_ge(S["pack0"], b * (PAIRS_A // 2 * NPACK) + NPACK)
                e.sem_inc(S["pe_step"], 1)
                e.wait_ge(S["e_ready"], b * TPB + TPB)
                e.sem_inc(S["pe_step"], 1)
                for u in range(16):
                    max_unit(b * PAIRS_A, 0, u)
                m_transposes(b * PAIRS_A, 0)
                with e.Fori(0, PAIRS_A // 2 - 1) as gp:
                    for s in range(2):
                        pair(b * PAIRS_A + gp * 2 + s, b * (PAIRS_A // 2) + gp, s, True)
                pair(b * PAIRS_A + (PAIRS_A - 2), b * (PAIRS_A // 2) + (PAIRS_A // 2 - 1), 0, True)
                pair(b * PAIRS_A + (PAIRS_A - 1), b * (PAIRS_A // 2) + (PAIRS_A // 2 - 1), 1, False)
                e.wait_ge(S["ctx"], (b + 1) * PAIRS_A + 2)
                for t in range(TPB):
                    x = e.transpose(PS_WIDE[0][:, P * t:P * t + P], CONTEXT[:, t, :], IDENT[:, :])
                x.then_inc(S["cT_ps"], 1)
                e.wait_ge(S["cT_ready"], b + 1)
                for t in range(TPB):
                    o = PS_WIDE[1][:, P * t:P * t + P]
                    e.matmul(o, CONTEXT_T[:, t, :], WOUT[:, :], start=True, stop=False)
                    x = e.matmul(o, ONES_ROW[:, :], ROWS[:, 2 * P:3 * P], start=False, stop=True)
                x.then_inc(S["dense_ps"], 1)
                for t in range(TPB):
                    e.wait_ge(S["w_ready"], b * TPB + t + 1)
                    for k in range(TPB):
                        x = e.transpose(PS_WIDE[0][:, P * k:P * k + P], KEPT[:, P * k:P * k + P], IDENT[:, :])
                    x.then_inc(S["wT_ps"], 1)
                    e.wait_ge(S["wT_ready"], b * TPB + t + 1)
                    if t >= 1:
                        e.wait_ge(S["r1"], b * TPB + t)
                    for k in range(TPB):
                        x = e.matmul(PS_OUT[:, 0:P], KEPT_T[:, k, :], SPARSE_V[:, k, :], start=(k == 0), stop=(k == TPB - 1))
                    x.then_inc(S["sp_ps"], 1)
                e.wait_ge(S["x1"], b + 1)
                for t in range(TPB):
                    x = e.transpose(PS_WIDE[0][:, P * t:P * t + P], NORM_OUT[:, t, :], IDENT[:, :])
                x.then_inc(S["x1T_ps"], 1)
                e.wait_ge(S["x1T_ready"], b + 1)
                for j in range(4):
                    if j >= 2:
                        e.wait_ge(S["h_ready"], b * 4 + j - 1)
                    for c in range(2):
                        x = e.matmul(PS_WIDE[j % 2][:, 512 * c:512 * c + 512], WF1[:, P * j:P * j + P],
                                     NORM_OUT_T[:, 512 * c:512 * c + 512], start=True, stop=True)
                    x.then_inc(S["h_ps"], 1)
                e.wait_ge(S["h_ready"], b * 4 + 4)
                for t in range(TPB):
                    o = PS_MAX[t // 4][:, P * (t % 4):P * (t % 4) + P]
                    for j in range(4):
                        e.matmul(o, HIDDEN_T[:, j, P * t:P * t + P], WF2[:, j, :], start=(j == 0), stop=False)
                    x = e.matmul(o, ONES_ROW[:, :], ROWS[:, 3 * P:4 * P], start=False, stop=True)
                x.then_inc(S["ff_ps"], 1)

        @block.scalar
        def _(e):
            e.wait_ge(S["loaded"], LOADS * 16)
            e.activation(SIGMOID[:, 0:1], LAM[:, :], ACT.Exp, scale=-1.0).then_inc(S["lam_e"], 1)

            def v9_copy(N, s, p):
                e.activation(V_ONES[s][:, :, :, 0:AD], V_DENSE[:, :, bass.ds(p * 2, 2), :], ACT.Copy).then_inc(S["v9"], 1)

            def exps(N):
                for u in range(16):
                    a = u % 2
                    e.wait_ge(S["st_ps"], N * 16 + (u + 1))
                    e.activation(PROBS_T[a][:, :], PS_WIDE[a][:, :], ACT.Exp, scale=AD ** -0.5).then_inc(S["exp"], 1)

            with e.Fori(0, BATCH) as b:
                e.wait_ge(S["xT_ps"], b + 1)
                e.activation(X_NORM_T[:, :], PS_WIDE[0][:, :], ACT.Copy).then_inc(S["xT_ready"], 1)
                for i, dst in enumerate((SPARSE_Q, SPARSE_K)):
                    for c in range(2):
                        e.wait_ge(S["s_ps"], b * 4 + 2 * i + c + 1)
                        e.activation(dst[:, 512 * c:512 * c + 512], PS_MAX[c][0:RANK, :], ACT.Identity,
                                     bias=COLS[0:RANK, 2 + i:3 + i]).then_inc(S["s_ready"], 1)
                for i in range(2):
                    e.wait_ge(S["v_ps"], b * 2 + i + 1)
                    v = PS_WIDE[i][:, :].rearrange("p (t x) -> p t x", t=4)
                    e.activation(V_DENSE[:, 4 * i:4 * i + 4, :, :].rearrange("p t h d -> p t (h d)"), v[:, :, 0:P], ACT.Copy)
                    e.activation(SPARSE_V[:, 4 * i:4 * i + 4, :], v[:, :, P:2 * P], ACT.Copy)
                    e.drain().then_inc(S["v_ready"], 1)
                for t in range(TPB):
                    e.wait_ge(S["ssm_ready"], b * TPB + t + 1)
                    e.activation(WEIGHTS[:, t, :], PS_WIDE[t % 2][:, :], ACT.Exp, bias=EXP_BIAS[:, t:t + 1], scale=RANK ** -0.5,
                                 accum_out=WEIGHT_SUM[:, t:t + 1]).then_inc(S["e_ready"], 1)
                e.drain()
                for t in range(TPB):
                    x = e.activation(WEIGHTS_HIGH[:, t, :], WEIGHTS[:, t, :].bitcast(BF16).rearrange("p (s h) -> p s h", h=2)[:, :, 1], ACT.Copy)
                x.then_inc(S["e_high"], 1)
                with e.Fori(0, PAIRS_A // 2) as gp:
                    for s in range(2):
                        N = b * PAIRS_A + gp * 2 + s
                        v9_copy(N, s, gp * 2 + s)
                        exps(N)
                e.wait_ge(S["cT_ps"], b + 1)
                e.activation(CONTEXT_T[:, :, :].rearrange("p t d -> p (t d)"), PS_WIDE[0][:, :], ACT.Copy).then_inc(S["cT_ready"], 1)
                for t in range(TPB):
                    e.wait_ge(S["wT_ps"], b * TPB + t + 1)
                    e.activation(KEPT_T[:, :, :].rearrange("p t d -> p (t d)"), PS_WIDE[0][:, :], ACT.Copy)\
                        .then_inc(S["wT_ready"], 1)
                e.wait_ge(S["x1T_ps"], b + 1)
                e.activation(NORM_OUT_T[:, :], PS_WIDE[0][:, :], ACT.Copy).then_inc(S["x1T_ready"], 1)
                for j in range(4):
                    e.wait_ge(S["h_ps"], b * 4 + j + 1)
                    e.activation(HIDDEN_T[:, j, :], PS_WIDE[j % 2][:, :], ACT.Relu, bias=COLS[:, 4 + j:5 + j])\
                        .then_inc(S["h_ready"], 1)

        @block.vector
        def _(e):
            e.wait_ge(S["loaded"], LOADS * 16)
            e.wait_ge(S["lam_e"], 1)
            e.tensor_scalar(SIGMOID[:, 1:2], SIGMOID[:, 0:1], 1.0, None, ALU.add)
            e.drain()
            e.reciprocal(SIGMOID[:, 2:3], SIGMOID[:, 1:2])
            e.drain()
            e.tensor_scalar(SIGMOID[:, 3:4], SIGMOID[:, 2:3], -1.0, 1.0, ALU.mult, ALU.add)
            e.tensor_copy(IDENT_BF[:, :], IDENT[:, :])
            for s in range(2):
                e.tensor_scalar(K_PACK[s][:, :], K_PACK[s][:, :], COLS[:, 8:9], None, ALU.add)
            e.drain().then_inc(S["sig"], 1)
            e.sem_inc(S["ctx"], 2)
            e.sem_inc(S["qm"], 1)

            def layernorm(get, put, nth, b):
                for t in range(TPB):
                    e.bn_stats(STATS[:, t, :], get(t))
                e.drain()
                for t in range(TPB):
                    e.bn_aggr(MEAN_VAR[:, t, :], STATS[:, t, :])
                e.drain()
                e.tensor_scalar(VAR_EPS[:, :], MEAN_VAR[:, :, 1], EPS, None, ALU.add).then_inc(S["var"], 1)
                e.wait_ge(S["rstd"], b * 3 + nth + 1)
                for t in range(TPB):
                    x = e.tensor_scalar(put(t), get(t), MEAN_VAR[:, t, 0:1], RSTD[:, t:t + 1], ALU.subtract, ALU.mult)
                return x

            def maxima(N, s):
                for u in range(16):
                    qt, a = u // 2, u % 2
                    for h in range(2):
                        e.wait_ge(S["mx_ps"], N * 32 + (2 * u + h + 1))
                        e.tensor_reduce(MAX_HALF[:, a, qt, h:h + 1], PS_MAX[h][:, :], AX.X, ALU.max).then_inc(S["mx_red"], 1)
                e.drain()
                e.tensor_reduce(NEG_MAX[:, :, :], MAX_HALF[:, :, :, :], AX.X, ALU.max, negate=True)
                e.drain()
                mt = NEG_MAX_ROWS[:, :, :].rearrange("p t (a r) -> p a t r", a=2)
                for k in range(3):
                    e.tensor_copy(mt[:, :, :, MROW + k], NEG_MAX[:, :, :])
                    e.drain()
                    if k < 2:
                        e.tensor_tensor(NEG_MAX[:, :, :], NEG_MAX[:, :, :], mt[:, :, :, MROW + k], ALU.subtract)
                        e.drain()
                e.drain().then_inc(S["nm"], 1)

            def add_m(N, s):
                e.wait_ge(S["mt_ps"], N + 1)
                e.tensor_tensor(Q_WITH_MAX[s][:, :], Q_PACK[s][:, :], PS_TR_BF, ALU.add).then_inc(S["qm"], 1)

            def context(N, s, p, nxt):
                if nxt:
                    maxima(N + 1, 1 - s)
                e.wait_ge(S["pv_ps"], N * 16 + 16)
                e.tensor_copy(OUT_T[:, :], PS_OUT[:, :]).then_inc(S["oe"], 1)
                if nxt:
                    add_m(N + 1, 1 - s)
                e.wait_ge(S["ot_ps"], N + 1)
                o = PS_TR[:, :].rearrange("p (t a c r) -> p a c t r", t=4, a=2, c=2)
                for a in range(2):
                    e.reciprocal(SUM_INV[:, a, :, :], o[:, a, :, :, AD])
                e.drain()
                for a in range(2):
                    x = e.tensor_tensor(CONTEXT[:, :, bass.ds(p * 16 + 8 * a, AD)].rearrange("p (c t) d -> p c t d", c=2),
                                        o[:, a, :, :, 0:AD], SUM_INV[:, a, :, :].unsqueeze(3).to_broadcast([P, 2, 4, AD]),
                                        ALU.mult)
                e.drain().then_inc(S["ctx"], 1)

            with e.Fori(0, BATCH) as b:
                xt = lambda t: X[:, bass.ds(b * TPB + t, 1), :].rearrange("p a d -> p (a d)")
                layernorm(xt, lambda t: X_NORM[:, t, :], 0, b)
                e.drain().then_inc(S["xn"], 1)
                for i in range(2):
                    e.wait_ge(S["q_ps"], b * 2 + i + 1)
                    e.tensor_scalar(QK_FULL[:, :], PS_WIDE[i][:, :], COLS[:, i:i + 1], None, ALU.add)
                    e.drain()
                    e.tensor_copy(QK_PARTS[:, i, 0, :], QK_FULL[:, :])
                    e.drain()
                    e.tensor_tensor(QK_REST[:, :], QK_FULL[:, :], QK_PARTS[:, i, 0, :], ALU.subtract)
                    e.drain()
                    e.tensor_copy(QK_PARTS[:, i, 1, :], QK_REST[:, :])
                    e.drain()
                    e.tensor_tensor(QK_PARTS[:, i, 2, :], QK_REST[:, :], QK_PARTS[:, i, 1, :], ALU.subtract).then_inc(S["split"], 1)
                for t in range(TPB):
                    e.wait_ge(S["ss_ps"], b * TPB + t + 1)
                    e.tensor_reduce(NEG_SCORE_MAX[:, t:t + 1], PS_WIDE[t % 2][:, :], AX.X, ALU.max, negate=True)
                    e.drain()
                    e.tensor_scalar(EXP_BIAS[:, t:t + 1], NEG_SCORE_MAX[:, t:t + 1], RANK ** -0.5, None, ALU.mult).then_inc(S["ssm_ready"], 1)
                maxima(b * PAIRS_A, 0)
                add_m(b * PAIRS_A, 0)
                with e.Fori(0, PAIRS_A // 2 - 1) as gp:
                    for s in range(2):
                        context(b * PAIRS_A + gp * 2 + s, s, gp * 2 + s, True)
                context(b * PAIRS_A + (PAIRS_A - 2), 0, PAIRS_A - 2, True)
                context(b * PAIRS_A + (PAIRS_A - 1), 1, PAIRS_A - 1, False)
                e.wait_ge(S["e_ready"], b * TPB + TPB)
                e.memset(THRESHOLD[:, :], 0)
                e.memset(BIT[:, :], 1 << 29)
                e.drain()
                def narrow(weights):
                    e.tensor_tensor(CANDIDATE[:, :], THRESHOLD[:, :], BIT[:, :], ALU.bitwise_or)
                    e.drain()
                    for t in range(TPB):
                        e.tensor_scalar(UNUSED_OUT[:, t, :], weights[:, t, :], CANDIDATE[:, t:t + 1].bitcast(F32), 0.0, ALU.is_ge, ALU.add,
                                        accum_out=COUNT[:, t:t + 1])
                    e.drain()
                    e.tensor_scalar(ENOUGH[:, :], COUNT[:, :], float(KEEP), None, ALU.is_ge)
                    e.tensor_scalar(BIT[:, :], BIT[:, :], 1, None, ALU.logical_shift_right)
                    e.drain()
                    e.copy_predicated(THRESHOLD[:, :], ENOUGH[:, :], CANDIDATE[:, :])
                    e.drain()

                e.wait_ge(S["e_high"], b + 1)
                e.sem_inc(S["dve_step"], 1)
                with e.Fori(0, 14):
                    narrow(WEIGHTS_HIGH)
                with e.Fori(0, 16):
                    narrow(WEIGHTS)
                for t in range(TPB):
                    th = THRESHOLD[:, t:t + 1].bitcast(F32)
                    e.tensor_scalar(ABOVE[:, :], WEIGHTS[:, t, :], th, 0.0, ALU.is_gt, ALU.add, accum_out=COUNT[:, t:t + 1])
                    e.tensor_scalar(TIED[:, :], WEIGHTS[:, t, :], th, None, ALU.is_equal)
                    e.drain()
                    e.tensor_scalar(MISSING[:, t:t + 1], COUNT[:, t:t + 1], -1.0, float(KEEP), ALU.mult, ALU.add)
                    e.tensor_tensor_scan(TIE_RANK[:, :], TIED[:, :], TIED[:, :], 0.0, ALU.add, ALU.max)
                    e.drain()
                    e.scalar_tensor_tensor(TIED[:, :], TIE_RANK[:, :], MISSING[:, t:t + 1], TIED[:, :], ALU.is_le, ALU.mult)
                    e.drain()
                    e.tensor_tensor(ABOVE[:, :], ABOVE[:, :], TIED[:, :], ALU.add)
                    e.drain()
                    if t >= 1:
                        e.wait_ge(S["wT_ps"], b * TPB + t)
                    e.scalar_tensor_tensor(KEPT[:, :], WEIGHTS[:, t, :], 1.0, ABOVE[:, :], ALU.mult, ALU.mult,
                                           accum_out=KEPT_SUM[:, t:t + 1]).then_inc(S["w_ready"], 1)
                    e.drain()
                    e.scalar_tensor_tensor(DENOM[:, t:t + 1], WEIGHT_SUM[:, t:t + 1], 1e-9, KEPT_SUM[:, t:t + 1], ALU.mult, ALU.add)
                    e.drain()
                    e.reciprocal(DENOM_INV[:, t:t + 1], DENOM[:, t:t + 1])
                    e.drain()
                    e.wait_ge(S["sp_ps"], b * TPB + t + 1)
                    e.tensor_scalar(MIXED[:, t, :], PS_OUT[:, 0:P], DENOM_INV[:, t:t + 1], SIGMOID[:, 3:4], ALU.mult, ALU.mult)\
                        .then_inc(S["r1"], 1)
                e.drain()
                e.wait_ge(S["dense_ps"], b + 1)
                sp = MIXED[:, :, :].rearrange("p t d -> p (t d)")
                e.scalar_tensor_tensor(sp, PS_WIDE[1][:, :], SIGMOID[:, 2:3], sp, ALU.mult, ALU.add)
                e.drain()
                e.tensor_tensor(MIXED[:, :, :], MIXED[:, :, :], X_NORM[:, :, :], ALU.add)
                e.drain()

                def affine(i):
                    e.drain()
                    e.tensor_tensor(NORM_OUT[:, :, :], NORM_OUT[:, :, :], LN_GB[:, i, :].unsqueeze(1).to_broadcast([P, TPB, P]), ALU.mult)
                    e.drain()
                    return e.tensor_tensor(NORM_OUT[:, :, :], NORM_OUT[:, :, :], LN_GB[:, i + 1, :].unsqueeze(1).to_broadcast([P, TPB, P]),
                                           ALU.add)

                layernorm(lambda t: MIXED[:, t, :], lambda t: NORM_OUT[:, t, :], 1, b)
                affine(0).then_inc(S["x1"], 1)
                e.wait_ge(S["ff_ps"], b + 1)
                for i in range(2):
                    x = e.tensor_tensor(MIXED[:, 4 * i:4 * i + 4, :].rearrange("p t d -> p (t d)"),
                                        NORM_OUT[:, 4 * i:4 * i + 4, :].rearrange("p t d -> p (t d)"), PS_MAX[i][:, :], ALU.add)
                e.drain()
                layernorm(lambda t: MIXED[:, t, :], lambda t: NORM_OUT[:, t, :], 2, b)
                affine(2)
                e.drain()
                xb = X[:, bass.ds(b * TPB, TPB), :]
                e.tensor_tensor(xb, xb, NORM_OUT[:, :, :], ALU.add)
                e.drain()
            e.drain().then_inc(S["xout"], 1)


def encoder_inputs(f):
    t = lambda n: np.ascontiguousarray(f(n).T)
    w = f('L0_attn_in_proj_w')
    b = f('L0_attn_in_proj_b')
    cols = np.zeros((P, 9), np.float32)
    cols[:, 0], cols[:, 1] = b[0:P], b[P:2 * P]
    cols[:RANK, 2], cols[:RANK, 3] = f('L0_attn_Qp_b'), f('L0_attn_Kp_b')
    cols[:, 4:8] = f('L0_attn_ff1_b').reshape(4, P).T
    rows = np.concatenate([b[2 * P:], f('L0_attn_Vp_b'), f('L0_attn_out_proj_b'), f('L0_attn_ff2_b'),
                           f('L0_attn_ln1_g'), f('L0_attn_ln1_b'), f('L0_attn_ln2_g'), f('L0_attn_ln2_b')])[None]
    for a in range(2):
        cols[64 * a + MROW:64 * a + MROW + 3, 8] = 1
    return dict(
        wqk=np.ascontiguousarray(w[:2 * P].reshape(2, P, P).transpose(2, 0, 1)), wqs=t('L0_attn_Qp_w'), wks=t('L0_attn_Kp_w'),
        wv2=np.ascontiguousarray(np.concatenate([w[2 * P:], f('L0_attn_Vp_w')], 0).T), wout=t('L0_attn_out_proj_w'),
        wf1=t('L0_attn_ff1_w'), wf2=np.ascontiguousarray(f('L0_attn_ff2_w').T.reshape(4, P, P).transpose(1, 0, 2)),
        rows=np.ascontiguousarray(rows), cols=cols, lam=np.ascontiguousarray(f('L0_attn_lam').reshape(1, 1)))


def stage_b(nc, X, wqkv, wo, w1, w2, b1, b2, lngb, scales, rope, mask, ident, shift, edge, out):
    ctx = ExitStack()
    with ctx:
        def sb(name, shape, dt=F32):
            return ctx.enter_context(nc.sbuf_tensor("b_" + name, shape, dt))

        def pb(name, shape, dt=F32):
            return ctx.enter_context(nc.psum_tensor("b_" + name, shape, dt))

        def sem(name):
            return ctx.enter_context(nc.semaphore("b_" + name))

        H = sb("H", [P, TILES, P])
        IDENT = sb("IDENT", [P, P])
        SHIFT = sb("SHIFT", [P, P])
        EDGE = sb("EDGE", [P, P])
        IDENT_BF = sb("IDENT_BF", [P, P], BF16)
        MASK = sb("MASK", [P, 2, 512], BF16)
        Wqkv = sb("Wqkv", [P, 3 * INNER])
        Wo = sb("Wo", [P, PAIRS, P])
        W_UP = sb("W_UP", [P, 2 * FF])
        W_DOWN = sb("W_DOWN", [P, 3, P])
        B_UP = sb("B_UP", [P, 2, 3])
        LN_GB = sb("LN_GB", [P, 2])
        SCALES = sb("SCALES", [P, 4, DH])
        ROPE_BASE = sb("ROPE_BASE", [P, 4, TPB, DH])
        ROPE = sb("ROPE", [P, 4, TPB, DH])
        TILE = [sb(f"TILE{i}", [P, P]) for i in range(2)]
        MID = [sb(f"MID{i}", [P, P]) for i in range(2)]
        TILE_T = [sb(f"TILE_T{i}", [P, WIN + P]) for i in range(2)]
        SQUARES = sb("SQUARES", [P, 2, INNER])
        SQUARE_SUM = sb("SQUARE_SUM", [P, 2, HEADS])
        INV_NORM = sb("INV_NORM", [P, 2, HEADS])
        NHALF = sb("NHALF", [P, HEADS])
        TURN_COS = sb("TURN_COS", [P, 2, INNER])
        TURN_SIN = sb("TURN_SIN", [P, 2, INNER])
        UNIT_QK = sb("UNIT_QK", [P, 2, INNER])
        Q_T = [sb(f"Q_T{i}", [P, PAIRS, P]) for i in range(2)]
        K_T = [sb(f"K_T{i}", [P, PAIRS, WIN + P]) for i in range(2)]
        V_WINDOWS = [sb(f"V_WINDOWS{i}", [P, NWIN, 512]) for i in range(2)]
        ROW_MAX = sb("ROW_MAX", [P, HEADS])
        SHIFTED = sb("SHIFTED", [P, PAIRS, 2, SPAN])
        PROBS = sb("PROBS", [P, PAIRS, 2, SPAN])
        ROW_SUM = sb("ROW_SUM", [P, HEADS])
        SUM_INV = sb("SUM_INV", [P, HEADS])
        PROBS_T = sb("PROBS_T", [P, PAIRS, P])
        ATT_OUT = sb("ATT_OUT", [P, PAIRS, 2, DH])
        ATT_OUT_T = sb("ATT_OUT_T", [P, PAIRS, P])
        JOINED = sb("JOINED", [P, P])
        STATS = sb("STATS", [P, 6])
        MEAN_VAR = sb("MEAN_VAR", [P, 2])
        VAR_EPS = sb("VAR_EPS", [P, 1])
        RSTD = sb("RSTD", [P, 1])
        NORMED = sb("NORMED", [P, P])
        NORMED_T = sb("NORMED_T", [P, P])
        GATE = sb("GATE", [P, 3, P])
        HIDDEN_T = sb("HIDDEN_T", [P, 3, P])
        LN0_STATS = sb("LN0_STATS", [P, TILES, 6])
        LN0_MEAN_VAR = sb("LN0_MEAN_VAR", [P, TILES, 2])
        LN0_VAR_EPS = sb("LN0_VAR_EPS", [P, TILES])
        LN0_RSTD = sb("LN0_RSTD", [P, TILES])
        LN0_NHALF = sb("LN0_NHALF", [P, TILES])

        PS_ATT = pb("PS_ATT", [P, 1024])
        PS_QK = pb("PS_QK", [P, 1024])
        PS_MIX = [pb(f"PS_MIX{i}", [P, 512]) for i in range(2)]
        PS_TR = [pb(f"PS_TR{i}", [P, 512]) for i in range(2)]

        names = """loaded consts ln0_var ln0_rstd ln0_done hs_ready xsT_ps xsT_ready qk_ps v_ps v_ready sq_ready
            ss_ready rn_ready rope_ready tr_ps qkT_ready s_ps sub_ready p_ready pt_ps pt_ready o_ps o_ready
            ot_ps ot_ready wo_ps hm_ready shift_ps var_ready rstd_ready xn_ready xnT_ps xnT_ready hg_ps
            gelu_ready hp_ready ff_ps h_ready out_ready stored pe_step pool_step dve_step zeroed sc_load
            q_load kv_load a_load n_load rl_done hm_zeroed turned""".split()
        S = {n: sem(n) for n in names}

        def wait(e, name, value):
            if not isinstance(value, int) or value > 0:
                e.wait_ge(S[name], value)

        def pe_enter(e, TF, sf, first_f):
            wait(e, "hs_ready", TF + 1)
            e.matmul(PS_MIX[1][0:64, 3 * P:], TILE[sf][:, 0:64], IDENT[:, :], start=True, stop=True)
            x = e.matmul(PS_MIX[1][64:128, 3 * P:], TILE[sf][:, 64:128], SHIFT[:, :], start=True, stop=first_f)
            if not first_f:
                x = e.matmul(PS_MIX[1][64:128, 3 * P:], TILE[1 - sf][:, 64:128], EDGE[:, :], start=False, stop=True)
            x.then_inc(S["xsT_ps"], 1)

        def project(e, TF, sf, i):
            if i == 0:
                wait(e, "xsT_ready", TF + 1)
                wait(e, "turned", 2 * TF)
            else:
                wait(e, "turned", 2 * TF + 1)
            for j in range(2):
                col = (2 * i + j) * 512
                x = e.matmul(PS_QK[:, 512 * j:512 * j + 512], TILE_T[sf][:, WIN:], Wqkv[:, col:col + 512],
                             start=True, stop=True)
            x.then_inc(S["qk_ps"], 1)

        def pe_round(e, T, s, n=True, a=True, f=True, first_a=False, first_next=False):
            TA, TF, sa, sf = T + 1, T + 2, 1 - s, s

            def qk():
                wait(e, "ot_ready", 2 * TA)
                wait(e, "qkT_ready", 4 * TA + 4)
                e.sem_inc(S["pe_step"], 1)
                for h in range(2):
                    e.matmul(PS_ATT[:, 512 * h:512 * h + 512], IDENT_BF[:, :], MASK[:, 0 if first_a else 1, :],
                             start=True, stop=False, skip_group_check=True)
                for p in range(PAIRS):
                    for h in range(2):
                        for w in range(NWIN):
                            x = e.matmul(PS_ATT[WIN * w:WIN * w + WIN, 512 * h + SPAN * p:512 * h + SPAN * p + SPAN],
                                         Q_T[sa][64 * h:64 * h + 64, p, WIN * w:WIN * w + WIN],
                                         K_T[sa][64 * h:64 * h + 64, p, WIN * w:WIN * w + SPAN],
                                         start=False, stop=True, skip_group_check=True)
                x.then_inc(S["s_ps"], 1)

            def shift_mid():
                wait(e, "hm_ready", T + 1)
                wait(e, "qkT_ready", 4 * TA + 4)
                e.matmul(PS_TR[0][:, 0:64], SHIFT[:, :], MID[s][:, 64:128], start=True, stop=False)
                e.matmul(PS_TR[0][:, 0:64], EDGE[:, :], MID[1 - s][:, 64:128], start=False, stop=True)\
                    .then_inc(S["shift_ps"], 1)

            def values(w):
                if w == 0:
                    wait(e, "h_ready", T + 1)
                if w == 1:
                    wait(e, "xsT_ready", TF + 1)
                    wait(e, "hm_ready", TA)
                if w >= 2:
                    wait(e, "v_ready", TF * NWIN + (w - 1))
                for h in range(2):
                    x = e.matmul(PS_MIX[w % 2][64 * h:64 * h + 64, :], TILE_T[sf][:, WIN * w:WIN * w + SPAN],
                                 Wqkv[:, 2 * INNER + 512 * h:2 * INNER + 512 * h + 512], start=True, stop=True)
                x.then_inc(S["v_ps"], 1)

            def p_transposes():
                wait(e, "p_ready", TA + 1)
                if n:
                    wait(e, "var_ready", T + 1)
                for hb in range(2):
                    for j in range(4):
                        x = e.transpose(PS_TR[hb][:, P * j:P * j + P],
                                        PROBS[:, 4 * hb + j, :, :].rearrange("p a k -> p (a k)"), IDENT[:, :])
                    x.then_inc(S["pt_ps"], 1)

            def pv():
                wait(e, "v_ready", TA * NWIN + NWIN)
                for hb in range(2):
                    wait(e, "pt_ready", 2 * TA + (hb + 1))
                    e.sem_inc(S["pe_step"], 1)
                    for p in range(4 * hb, 4 * hb + 4):
                        for h in range(2):
                            for w in range(NWIN):
                                x = e.matmul(PS_ATT[WIN * w:WIN * w + WIN, 512 * h + DH * p:512 * h + DH * p + DH],
                                             PROBS_T[64 * h:64 * h + 64, p, WIN * w:WIN * w + WIN],
                                             V_WINDOWS[sa][64 * h:64 * h + 64, w, DH * p:DH * p + DH],
                                             start=True, stop=True)
                x.then_inc(S["o_ps"], 1)

            def o_transposes():
                wait(e, "o_ready", TA + 1)
                for hb in range(2):
                    for j in range(4):
                        x = e.transpose(PS_ATT[:, 512 * hb + P * j:512 * hb + P * j + P],
                                        ATT_OUT[:, 4 * hb + j, :, :].rearrange("p a k -> p (a k)"), IDENT[:, :])
                    x.then_inc(S["ot_ps"], 1)

            def qk_transposes(i):
                wait(e, "rope_ready", 2 * TF + (i + 1))
                for hb in range(2):
                    if i == 0 and a:
                        wait(e, "pt_ready", 2 * TA + (hb + 1))
                    if i == 1:
                        wait(e, "qkT_ready", 4 * TF + (hb + 1))
                    for j in range(4):
                        c = (4 * hb + j) * P
                        x = e.transpose(PS_TR[hb][:, P * j:P * j + P], UNIT_QK[:, i, c:c + P], IDENT[:, :])
                    x.then_inc(S["tr_ps"], 1)

            def xn_transpose():
                wait(e, "xn_ready", T + 1)
                wait(e, "v_ready", TF * NWIN + 3)
                e.transpose(PS_MIX[0][:, 3 * P:], NORMED[:, :], IDENT[:, :]).then_inc(S["xnT_ps"], 1)

            def ff_up():
                wait(e, "xnT_ready", T + 1)
                wait(e, "v_ready", TF * NWIN + NWIN)
                for i in (1, 0):
                    for j, (c, m) in enumerate(FFC):
                        x = e.matmul(PS_MIX[i][0:m, P * j:P * j + P], W_UP[:, FF * i + c:FF * i + c + m], NORMED_T[:, :],
                                     start=True, stop=True)
                    x.then_inc(S["hg_ps"], 1)

            def out_project():
                wait(e, "v_ready", TF * NWIN + NWIN)
                for hb in range(2):
                    wait(e, "ot_ready", 2 * TA + (hb + 1))
                    for j in range(4 * hb, 4 * hb + 4):
                        x = e.matmul(PS_MIX[1][:, 0:P], ATT_OUT_T[:, j, :], Wo[:, j, :], start=(j == 0), stop=(j == 7))
                x.then_inc(S["wo_ps"], 1)

            def ff_down():
                wait(e, "hp_ready", T + 1)
                for j in range(3):
                    x = e.matmul(PS_MIX[0][:, 0:P], HIDDEN_T[:, j, :], W_DOWN[:, j, :], start=(j == 0), stop=(j == 2))
                x.then_inc(S["ff_ps"], 1)

            if f:
                values(0)
            if a:
                qk()
            if n:
                shift_mid()
            if f:
                for w in range(1, NWIN):
                    values(w)
                project(e, TF, sf, 1)
            if n:
                xn_transpose()
            if a:
                p_transposes()
            if n:
                ff_up()
            if a:
                pv()
            if n:
                wait(e, "gelu_ready", 3 * T + 3)
            pe_enter(e, TF + 1, 1 - sf, first_next)
            if f:
                qk_transposes(0)
            project(e, TF + 1, 1 - sf, 0)
            if n:
                ff_down()
            if a:
                o_transposes()
            if f:
                qk_transposes(1)
            if a:
                out_project()

        quads = lambda t: t.rearrange("p (j t) -> p j t", t=P)

        def act_enter(e, TF, sf, tile):
            wait(e, "xsT_ps", TF)
            e.activation(TILE[sf][:, :], H[:, tile, :].rearrange("p a d -> p (a d)"), ACT.Copy)\
                .then_inc(S["hs_ready"], 1)
            e.activation(TILE_T[sf][:, 0:WIN], TILE_T[1 - sf][:, P:P + WIN], ACT.Copy)
            wait(e, "xsT_ps", TF + 1)
            e.activation(TILE_T[sf][:, WIN:], PS_MIX[1][:, 3 * P:], ACT.Copy)
            e.drain().then_inc(S["xsT_ready"], 1)

        def square(e, TF, i):
            wait(e, "qk_ps", 2 * TF + (i + 1))
            e.activation(SQUARES[:, i, :], PS_QK[:, :], ACT.Square).then_inc(S["sq_ready"], 1)

        def act_round(e, T, s, tile_next, n=True, a=True, f=True, first_f=False):
            TA, TF, sa, sf = T + 1, T + 2, 1 - s, s

            def copy_v(w):
                wait(e, "v_ps", NWIN * TF + (w + 1))
                e.activation(V_WINDOWS[sf][:, w, :], PS_MIX[w % 2][:, :], ACT.Copy).then_inc(S["v_ready"], 1)

            def copy_qk(i):
                for hb in range(2):
                    wait(e, "tr_ps", 4 * TF + (2 * i + hb + 1))
                    dst = Q_T[sf][:, 4 * hb:4 * hb + 4, :] if i == 0 else K_T[sf][:, 4 * hb:4 * hb + 4, WIN:]
                    e.activation(dst, quads(PS_TR[hb][:, :]), ACT.Copy).then_inc(S["qkT_ready"], 1)

            if f:
                copy_v(0)
                copy_v(1)
            if a:
                wait(e, "sub_ready", TA + 1)
                e.activation(PROBS[:, :, :, :], SHIFTED[:, :, :, :], ACT.Exp, scale=QK_SCALE).then_inc(S["p_ready"], 1)
            if f:
                copy_v(2)
                copy_v(3)
                if first_f:
                    e.memzero(K_T[sf][:, :, 0:WIN])
                else:
                    e.activation(K_T[sf][:, :, 0:WIN], K_T[1 - sf][:, :, P:P + WIN], ACT.Copy)
            if f:
                square(e, TF, 1)
            if a:
                for hb in range(2):
                    wait(e, "pt_ps", 2 * TA + (hb + 1))
                    e.activation(PROBS_T[:, 4 * hb:4 * hb + 4, :], quads(PS_TR[hb][:, :]), ACT.Copy).then_inc(S["pt_ready"], 1)
            if n:
                wait(e, "hg_ps", 2 * T + 1)
                for j, (c, m) in enumerate(FFC):
                    e.activation(GATE[0:m, j, :], PS_MIX[1][0:m, P * j:P * j + P], ACT.Gelu, bias=B_UP[0:m, 1, j:j + 1])\
                        .then_inc(S["gelu_ready"], 1)
            act_enter(e, TF + 1, 1 - sf, tile_next)
            if f:
                copy_qk(0)
            square(e, TF + 1, 0)
            if a:
                for hb in range(2):
                    wait(e, "ot_ps", 2 * TA + (hb + 1))
                    e.activation(ATT_OUT_T[:, 4 * hb:4 * hb + 4, :], quads(PS_ATT[:, 512 * hb:512 * hb + 512]), ACT.Copy)\
                        .then_inc(S["ot_ready"], 1)
            if f:
                copy_qk(1)

        def turn(e, TF, i, tp, between=None):
            v = PS_QK[:, :].rearrange("p (h d) -> p h d", d=DH)
            t1 = TURN_COS[:, i, :].rearrange("p (h d) -> p h d", d=DH)
            t2 = TURN_SIN[:, i, :].rearrange("p (h d) -> p h d", d=DH)
            wait(e, "sq_ready", 2 * TF + (i + 1))
            e.tensor_reduce(SQUARE_SUM[:, i, :], SQUARES[:, i, :].rearrange("p (h d) -> p h d", d=DH), AX.X, ALU.add)\
                .then_inc(S["ss_ready"], 1)
            e.tensor_tensor(t1, v, ROPE[:, 2 * i, tp, :].to_broadcast([P, HEADS, DH]), ALU.mult)
            if between:
                between()
            for hf in range(2):
                sn = ROPE[:, 2 * i + 1, tp, WIN * hf:WIN * hf + WIN].to_broadcast([P, HEADS, WIN])
                x = e.tensor_tensor(t2[:, :, WIN * hf:WIN * hf + WIN],
                                    v[:, :, WIN * (1 - hf):WIN * (1 - hf) + WIN], sn, ALU.mult)
            x.then_inc(S["turned"], 1)

        def add_turned(e, i):
            e.drain()
            e.tensor_tensor(TURN_COS[:, i, :], TURN_COS[:, i, :], TURN_SIN[:, i, :], ALU.add)

        def dve_round(e, T, s, tp, tp_next, tile, tile_a, new_q=None, n=True, a=True, f=True):
            TA, TF, sa, sf = T + 1, T + 2, 1 - s, s

            def xn():
                wait(e, "rstd_ready", T + 1)
                e.tensor_scalar(NORMED[:, :], JOINED[:, :], MEAN_VAR[:, 0:1], RSTD[:, :], ALU.subtract, ALU.mult)\
                    .then_inc(S["xn_ready"], 1)

            def normed(i):
                e.drain()
                wait(e, "rn_ready", 2 * TF + (i + 1))
                e.tensor_tensor(UNIT_QK[:, i, :].rearrange("p (h d) -> p h d", d=DH),
                                TURN_COS[:, i, :].rearrange("p (h d) -> p h d", d=DH),
                                INV_NORM[:, i, :].unsqueeze(2).to_broadcast([P, HEADS, DH]), ALU.mult)\
                    .then_inc(S["rope_ready"], 1)

            if n:
                wait(e, "shift_ps", T + 1)
                e.tensor_copy(JOINED[:, 0:64], MID[s][:, 0:64])
                e.tensor_copy(JOINED[:, 64:128], PS_TR[0][:, 0:64])
                e.drain()
                e.bn_stats(STATS[:, :], JOINED[:, :])
                e.drain()
                e.bn_aggr(MEAN_VAR[:, :], STATS[:, :])
                e.drain()
                e.tensor_scalar(VAR_EPS[:, :], MEAN_VAR[:, 1:2], EPS, None, ALU.add).then_inc(S["var_ready"], 1)
            if a:
                wait(e, "s_ps", TA + 1)
                e.tensor_reduce(ROW_MAX[:, :], PS_ATT[:, :].rearrange("p (h k) -> p h k", k=SPAN), AX.X, ALU.max)
                e.drain()
                e.tensor_tensor(SHIFTED[:, :, :, :].rearrange("p j a k -> p a j k"),
                                PS_ATT[:, :].rearrange("p (a j k) -> p a j k", a=2, k=SPAN),
                                ROW_MAX[:, :].rearrange("p (a j) -> p a j", a=2).unsqueeze(3)
                                .to_broadcast([P, 2, PAIRS, SPAN]),
                                ALU.subtract).then_inc(S["sub_ready"], 1)
            if n:
                xn()
            if f:
                normed(0)
            if n:
                wait(e, "xnT_ps", T + 1)
                e.tensor_scalar(NORMED_T[:, :], PS_MIX[0][:, 3 * P:], LN_GB[:, 0:1], LN_GB[:, 1:2], ALU.mult, ALU.add)\
                    .then_inc(S["xnT_ready"], 1)
            if a:
                wait(e, "p_ready", TA + 1)
                e.tensor_reduce(ROW_SUM[:, :], PROBS[:, :, :, :].rearrange("p j a k -> p (j a) k"), AX.X, ALU.add)
                e.drain()
                e.reciprocal(SUM_INV[:, :], ROW_SUM[:, :])
            if f:
                turn(e, TF, 1, tp)
            if n:
                for j, (c, m) in enumerate(FFC):
                    wait(e, "gelu_ready", 3 * T + (j + 1))
                    if j == 0:
                        wait(e, "hg_ps", 2 * T + 2)
                    x = e.scalar_tensor_tensor(HIDDEN_T[0:m, j, :], PS_MIX[0][0:m, P * j:P * j + P], B_UP[0:m, 0, j:j + 1],
                                               GATE[0:m, j, :], ALU.add, ALU.mult)
                x.then_inc(S["hp_ready"], 1)
            if f:
                add_turned(e, 1)
            if a:
                e.drain()
                wait(e, "o_ps", TA + 1)
                e.tensor_tensor(ATT_OUT[:, :, :, :].rearrange("p j a k -> p a j k"),
                                PS_ATT[:, :].rearrange("p (a j k) -> p a j k", a=2, k=DH),
                                SUM_INV[:, :].rearrange("p (j a) -> p a j", a=2).unsqueeze(3)
                                .to_broadcast([P, 2, PAIRS, DH]),
                                ALU.mult).then_inc(S["o_ready"], 1)
            if f:
                normed(1)
            if n:
                wait(e, "ff_ps", T + 1)
                e.tensor_tensor(H[:, tile, :].rearrange("p a d -> p (a d)"), MID[s][:, :], PS_MIX[0][:, 0:P], ALU.add)\
                    .then_inc(S["h_ready"], 1)
            if new_q:
                new_q()

            def residual():
                wait(e, "wo_ps", TA + 1)
                e.tensor_tensor(MID[sa][:, :], H[:, tile_a, :].rearrange("p a d -> p (a d)"), PS_MIX[1][:, 0:P],
                                ALU.add).then_inc(S["hm_ready"], 1)

            turn(e, TF + 1, 0, tp_next, residual if a else None)
            add_turned(e, 0)

        def pool_round(e, T, n=True, f=True):
            TF = T + 2

            def norms(i):
                wait(e, "ss_ready", 2 * TF + (i + 1))
                e.sem_inc(S["pool_step"], 1)
                e.tensor_scalar(SQUARE_SUM[:, i, :], SQUARE_SUM[:, i, :], 1e-24, None, ALU.max)
                e.drain()
                e.tensor_tensor(INV_NORM[:, i, :], SQUARE_SUM[:, i, :], NHALF[:, :], ALU.pow).then_inc(S["rn_ready"], 1)

            if n:
                wait(e, "var_ready", T + 1)
                e.tensor_tensor(RSTD[:, :], VAR_EPS[:, :], NHALF[:, 0:1], ALU.pow).then_inc(S["rstd_ready"], 1)
            if f:
                norms(0)
                norms(1)

        HALF = TPB // 2
        block = ctx.enter_context(nc.Block())

        @block.sync
        def _(e):
            for dst, s_ in ((IDENT[:, :], ident), (SHIFT[:, :], shift), (EDGE[:, :], edge),
                            (TURN_COS[:, :, :].rearrange("p i (v x) -> p (i v) x", v=2)[:, 0:2, :], mask),
                            (ROPE_BASE[:, :, :, :], rope)):
                e.dma_start(dst, s_).then_inc(S["consts"], 16)
            e.wait_ge(S["zeroed"], 1)

            def load(L, ly):
                if L is not None:
                    e.wait_ge(S["rl_done"], L * BATCH + BATCH)
                e.dma_start(SCALES[:, :, :].rearrange("p a d -> p (a d)"),
                            scales[ly, :].to_broadcast([P, 4 * DH])).then_inc(S["sc_load"], 16)
                if L is not None:
                    e.wait_ge(S["qk_ps"], L * (2 * TILES) + (2 * TILES - 1))
                e.dma_start(Wqkv[:, 0:INNER], wqkv[ly].squeeze(0)[:, 0:INNER]).then_inc(S["q_load"], 16)
                if L is not None:
                    e.wait_ge(S["qk_ps"], (L + 1) * (2 * TILES))
                e.dma_start(Wqkv[:, INNER:], wqkv[ly].squeeze(0)[:, INNER:]).then_inc(S["kv_load"], 16)
                if L is not None:
                    e.wait_ge(S["wo_ps"], (L + 1) * TILES)
                e.dma_start(Wo[:, :, :], wo[ly].squeeze(0).rearrange("(j p) n -> p j n", p=P)).then_inc(S["a_load"], 16)
                if L is not None:
                    e.wait_ge(S["h_ready"], (L + 1) * TILES + 1)
                w2l = w2[ly].squeeze(0)
                for dst, s_ in ((W_UP[:, :], w1[ly].squeeze(0)),
                                (W_DOWN[:, 0:2, :], w2l[0:2 * P, :].rearrange("(j p) n -> p j n", p=P)),
                                (W_DOWN[0:FF - 2 * P, 2, :], w2l[2 * P:FF, :]),
                                (B_UP[:, :, :], b1[ly].squeeze(0)), (W_DOWN[FF - 2 * P:FF - 2 * P + 1, 2, :], b2[ly, :]),
                                (LN_GB[:, :], lngb[ly].squeeze(0))):
                    e.dma_start(dst, s_).then_inc(S["n_load"], 16)

            def load_ahead(L):
                e.wait_ge(S["rl_done"], L * BATCH + BATCH)
                for name in ("sc_load", "q_load", "kv_load", "a_load"):
                    e.sem_inc(S[name], 16)

            load(None, slice(0, 1))
            with e.Fori(0, DEPTH - 1) as L:
                load(L, bass.ds(L + 1, 1))
            load_ahead(DEPTH - 1)
            e.wait_ge(S["out_ready"], 1)
            e.dma_start(out.rearrange("b (t p) d -> p (b t) d", p=P), X[:, :, :]).then_inc(S["stored"], 16)
            e.wait_ge(S["stored"], 16)

        N_LOADS = 6 * 16

        def loads_for_next(B):
            return ((B + 1) // BATCH + 1) * 16

        @block.gpsimd
        def _(e):
            e.memset(NHALF[:, :], -0.5)
            e.memset(LN0_NHALF[:, :], -0.5)
            e.memset(W_DOWN[:, :, :], 0.0)
            e.memset(HIDDEN_T[:, :, :], 1.0)
            for t in (*K_T, *TILE_T, *TILE, *MID):
                e.memset(t[:], 0.0)
            e.drain().then_inc(S["zeroed"], 1)
            e.wait_ge(S["ln0_var"], 1)
            e.tensor_tensor(LN0_RSTD[:, :], LN0_VAR_EPS[:, :], LN0_NHALF[:, :], ALU.pow).then_inc(S["ln0_rstd"], 1)
            pool_round(e, -2, n=False)
            pool_round(e, -1, n=False)
            with e.Fori(0, DEPTH * BATCH) as B:
                with e.Fori(0, HALF) as g:
                    for s in range(2):
                        pool_round(e, B * TPB + g * 2 + s)

        @block.scalar
        def _(e):
            e.wait_ge(S["ln0_done"], 1)
            act_enter(e, 0, 0, slice(0, 1))
            square(e, 0, 0)
            act_round(e, -2, 0, slice(1, 2), n=False, a=False, first_f=True)
            act_round(e, -1, 1, slice(2, 3), n=False)
            with e.Fori(0, DEPTH * BATCH) as B:
                with e.Fori(0, HALF - 1) as g:
                    for s in range(2):
                        act_round(e, B * TPB + g * 2 + s, s, bass.ds((B * TPB + g * 2 + (s + 3)) % TILES, 1))
                for s in range(2):
                    act_round(e, B * TPB + (TPB - 2 + s), s, bass.ds(((B + 1) % BATCH) * TPB + (s + 1), 1),
                              first_f=(s == 0))

        @block.vector
        def _(e):
            e.wait_ge(S["zeroed"], 1)
            for t in range(TILES):
                e.bn_stats(LN0_STATS[:, t, :], X[:, t, :])
            e.drain()
            for t in range(TILES):
                e.bn_aggr(LN0_MEAN_VAR[:, t, :], LN0_STATS[:, t, :])
            e.drain()
            e.tensor_scalar(LN0_VAR_EPS[:, :], LN0_MEAN_VAR[:, :, 1], EPS, None, ALU.add).then_inc(S["ln0_var"], 1)
            e.wait_ge(S["ln0_rstd"], 1)
            for t in range(TILES):
                e.tensor_scalar(H[:, t, :], X[:, t, :], LN0_MEAN_VAR[:, t, 0:1], LN0_RSTD[:, t:t + 1], ALU.subtract, ALU.mult)
            e.drain().then_inc(S["ln0_done"], 1)
            e.wait_ge(S["consts"], 16 * 5)
            e.tensor_copy(MASK[:, :, :], TURN_COS[:, :, :].rearrange("p i (v x) -> p (i v) x", v=2)[:, 0:2, :])
            e.tensor_copy(IDENT_BF[:, :], IDENT[:, :])
            e.drain().then_inc(S["h_ready"], 1)

            def tables(i):
                for k in (2 * i, 2 * i + 1):
                    e.tensor_tensor(ROPE[:, k, :, :], ROPE_BASE[:, k, :, :],
                                    SCALES[:, k, :].unsqueeze(1).to_broadcast([P, TPB, DH]), ALU.mult)
                x = e.drain()
                if i == 1:
                    x.then_inc(S["rl_done"], 1)

            e.wait_ge(S["sc_load"], 16)
            tables(0)
            tables(1)
            turn(e, 0, 0, slice(0, 1))
            add_turned(e, 0)
            dve_round(e, -2, 0, slice(0, 1), slice(1, 2), None, None, n=False, a=False)
            dve_round(e, -1, 1, slice(1, 2), slice(2, 3), None, slice(0, 1), n=False)
            with e.Fori(0, DEPTH * BATCH) as B:
                def tile(k):
                    return bass.ds((B * TPB + k) % TILES, 1)

                def new_q():
                    e.drain()
                    e.wait_ge(S["sc_load"], loads_for_next(B))
                    tables(0)

                e.drain()
                e.memset(MID[1][:, :], 0.0).then_inc(S["hm_zeroed"], 1)
                e.drain()
                e.wait_ge(S["n_load"], (B // BATCH + 1) * N_LOADS)
                e.sem_inc(S["dve_step"], 1)
                with e.Fori(0, HALF - 2) as g:
                    for s in range(2):
                        dve_round(e, B * TPB + g * 2 + s, s, bass.ds(g * 2 + (s + 2), 1), bass.ds(g * 2 + (s + 3), 1),
                                  tile(g * 2 + s), tile(g * 2 + (s + 1)))
                dve_round(e, B * TPB + (TPB - 4), 0, slice(TPB - 2, TPB - 1), slice(TPB - 1, TPB),
                          tile(TPB - 4), tile(TPB - 3))
                dve_round(e, B * TPB + (TPB - 3), 1, slice(TPB - 1, TPB), slice(0, 1),
                          tile(TPB - 3), tile(TPB - 2), new_q)
                e.drain()
                tables(1)
                for s in range(2):
                    dve_round(e, B * TPB + (TPB - 2 + s), s, slice(s, s + 1), slice(s + 1, s + 2),
                              tile(TPB - 2 + s), tile(TPB - 1 + s))
            e.drain()
            e.tensor_tensor(X[:, :, :], X[:, :, :], H[:, :, :], ALU.add).then_inc(S["out_ready"], 1)

        @block.tensor
        def _(e):
            e.wait_ge(S["consts"], 16 * 5)
            e.wait_ge(S["h_ready"], 1)
            e.wait_ge(S["q_load"], 16)
            e.wait_ge(S["kv_load"], 16)
            e.wait_ge(S["a_load"], 16)
            pe_enter(e, 0, 0, True)
            project(e, 0, 0, 0)
            pe_round(e, -2, 0, n=False, a=False)
            pe_round(e, -1, 1, n=False, first_a=True)
            with e.Fori(0, DEPTH * BATCH) as B:
                e.wait_ge(S["n_load"], (B // BATCH + 1) * N_LOADS)
                e.wait_ge(S["hm_zeroed"], B + 1)
                e.sem_inc(S["pe_step"], 1)
                with e.Fori(0, HALF - 2) as g:
                    for s in range(2):
                        pe_round(e, B * TPB + g * 2 + s, s)
                pe_round(e, B * TPB + (TPB - 4), 0)
                e.wait_ge(S["q_load"], loads_for_next(B))
                e.sem_inc(S["pe_step"], 1)
                pe_round(e, B * TPB + (TPB - 3), 1, first_next=True)
                e.wait_ge(S["kv_load"], loads_for_next(B))
                e.sem_inc(S["pe_step"], 1)
                pe_round(e, B * TPB + (TPB - 2), 0)
                e.wait_ge(S["a_load"], loads_for_next(B))
                e.sem_inc(S["pe_step"], 1)
                pe_round(e, B * TPB + (TPB - 1), 1, first_a=True)


def rope_tables():
    half = np.arange(0, DH, 2, dtype=np.float32)
    inv_freq = (np.float32(1.0) / np.float32(10000.0) ** (half / np.float32(DH))).astype(np.float32)
    t = np.arange(SEQ, dtype=np.float32)
    fr = t[:, None] * inv_freq[None, :]
    fr = np.concatenate([fr, fr], -1).astype(np.float32)
    base = ((half + np.float32(0.4 * DH)) / np.float32(1.4 * DH)).astype(np.float32)
    power = ((t - SEQ // 2) / np.float32(WIN // 2)).astype(np.float32)
    scale = (base[None, :] ** power[:, None]).astype(np.float32)
    scale = np.concatenate([scale, scale], -1)
    sign = np.where(np.arange(DH) < DH // 2, -1.0, 1.0).astype(np.float32)
    cos, sin = np.cos(fr), np.sin(fr) * sign
    tabs = np.stack([cos * scale, sin * scale, cos / scale, sin / scale]).astype(np.float32)
    return np.ascontiguousarray(tabs.reshape(4, TPB, P, DH).transpose(2, 0, 1, 3))


def masks():
    i = np.arange(P)[:, None] % WIN
    j = np.arange(SPAN)[None, :]
    seen = (i <= j) & (j <= i + WIN)
    first = seen & ~((np.arange(P)[:, None] < WIN) & (j < WIN))
    tab = np.stack([first, seen], 1)
    tab = np.where(tab, 0.0, -1e30)
    return np.tile(tab, (1, 1, 8)).astype(np.float32)


def up_biases(b1):
    cols = np.zeros((DEPTH, 2, 3 * P), np.float32)
    cols[:, :, :FF] = b1.reshape(DEPTH, 2, FF)
    return np.ascontiguousarray(cols.reshape(DEPTH, 2, 3, P).transpose(0, 3, 1, 2))


def build(nc, enc, stk, scratch, out):
    with nc.sbuf_tensor("X", [P, TILES, P], F32) as X:
        stage_a(nc, X, scratch=scratch, **enc)
        stage_b(nc, X, out=out, **stk)


def stack_inputs(f):
    rot = np.r_[DH // 2:DH, 0:DH // 2]
    heads = [np.arange(a, HEADS, 2) for a in range(2)]
    vcols = [(2 * INNER + h[:, None] * DH + np.arange(DH)).ravel() for h in heads]
    order = np.concatenate([np.arange(2 * INNER)] + vcols)
    qs, ks = f('L0_ffn_q_scale'), f('L0_ffn_k_scale')
    edge = np.zeros((P, P), np.float32)
    edge[P - 1, 0] = 1
    return dict(
        wqkv=np.ascontiguousarray(f('L0_ffn_Wqkv')[:, :, order]), wo=f('L0_ffn_Wo'), w1=f('L0_ffn_W1'),
        w2=f('L0_ffn_W2'), b1=up_biases(f('L0_ffn_b1')), b2=f('L0_ffn_b2'),
        lngb=np.ascontiguousarray(np.stack([f('L0_ffn_ln_g'), f('L0_ffn_ln_b')], -1)),
        scales=np.ascontiguousarray(np.concatenate([qs, qs[:, rot], ks, ks[:, rot]], -1)),
        rope=rope_tables(), mask=masks(), shift=np.eye(P, k=1, dtype=np.float32), edge=edge)


def kernel(**inputs):
    import concourse.bacc as bacc
    from concourse.bass_utils import run_bass_kernel_spmd as run
    f = lambda n: np.ascontiguousarray(inputs[n])
    onesrow = np.zeros((P, P), np.float32)
    onesrow[0] = 1
    both = dict(ident=np.eye(P, dtype=np.float32))
    enc = dict(onesrow=onesrow, src=f('L0_attn_src'), **encoder_inputs(f))
    stk = stack_inputs(f)
    nc = bacc.Bacc("TRN2", target_bir_lowering=False, num_devices=1)
    arrays = {**both, **enc, **stk}
    dram = {n: nc.dram_tensor(n + "_dram", a.shape, mybir.dt.from_np(a.dtype), kind="ExternalInput").ap()
            for n, a in arrays.items()}
    out = nc.dram_tensor("out_dram", (BATCH, SEQ, P), F32, kind="ExternalOutput").ap()
    scratch = nc.dram_tensor("parts_dram", (2, 3, P, SEQ), BF16, kind="Internal").ap()
    build(nc, {n: dram[n] for n in (*both, *enc)}, {n: dram[n] for n in (*both, *stk)}, scratch, out)
    r = run(nc, [{n + "_dram": a for n, a in arrays.items()}], core_ids=[0])
    return r.results[0]["out_dram"]
```
